# Optimizing a Trainium2 kernel written in Bass

```python
import numpy as np
import jax
import jax.numpy as jnp

def _softmax(x, axis=-1):
    return jax.nn.softmax(x, axis=axis)

def _gelu(x):
    return jax.nn.gelu(x, approximate=True)

def _silu(x):
    return jax.nn.silu(x)

def _sigmoid(x):
    return jax.nn.sigmoid(x)

def _layernorm(x, axis=-1, eps=1e-05):
    m = jnp.mean(x, axis=axis, keepdims=True)
    v = jnp.var(x, axis=axis, keepdims=True)
    return (x - m) / jnp.sqrt(v + eps)

def _scatter_add(tgt, idx, src, axis=0):
    return tgt.at[idx].add(src)

def _segment_sum(src, seg, n):
    return jax.ops.segment_sum(src, seg, n)
kernel_name = 'mk_vit_tower_cls_d1_tok_img1024_r4_c891e0'

def setup_inputs(seed: int=0):
    np.random.seed(seed)
    _w = jnp.asarray

    def _rec_inputs():
        import jax
        import jax.numpy as jnp
        _rk = jax.random.key(seed)
        x = -0.000348323 + 0.999952 * jax.random.normal(jax.random.fold_in(_rk, 1), (8, 3, 128, 128), jnp.float32)
        cls_tok = 0.02 * jax.random.normal(jax.random.fold_in(_rk, 5), (1, 1, 256), jnp.float32)
        return (x, cls_tok)
    x, cls_tok = _rec_inputs()

    def _L0_tok_setup():
        import jax, jax.numpy as jnp
        import numpy as np
        from jax import lax
        PATCH = 16
        key = jax.random.key(seed)
        k1, k2 = jax.random.split(key)
        B, C, IMG, HID = (32, 3, 96, 256)
        inputs = jax.random.normal(k1, (B, C, IMG, IMG), dtype=jnp.float32)
        flat = C * PATCH * PATCH
        W = jax.random.normal(k2, (flat, HID), dtype=jnp.float32) / np.sqrt(flat)
        return {'inputs': inputs, 'W': W}
    _L0_tok_all = _L0_tok_setup()
    _L0_tok_in = {k: v for k, v in _L0_tok_all.items() if k in ('W',)}
    del _L0_tok_all

    def _L0_attn_setup():
        import math
        import jax, jax.numpy as jnp
        import numpy as np
        B, S, D, H = (4, 256, 256, 16)
        HD = D // H
        EPS = 1e-05

        def _sinusoidal_encodings(length, d):
            pos = jnp.arange(length, dtype=jnp.float32)
            inv_freq = 1.0 / 10000.0 ** (jnp.arange(0.0, d, 2.0) / d)
            angles = pos[:, None] * inv_freq[None, :]
            enc = jnp.zeros((length, d), dtype=jnp.float32)
            enc = enc.at[:, 0::2].set(jnp.sin(angles))
            enc = enc.at[:, 1::2].set(jnp.cos(angles))
            return enc

        def _relative_shift(emb):
            b, h, l1, l2 = emb.shape
            padded = jnp.concatenate([jnp.zeros((b, h, l1, 1), emb.dtype), emb], axis=-1)
            padded = padded.reshape(b, h, l2 + 1, l1)
            return padded[:, :, 1:, :].reshape(b, h, l1, l2)
        key = jax.random.key(seed)
        ks = jax.random.split(key, 12)
        s = 0.02
        inp = {'x': jax.random.normal(ks[0], (B, S, D), dtype=jnp.float32), 'Wq': jax.random.normal(ks[1], (D, D), dtype=jnp.float32) * s, 'bq': jnp.zeros((D,), jnp.float32), 'Wk': jax.random.normal(ks[2], (D, D), dtype=jnp.float32) * s, 'bk': jnp.zeros((D,), jnp.float32), 'Wv': jax.random.normal(ks[3], (D, D), dtype=jnp.float32) * s, 'bv': jnp.zeros((D,), jnp.float32), 'Wpos': jax.random.normal(ks[4], (D, D), dtype=jnp.float32) * s, 'Wf': jax.random.normal(ks[5], (D, D), dtype=jnp.float32) * s, 'bf': jnp.zeros((D,), jnp.float32), 'u': jax.random.normal(ks[6], (H, HD), dtype=jnp.float32) * s, 'v': jax.random.normal(ks[7], (H, HD), dtype=jnp.float32) * s, 'gamma': jnp.ones((D,), jnp.float32), 'beta': jnp.zeros((D,), jnp.float32)}
        return inp
    _L0_attn_all = _L0_attn_setup()
    _L0_attn_in = {k: v for k, v in _L0_attn_all.items() if k in ('Wq', 'bq', 'Wk', 'bk', 'Wv', 'bv', 'Wpos', 'Wf', 'bf', 'u', 'v', 'gamma', 'beta')}
    del _L0_attn_all

    def _L0_ffn_setup():
        import jax, jax.numpy as jnp
        import numpy as np
        E, K, D = (8, 2, 256)
        B, S = (2, 1024)

        def _layernorm(x, g, b, eps=1e-06):
            m = jnp.mean(x, axis=-1, keepdims=True)
            v = jnp.var(x, axis=-1, keepdims=True)
            return (x - m) * jax.lax.rsqrt(v + eps) * g + b
        key = jax.random.key(seed)
        ks = jax.random.split(key, 6)
        n = lambda k, shape, scale: jax.random.normal(k, shape, jnp.float32) * scale
        return {'x': n(ks[0], (B, S, D), 1.0), 'gate_w': n(ks[1], (D, E), 0.02), 'w1': n(ks[2], (E, D, 2 * D), 0.02), 'b1': jnp.zeros((E, 2 * D), jnp.float32), 'w2': n(ks[3], (E, 2 * D, D), 0.02), 'b2': jnp.zeros((E, D), jnp.float32), 'ln_g': jnp.ones((E, D), jnp.float32), 'ln_b': jnp.zeros((E, D), jnp.float32)}
    _L0_ffn_all = _L0_ffn_setup()
    _L0_ffn_in = {k: v for k, v in _L0_ffn_all.items() if k in ('gate_w', 'w1', 'b1', 'w2', 'b2', 'ln_g', 'ln_b')}
    del _L0_ffn_all
    return {'x': x, 'cls_tok': cls_tok, 'L0_tok_W': _L0_tok_in['W'], 'L0_attn_Wq': _L0_attn_in['Wq'], 'L0_attn_bq': _L0_attn_in['bq'], 'L0_attn_Wk': _L0_attn_in['Wk'], 'L0_attn_bk': _L0_attn_in['bk'], 'L0_attn_Wv': _L0_attn_in['Wv'], 'L0_attn_bv': _L0_attn_in['bv'], 'L0_attn_Wpos': _L0_attn_in['Wpos'], 'L0_attn_Wf': _L0_attn_in['Wf'], 'L0_attn_bf': _L0_attn_in['bf'], 'L0_attn_u': _L0_attn_in['u'], 'L0_attn_v': _L0_attn_in['v'], 'L0_attn_gamma': _L0_attn_in['gamma'], 'L0_attn_beta': _L0_attn_in['beta'], 'L0_ffn_gate_w': _L0_ffn_in['gate_w'], 'L0_ffn_w1': _L0_ffn_in['w1'], 'L0_ffn_b1': _L0_ffn_in['b1'], 'L0_ffn_w2': _L0_ffn_in['w2'], 'L0_ffn_b2': _L0_ffn_in['b2'], 'L0_ffn_ln_g': _L0_ffn_in['ln_g'], 'L0_ffn_ln_b': _L0_ffn_in['ln_b']}

def reference(x, cls_tok, L0_tok_W, L0_attn_Wq, L0_attn_bq, L0_attn_Wk, L0_attn_bk, L0_attn_Wv, L0_attn_bv, L0_attn_Wpos, L0_attn_Wf, L0_attn_bf, L0_attn_u, L0_attn_v, L0_attn_gamma, L0_attn_beta, L0_ffn_gate_w, L0_ffn_w1, L0_ffn_b1, L0_ffn_w2, L0_ffn_b2, L0_ffn_ln_g, L0_ffn_ln_b):
    import jax
    import jax.numpy as jnp

    def _L0_tok_ref(inputs, W):
        import jax, jax.numpy as jnp
        import numpy as np
        from jax import lax
        PATCH = 16
        B, C, H, Wimg = inputs.shape
        patches = lax.conv_general_dilated_patches(inputs, filter_shape=[PATCH, PATCH], window_strides=[PATCH, PATCH], padding='VALID', dimension_numbers=('NCHW', 'HWIO', 'NCHW'))
        patches = patches.reshape(B, -1, C * PATCH * PATCH)
        return jnp.einsum('bnf,fh->bnh', patches, W)

    def _L0_attn_ref(x, Wq, bq, Wk, bk, Wv, bv, Wpos, Wf, bf, u, v, gamma, beta):
        import math
        import jax, jax.numpy as jnp
        import numpy as np
        B, S, D, H = (4, 256, 256, 16)
        HD = D // H
        EPS = 1e-05

        def _sinusoidal_encodings(length, d):
            pos = jnp.arange(length, dtype=jnp.float32)
            inv_freq = 1.0 / 10000.0 ** (jnp.arange(0.0, d, 2.0) / d)
            angles = pos[:, None] * inv_freq[None, :]
            enc = jnp.zeros((length, d), dtype=jnp.float32)
            enc = enc.at[:, 0::2].set(jnp.sin(angles))
            enc = enc.at[:, 1::2].set(jnp.cos(angles))
            return enc

        def _relative_shift(emb):
            b, h, l1, l2 = emb.shape
            padded = jnp.concatenate([jnp.zeros((b, h, l1, 1), emb.dtype), emb], axis=-1)
            padded = padded.reshape(b, h, l2 + 1, l1)
            return padded[:, :, 1:, :].reshape(b, h, l1, l2)
        b, s, d = x.shape
        mu = jnp.mean(x, axis=-1, keepdims=True)
        var = jnp.mean((x - mu) ** 2, axis=-1, keepdims=True)
        xn = (x - mu) * jax.lax.rsqrt(var + EPS) * gamma + beta
        pe = _sinusoidal_encodings(s, d)
        q = (xn @ Wq + bq).reshape(b, s, H, HD)
        k = (xn @ Wk + bk).reshape(b, s, H, HD)
        val = (xn @ Wv + bv).reshape(b, s, H, HD)
        p = (pe @ Wpos).reshape(s, H, HD)
        AC = jnp.einsum('bihd,bjhd->bhij', q + u, k)
        BD = jnp.einsum('bihd,jhd->bhij', q + v, p)
        BD = _relative_shift(BD)
        attn = jax.nn.softmax((AC + BD) / math.sqrt(d), axis=-1)
        out = jnp.einsum('bhij,bjhd->bihd', attn, val).reshape(b, s, d)
        out = out @ Wf + bf
        return out

    def _L0_ffn_ref(x, gate_w, w1, b1, w2, b2, ln_g, ln_b):
        import jax, jax.numpy as jnp
        import numpy as np
        E, K, D = (8, 2, 256)
        B, S = (2, 1024)

        def _layernorm(x, g, b, eps=1e-06):
            m = jnp.mean(x, axis=-1, keepdims=True)
            v = jnp.var(x, axis=-1, keepdims=True)
            return (x - m) * jax.lax.rsqrt(v + eps) * g + b
        orig_shape = x.shape
        xt = x.reshape(-1, orig_shape[-1])
        scores = xt @ gate_w
        ew, ei = jax.lax.top_k(scores, K)
        ew = jax.nn.softmax(ew, axis=-1)
        mask = ei[None, :, :] == jnp.arange(E)[:, None, None]
        wE = jnp.sum(ew[None, :, :] * mask, axis=-1)
        h = jax.nn.gelu(jnp.einsum('td,edf->etf', xt, w1) + b1[:, None, :], approximate=False)
        o = jnp.einsum('etf,efd->etd', h, w2) + b2[:, None, :]
        y = _layernorm(xt[None, :, :] + o, ln_g[:, None, :], ln_b[:, None, :])
        out = jnp.einsum('et,etd->td', wE, y)
        return out.reshape(orig_shape)
    h = _L0_tok_ref(x, L0_tok_W)
    h = jnp.concatenate([jnp.broadcast_to(cls_tok, (h.shape[0], 1, h.shape[2])), h], axis=1)
    h = h + _L0_attn_ref(_layernorm(h, axis=-1), L0_attn_Wq, L0_attn_bq, L0_attn_Wk, L0_attn_bk, L0_attn_Wv, L0_attn_bv, L0_attn_Wpos, L0_attn_Wf, L0_attn_bf, L0_attn_u, L0_attn_v, L0_attn_gamma, L0_attn_beta)
    h = h + _L0_ffn_ref(_layernorm(h, axis=-1), L0_ffn_gate_w, L0_ffn_w1, L0_ffn_b1, L0_ffn_w2, L0_ffn_b2, L0_ffn_ln_g, L0_ffn_ln_b)
    return h

_drawn_inputs = setup_inputs


def setup_inputs(seed=0):
    import zlib

    import numpy as np

    out = dict(_drawn_inputs(seed))
    spreads = {'L0_attn_bq': (0.0, 0.8),
     'L0_attn_bk': (0.0, 2.0),
     'L0_attn_bv': (0.0, 0.1),
     'L0_attn_bf': (0.0, 0.1),
     'L0_attn_gamma': (1.0, 0.6),
     'L0_attn_beta': (0.0, 0.532),
     'L0_ffn_b1': (0.0, 0.8),
     'L0_ffn_b2': (0.0, 0.1),
     'L0_ffn_ln_g': (1.0, 0.2),
     'L0_ffn_ln_b': (0.0, 0.1)}
    factors = {'cls_tok': 3.651,
     'L0_attn_Wq': 8.0,
     'L0_attn_Wk': 8.0,
     'L0_attn_Wpos': 8.0,
     'L0_attn_u': 45.07,
     'L0_attn_v': 64.0}
    for name, (base, spread) in spreads.items():
        noise = np.random.default_rng([zlib.crc32(name.encode()), seed]).standard_normal(out[name].shape)
        drawn = base * np.exp(spread * noise) if base else spread * noise
        out[name] = jnp.asarray(drawn.astype(out[name].dtype))
    for name, factor in factors.items():
        out[name] = (out[name] * factor).astype(out[name].dtype)
    return out
```

```python
from contextlib import ExitStack

import concourse.bass as bass
from concourse import mybir

F32 = mybir.dt.float32
F32R = mybir.dt.float32r
U32 = mybir.dt.uint32
ALU = mybir.AluOpType
ACT = mybir.ActivationFunctionType
AX = mybir.AxisListType.X

P = 128
B = 8
NP = 64
S = NP + 1
D = 256
DC = D // P
H = 16
HD = D // H
QH = 4
NQ = H // QH
T = B * NP // P
FP = 3 * 16 * 16
KP = FP // P
E = 8
F = 2 * D
FC = F // P
NT = B + T * P
HALF = NT // 2
EPS = 1e-5
EPS_FFN = 1e-6
QC = QH * S


def constants():
    import numpy as np

    at, parts, n = {}, [], 0

    def put(name, a):
        nonlocal n
        a = np.asarray(a, np.float32)
        full = np.zeros((P, a.shape[1]), np.float32)
        full[:a.shape[0]] = a
        at[name] = (n, n + a.shape[1])
        n += a.shape[1]
        parts.append(full)

    p = np.arange(P)
    pos = np.arange(S, dtype=np.float32)
    inv = (1.0 / 10000.0 ** (np.arange(0.0, D, 2.0, dtype=np.float32) / np.float32(D))).astype(np.float32)
    ang = pos[:, None] * inv[None, :]
    pe = np.zeros((S, D), np.float32)
    pe[:, 0::2], pe[:, 1::2] = np.sin(ang), np.cos(ang)
    put("pe", pe.T.reshape(DC, P, S).transpose(1, 0, 2).reshape(P, DC * S))
    put("ident", np.eye(P))
    put("quad", (p[:, None] // HD) % QH == np.arange(QH)[None])
    put("head", np.concatenate([p[:, None] // HD + 8 * g == np.arange(H)[None] for g in range(DC)], 1))
    put("parity", p[:, None] // NP == (np.arange(D)[None] // HD) % 2)
    put("image", p[:, None] // H == np.arange(B)[None])
    put("headof", p[:, None] % H == np.arange(H)[None])
    put("headrow", np.arange(H)[:, None] == np.arange(D)[None] // HD)
    put("iota", np.broadcast_to(np.arange(E), (P, E)))
    put("power", np.full((P, 8), -0.5))
    put("eps", np.full((P, T), D * EPS_FFN))
    put("spread", np.arange(B)[:, None] == np.arange(E * B)[None] % B)
    put("expert", np.arange(E * B)[:, None] // B == np.arange(E)[None])
    put("imageof", np.arange(E * B)[:, None] % B == np.arange(B)[None])
    return at, np.concatenate(parts, 1)


PARAMS = ["bq", "bk", "bv", "u", "v", "gamma", "beta"]


def build(nc, consts, params, xp, cls_tok, tok_w, wq, wk, wv, wpos, wf, bf, gate_w, w1, b1t, w2, b2,
          ln_g, ln_b, out, at):
    with ExitStack() as ctx:
        def sb(name, shape, dt=F32):
            return ctx.enter_context(nc.sbuf_tensor(name, shape, dt))

        def sem(name):
            return ctx.enter_context(nc.semaphore(name))

        C = sb("C", [P, consts.shape[1]])

        def const(name, rows=P):
            return C[0:rows, at[name][0]:at[name][1]]

        ident = const("ident")
        PAR = sb("PAR", [P, len(PARAMS) * DC])

        def par(name, g):
            k = PARAMS.index(name) * DC + g
            return PAR[:, k:k + 1]

        bqu = sb("bqu", [P, DC])
        bqv = sb("bqv", [P, DC])
        early = sb("early", [P, KP * (T * P + D)])
        xp_sb = early[:, 0:KP * T * P].rearrange("p (t n) -> p t n", t=T)
        w_tok = early[:, KP * T * P:].rearrange("p (k n) -> p k n", k=KP)
        w_q, w_k, w_v, w_p, w_f = (sb(f"w_{x}", [P, DC, D]) for x in "qkvpf")
        w_gate = sb("w_gate", [P, DC, E])
        w_gate_h = sb("w_gate_h", [P, DC, E], F32R)
        w_gate_l = sb("w_gate_l", [P, DC, E], F32R)
        bf_rows = sb("bf_rows", [P, D])
        lnb_rows = sb("lnb_rows", [E, D])
        b2_cls = sb("b2_cls", [E * B, D])
        g_cls = sb("g_cls", [E * B, D])
        lnb_cls = sb("lnb_cls", [E * B, D])
        b1_cols = sb("b1_cols", [P, E, FC])

        h_tok = sb("h_tok", [P, T, D])
        h_cls = sb("h_cls", [B, D])
        xn = sb("xn", [P, T, D])
        xn_cls = sb("xn_cls", [B, D])
        stats = sb("stats", [P, T + 1, 6])
        mv = sb("mv", [P, T + 1, 2])
        var = sb("var", [P, T + 1])
        rstd = sb("rstd", [P, T + 1])
        xnT = sb("xnT", [P, 2, DC, 2, 2, NP])
        xnT_cls = sb("xnT_cls", [P, DC, B])
        quT = sb("quT", [P, DC, T * P])
        qvT = sb("qvT", [P, DC, T * P])
        q0u = sb("q0u", [P, DC, B])
        q0v = sb("q0v", [P, DC, B])
        kT = sb("kT", [P, DC, B, S])
        pT = sb("pT", [P, DC, S])
        p_quad = sb("p_quad", [P, DC, QH, S])
        z_cls = sb("z_cls", [P, DC, 15 * H])
        z_last = sb("z_last", [P, DC, B, H])
        z_next = sb("z_next", [P, DC, B, H])
        v_pair = sb("v_pair", [P, B, D])
        v0_row = sb("v0_row", [H, D])
        prob0 = sb("prob0", [P, 2, H])
        probT_cls = sb("probT_cls", [H, B, S])
        e_cls = sb("e_cls", [P, S])
        p_cls = sb("p_cls", [P, 2, NP])
        e_cls0 = sb("e_cls0", [P, B])
        outT = sb("outT", [P, DC, B, NP])
        outT_cls = sb("outT_cls", [P, DC, B])
        small = sb("small", [P, 8])
        mx = sb("mx", [P, 2, H])
        rs = sb("rs", [P, 2, H])
        ri = sb("ri", [P, 2, H])

        xT_h = sb("xT_h", [P, DC, NT], F32R)
        xT_l = sb("xT_l", [P, DC, NT], F32R)
        w1_raw = sb("w1_raw", [P, 2, DC * F])
        w2_raw = sb("w2_raw", [P, 2, FC * D])
        w1_h = sb("w1_h", [P, 2, DC * F], F32R)
        w1_l = sb("w1_l", [P, 2, DC * F], F32R)
        w2_h = sb("w2_h", [P, 2, FC * D], F32R)
        w2_l = sb("w2_l", [P, 2, FC * D], F32R)
        gate = sb("gate", [P, T + 1, E])
        top = sb("top", [P, T + 1, 8])
        top_at = sb("top_at", [P, T + 1, 8], U32)
        top_atf = sb("top_atf", [P, T + 1, 2])
        tw = sb("tw", [P, T + 1, 4])
        pick = sb("pick", [P, 2, T + 1, E])
        wE = sb("wE", [P, T + 1, E])
        wE_d = sb("wE_d", [P, T + 1, E])
        wET = w_q[0:E, :, :].rearrange("e k n -> e (k n)").rearrange("e (t n) -> e t n", t=T)
        wcol_x = sb("wcol_x", [E * B, E])
        wcol = sb("wcol", [E * B, 1])
        wsel = sb("wsel", [E * B, B])
        half_early = 2 * T * D
        xb = early[:, 0:half_early].rearrange("p (a t n) -> p a t n", a=2, t=T)
        res = early[:, half_early:2 * half_early].rearrange("p (a t n) -> p a t n", a=2, t=T)
        res_sum = sb("res_sum", [P, 2, T])
        neg_mean = sb("neg_mean", [P, 2, T])
        sq_junk = (w_p[:, 0, :], w_v[:, 1, :])
        sq_sum = sb("sq_sum", [P, 2, T])
        e_var = sb("e_var", [P, 2, T])
        e_rstd = sb("e_rstd", [P, 2, T])
        e_scale = sb("e_scale", [P, 2, T])
        scaled = w_p[:, 1, :]
        oT_cls = w_v[:, 0, 0:DC * E * B].rearrange("p (k n) -> p k n", k=DC)
        r_cls = w_k[0:E * B, 0, :]
        cls_small = sb("cls_small", [E * B, 8])
        acc_cls = w_k[0:B, 1, :]

        kq_n, pt_n, em_n, sc_n = B * DC * QC, B * (H // 2) * S, (S + 1) * H, H * S
        with nc.sbuf_tensor("arena", [P, kq_n + pt_n + 2 * (em_n + 2 * sc_n + H * NP)], F32) as arena:
            o = 0
            k_quad = arena[:, o:o + kq_n].rearrange("p (b g q s) -> p b g q s", b=B, g=DC, q=QH)
            o += kq_n
            probT = arena[:, o:o + pt_n].rearrange("p (b h s) -> p b h s", b=B, s=S)
            o += pt_n
            emb = arena[:, o:o + 2 * em_n].rearrange("p (n m h) -> p n m h", n=2, h=H)
            o += 2 * em_n
            shifted = arena[:, o:o + 2 * sc_n].rearrange("p (n j h) -> p n j h", n=2, h=H)
            o += 2 * sc_n
            score = arena[:, o:o + 2 * sc_n].rearrange("p (n h j) -> p n h j", n=2, h=H)
            o += 2 * sc_n
            prob = arena[:, o:o + 2 * H * NP].rearrange("p (n h j) -> p n h j", n=2, h=H)
        hid = sb("hid", [P, FC, NT])
        hid_h = sb("hid_h", [P, 2, FC, NT], F32R)
        hid_l = sb("hid_l", [P, 2, FC, NT], F32R)
        g_rows = sb("g_rows", [P, E, D])
        acc = sb("acc", [P, T, D])
        b2_rows = sb("b2_rows", [P, E, D])

        psum = ctx.enter_context(nc.psum_tensor("psum", [P, 8, 512], F32))

        scratch = nc.dram_tensor("shift_scratch", [T * P * (S + 1) * H], F32, kind="Internal")

        s_const, s_par, s_cls, s_wtok = sem("s_const"), sem("s_par"), sem("s_cls"), sem("s_wtok")
        s_xp = [sem(f"s_xp{t}") for t in range(T)]
        s_wqk, s_wv, s_wp, s_wf, s_bf = (sem(f"s_{x}") for x in ("wqk", "wv", "wp", "wf", "bf"))
        s_gw, s_b1, s_b2, s_g, s_lnb, s_clsrows = (sem(f"s_{x}") for x in ("gw", "b1", "b2", "g", "lnb", "clsrows"))
        s_w1raw = [sem(f"s_w1raw{i}") for i in range(2)]
        s_w2raw = [sem(f"s_w2raw{i}") for i in range(2)]
        names = """
            zeros bias2 hps hsb hbf var1 rstd1 xn tz xnT pos_ps p_sb p_quad qps q_ev vps v_ev kps k_ev
            k_quad z_cls cls_qk cls_v q0_ev k0_ev v0_ev z_spread emb_ps emb_a emb_v emb_out shift_in
            ac_ps added maxed subbed exped summed recip normed clsac_ps cls_max cls_exp cls_norm
            cls_sub e0 tcls_ps tcls_ev te_ps te_ev te0_ps te0_ev pv_ps pv_ev wf_ps h2 h2cls wfcls_ps
            var2 rstd2 xt tx_ps tx_h tx_l gw_split gate_ps gate_sb tops diff dexp wE wET_ps wET wcol_ps
            wsel lnb_ps acc0
            w1h w1l w2h w2l hid_ps gelu hsplit o_ps r negm sq escale xb scaled p2
            clsT_sb clsT_ps r_cls cls_nm cls_sq cls_rs y_cls clsout_ps clsout out vchain gchain
        """.split()
        sems = {n: sem("s_" + n) for n in names}

        block = ctx.enter_context(nc.Block())

        @block.sync
        def _(sp):
            sp.dma_start(w_tok[:, :, :], tok_w.rearrange("(k p) n -> p k n", p=P)).then_inc(s_wtok, 16)
            for t in range(T):
                sp.dma_start(xp_sb[:, t, :], xp[t]).then_inc(s_xp[t], 16)
            sp.dma_start(w_v[:, :, :], wv.rearrange("(k p) n -> p k n", p=P)).then_inc(s_wv, 16)
            sp.dma_start(bf_rows[:, :], bf.rearrange("(o d) -> o d", o=1).broadcast_to([P, D])).then_inc(s_bf, 16)
            for e in range(2):
                sp.dma_start(w1_raw[:, e, :].rearrange("p (k n) -> p k n", k=DC),
                             w1[e].rearrange("(k p) n -> p k n", p=P)).then_inc(s_w1raw[e], 16)
                sp.dma_start(w2_raw[:, e, :].rearrange("p (k n) -> p k n", k=FC),
                             w2[e].rearrange("(k p) n -> p k n", p=P)).then_inc(s_w2raw[e], 16)
            sp.dma_start(w_f[:, :, :], wf.rearrange("(k p) n -> p k n", p=P)).then_inc(s_wf, 16)
            sp.dma_start(w_gate[:, :, :], gate_w.rearrange("(k p) n -> p k n", p=P)).then_inc(s_gw, 16)
            sp.dma_start(b1_cols[:, :, :], b1t).then_inc(s_b1, 16)
            sp.dma_start(lnb_rows[:, :], ln_b).then_inc(s_lnb, 16)
            for dst, src in ((b2_cls, b2), (g_cls, ln_g), (lnb_cls, ln_b)):
                for e in range(E):
                    sp.dma_start(dst[e * B:(e + 1) * B, :], src[e:e + 1, :].broadcast_to([B, D]))\
                        .then_inc(s_clsrows, 16)
            for t in range(T):
                sp.wait_ge(sems["emb_a"], 2 * (t + 1))
                sp.wait_ge(sems["emb_v"], 2 * (t + 1))
                sp.dma_start(bass.AP(scratch, t * P * em_n, [[em_n, P], [1, em_n]]),
                             emb[:, t % 2, :, :].rearrange("p m h -> p (m h)")).then_inc(sems["emb_out"], 16)
                sp.wait_ge(sems["emb_out"], 16 * (t + 1))
                if t >= 2:
                    sp.wait_ge(sems["added"], t - 1)
                for i in range(2):
                    src = bass.AP(scratch, (t * P + i * NP) * em_n + (S - 1) * H, [[S * H, NP], [1, S * H]])
                    sp.dma_start(shifted[i * NP:(i + 1) * NP, t % 2, :, :].rearrange("p j h -> p (j h)"), src)\
                        .then_inc(sems["shift_in"], 16)
            sp.wait_ge(sems["wf_ps"], T + 1)
            sp.dma_start(b2_rows[:, :, :], b2.rearrange("(o e) d -> o e d", o=1).broadcast_to([P, E, D]))\
                .then_inc(s_b2, 16)
            sp.dma_start(g_rows[:, :, :], ln_g.rearrange("(o e) d -> o e d", o=1).broadcast_to([P, E, D]))\
                .then_inc(s_g, 16)

            def load_w1(e, p, n):
                sp.wait_ge(sems["w1h"], e - 1)
                sp.wait_ge(sems["w1l"], e - 1)
                sp.dma_start(w1_raw[:, p, :].rearrange("p (k n) -> p k n", k=DC),
                             w1[bass.ds(e, 1)].rearrange("o (k p) n -> p (o k) n", p=P)).then_inc(s_w1raw[p], 16)

            def load_w2(e, p, n):
                sp.wait_ge(sems["w2h"], e - 1)
                sp.wait_ge(sems["w2l"], e - 1)
                sp.dma_start(w2_raw[:, p, :].rearrange("p (k n) -> p k n", k=FC),
                             w2[bass.ds(e, 1)].rearrange("o (k p) n -> p (o k) n", p=P)).then_inc(s_w2raw[p], 16)

            with sp.Fori(0, (E - 2) // 2) as i:
                for p in range(2):
                    load_w1(2 * i + 2 + p, p, i)
                    load_w2(2 * i + 2 + p, p, i)
            sp.wait_ge(sems["clsout"], 1)
            sp.dma_start(out[:, 0, :], acc_cls[:, :]).then_inc(sems["out"], 16)
            for t in range(T):
                sp.wait_ge(sems["p2"], T * (E - 1) + t + 1)
                for i in range(2):
                    sp.dma_start(out[2 * t + i, 1:S, :], acc[i * NP:(i + 1) * NP, t, :]).then_inc(sems["out"], 16)
            sp.wait_ge(sems["out"], 16 * (2 * T + 1))

        def keys(pool, t, quad):
            pool.wait_ge(sems["k_ev"], 2 * (t + 1))
            if t == 0:
                pool.wait_ge(sems["k0_ev"], DC)
            for b in (2 * t, 2 * t + 1):
                for g in range(DC):
                    nc.gpsimd.tensor_tensor(k_quad[:, b, g, :, :],
                                            kT[:, g, b, :].unsqueeze(1).to_broadcast([P, QH, S]),
                                            quad.to_broadcast([P, QH, S]), ALU.mult)\
                        .then_inc(sems["k_quad"], 1)

        def split_w1(eng, e, p, landed):
            eng.wait_ge(s_w1raw[p], landed)
            eng.wait_ge(sems["w1h"], e + 1)
            nc.gpsimd.tensor_tensor(w1_l[:, p, :], w1_raw[:, p, :], w1_h[:, p, :].bitcast(F32), ALU.subtract)\
                .then_inc(sems["w1l"], 1)

        def split_w2(eng, e, p, landed):
            eng.wait_ge(s_w2raw[p], landed)
            eng.wait_ge(sems["w2h"], e + 1)
            nc.gpsimd.tensor_tensor(w2_l[:, p, :], w2_raw[:, p, :], w2_h[:, p, :].bitcast(F32), ALU.subtract)\
                .then_inc(sems["w2l"], 1)


        def w1_high(act, e, p, landed):
            act.wait_ge(s_w1raw[p], landed)
            if not isinstance(e, int) or e >= 2:
                act.wait_ge(sems["hid_ps"], FC * (e - 1))
                act.wait_ge(sems["w1l"], e - 1)
            nc.scalar.activation(w1_h[:, p, :], w1_raw[:, p, :], ACT.Copy).then_inc(sems["w1h"], 1)

        def w2_high(act, e, p, landed):
            act.wait_ge(s_w2raw[p], landed)
            if not isinstance(e, int) or e >= 2:
                act.wait_ge(sems["o_ps"], (T + 1) * (e - 1))
                act.wait_ge(sems["w2l"], e - 1)
            nc.scalar.activation(w2_h[:, p, :], w2_raw[:, p, :], ACT.Copy).then_inc(sems["w2h"], 1)

        def tx_high(act, n):
            rows = P if n < T else B
            c0 = B + n * P if n < T else 0
            act.wait_ge(sems["tx_ps"], n + 1)
            nc.scalar.activation(xT_h[:, :, c0:c0 + rows],
                                 psum[:, 4 + n % 2, 0:DC * rows].rearrange("p (k n) -> p k n", k=DC), ACT.Copy)\
                .then_inc(sems["tx_h"], 1)

        @block.gpsimd
        def _(pool):
            chain = [0]

            def link(ins):
                chain[0] += 1
                ins.then_inc(sems["gchain"], 1)
                pool.wait_ge(sems["gchain"], chain[0])

            nc.gpsimd.memset(z_cls[:, :, :], 0.0).then_inc(sems["zeros"], 1)
            nc.gpsimd.memset(emb[:, :, 0, :], 0.0).then_inc(sems["zeros"], 1)
            nc.gpsimd.memset(gate[:, T, :], 0.0).then_inc(sems["zeros"], 1)
            pool.wait_ge(s_const, 16)

            def rsqrt(col, rows, n, signal, src, dst):
                nc.gpsimd.tensor_tensor(dst, src, C[0:rows, at["power"][0]:at["power"][0] + n], ALU.pow)\
                    .then_inc(sems[signal], 1)

            pool.wait_ge(sems["var1"], 1)
            rsqrt(T, B, 1, "rstd1", var[0:B, T:T + 1], rstd[0:B, T:T + 1])
            quad = const("quad").unsqueeze(2)
            for t in range(T):
                pool.wait_ge(sems["var1"], t + 2)
                rsqrt(t, P, 1, "rstd1", var[:, t:t + 1], rstd[:, t:t + 1])
            for t in range(T):
                keys(pool, t, quad)
            pool.wait_ge(sems["xn"], T + 1)
            pool.wait_ge(sems["hsb"], T)
            pool.wait_ge(s_bf, 16)
            nc.gpsimd.tensor_tensor(h_tok[:, :, :], h_tok[:, :, :],
                                    bf_rows[:, :].unsqueeze(1).to_broadcast([P, T, D]), ALU.add)\
                .then_inc(sems["hbf"], 1)
            nc.gpsimd.tensor_tensor(h_cls[:, :], h_cls[:, :], bf_rows[0:B, :], ALU.add).then_inc(sems["hbf"], 1)
            split_w1(pool, 0, 0, 16)
            split_w1(pool, 1, 1, 16)
            split_w2(pool, 0, 0, 16)
            def rstd2(n):
                pool.wait_ge(sems["var2"], n + 1)
                rsqrt(n, P, 1, "rstd2", var[:, n:n + 1], rstd[:, n:n + 1])

            for t in range(T):
                if t >= 2:
                    rstd2(t - 2)
                pool.wait_ge(sems["recip"], t + 1)
                if t >= 2:
                    pool.wait_ge(sems["te_ps"], 2 * (t - 1))
                    pool.wait_ge(sems["te0_ps"], t - 1)
                nc.gpsimd.tensor_tensor(prob[:, t % 2, :, :], score[:, t % 2, :, 1:S],
                                        ri[:, t % 2, :].unsqueeze(2).to_broadcast([P, H, NP]), ALU.mult)\
                    .then_inc(sems["normed"], 1)
                nc.gpsimd.tensor_tensor(prob0[:, t % 2, :], score[:, t % 2, :, 0], ri[:, t % 2, :], ALU.mult)\
                    .then_inc(sems["normed"], 1)
            rstd2(T - 2)
            rstd2(T - 1)
            pool.wait_ge(sems["var2"], T + 1)
            rsqrt(T, B, 1, "rstd2", var[0:B, T:T + 1], rstd[0:B, T:T + 1])

            def plus_b2(e, p):
                if not isinstance(e, int) or e >= 2:
                    pool.wait_ge(sems["r"], T * (e - 1))
                nc.gpsimd.tensor_tensor(xb[:, p, :, :], xn[:, :, :],
                                        b2_rows[:, bass.ds(e, 1), :].to_broadcast([P, T, D]), ALU.add)\
                    .then_inc(sems["xb"], 1)

            def scale_of(e, p):
                pool.wait_ge(sems["sq"], T * e + T)
                nc.gpsimd.tensor_tensor(e_var[:, p, :], sq_sum[:, p, :], const("eps"), ALU.add)\
                    .then_inc(sems["escale"], 1)
                pool.wait_ge(sems["escale"], 3 * e + 1)
                nc.gpsimd.tensor_tensor(e_rstd[:, p, :], e_var[:, p, :],
                                        C[:, at["power"][0]:at["power"][0] + T], ALU.pow)\
                    .then_inc(sems["escale"], 1)
                pool.wait_ge(sems["escale"], 3 * e + 2)
                nc.gpsimd.tensor_tensor(e_scale[:, p, :], e_rstd[:, p, :], wE_of(e), ALU.mult)\
                    .then_inc(sems["escale"], 1)

            def wE_of(e):
                return wE_d[:, 0:T, bass.ds(e, 1)].rearrange("p t o -> p (t o)")

            pool.wait_ge(s_b2, 16)
            pool.wait_ge(sems["xt"], T + 1)
            plus_b2(0, 0)
            pool.wait_ge(sems["wE"], 2)

            def slot(e, p, k):
                if not isinstance(e, int) or e + 1 < E:
                    split_w2(pool, e + 1, 1 - p, 16 * (k + 1 + p))
                if not isinstance(e, int) or e + 2 < E:
                    split_w1(pool, e + 2, p, 16 * (k + 2))
                if not isinstance(e, int) or e + 1 < E:
                    plus_b2(e + 1, 1 - p)
                scale_of(e, p)

            slot(0, 0, 0)
            with pool.Fori(0, 2) as i:
                slot(2 * i + 1, 1, i)
                slot(2 * i + 2, 0, i + 1)
            for e in range(5, E):
                slot(e, e % 2, e // 2)
            pool.wait_ge(sems["cls_sq"], 2)
            nc.gpsimd.tensor_tensor(cls_small[:, 4:5], cls_small[:, 3:4],
                                    C[0:E * B, at["power"][0]:at["power"][0] + 1], ALU.pow)\
                .then_inc(sems["cls_rs"], 1)

        @block.scalar
        def _(act):
            act.dma_start(PAR[:, :], params).then_inc(s_par, 16)
            act.dma_start(h_cls[:, :], cls_tok.rearrange("a b d -> (a b) d").broadcast_to([B, D])).then_inc(s_cls, 16)
            act.dma_start(C[:, :], consts).then_inc(s_const, 16)
            act.dma_start(w_p[:, :, :], wpos.rearrange("(k p) n -> p k n", p=P)).then_inc(s_wp, 16)
            act.dma_start(w_q[:, :, :], wq.rearrange("(k p) n -> p k n", p=P)).then_inc(s_wqk, 16)
            act.dma_start(w_k[:, :, :], wk.rearrange("(k p) n -> p k n", p=P)).then_inc(s_wqk, 16)
            act.wait_ge(s_par, 16)
            for t in range(T):
                act.wait_ge(sems["hps"], t + 1)
                nc.scalar.activation(h_tok[:, t, :], psum[:, t, 0:D], ACT.Copy).then_inc(sems["hsb"], 1)
            act.wait_ge(sems["tz"], 1)
            for k in range(DC):
                nc.scalar.activation(xnT_cls[:, k, :], psum[:, 5, k * B:(k + 1) * B], ACT.Identity,
                                     scale=par("gamma", k), bias=par("beta", k)).then_inc(sems["xnT"], 1)
            act.wait_ge(sems["bias2"], 2)
            def norm_turned(n):
                act.wait_ge(sems["tz"], n + 2)
                if n >= 2:
                    act.wait_ge(sems["vps"], n - 1)
                for k in range(DC):
                    nc.scalar.activation(xnT[:, n % 2, k, :, :, :],
                                         psum[:, 4 + n % 2, k * P:(k + 1) * P]
                                         .rearrange("p (i s) -> p i s", i=2).unsqueeze(2)
                                         .to_broadcast([P, 2, 2, NP]), ACT.Identity, scale=par("gamma", k), bias=par("beta", k))\
                        .then_inc(sems["xnT"], 1)

            norm_turned(0)
            for n in range(T):
                act.wait_ge(sems["qps"], n + 1)
                for g in range(DC):
                    q_ps = psum[:, 6, g * P:(g + 1) * P]
                    for dst, bias in ((quT, bqu), (qvT, bqv)):
                        nc.scalar.activation(dst[:, g, n * P:(n + 1) * P], q_ps, ACT.Identity,
                                             bias=bias[:, g:g + 1]).then_inc(sems["q_ev"], 1)
                if n + 1 < T:
                    norm_turned(n + 1)
                if n == 0:
                    act.wait_ge(sems["zeros"], 3)
                if n >= 2:
                    act.wait_ge(sems["emb_out"], 16 * (n - 1))
                for q in range(2):
                    act.wait_ge(sems["emb_ps"], NQ * n + q + 1)
                    nc.scalar.activation(emb[:, n % 2, 1:S + 1, q * QH:(q + 1) * QH].rearrange("p m h -> p h m"),
                                         psum[:, q, 0:QC].rearrange("p (h m) -> p h m", h=QH), ACT.Copy)\
                        .then_inc(sems["emb_a"], 1)
            w1_high(act, 0, 0, 16)
            w1_high(act, 1, 1, 16)
            w2_high(act, 0, 0, 16)
            def exponential(t):
                act.wait_ge(sems["subbed"], t + 1)
                nc.scalar.activation(score[:, t % 2, :, :], score[:, t % 2, :, :], ACT.Exp,
                                     scale=1.0 / float(D) ** 0.5).then_inc(sems["exped"], 1)

            exponential(0)
            act.wait_ge(sems["cls_sub"], 1)
            nc.scalar.activation(e_cls[:, :], e_cls[:, :], ACT.Exp, scale=1.0 / float(D) ** 0.5,
                                 accum_out=small[:, 1:2]).then_inc(sems["cls_exp"], 1)
            for t in range(T):
                for half in range(2):
                    act.wait_ge(sems["te_ps"], 2 * t + half + 1)
                    for i in range(2):
                        nc.scalar.activation(probT[:, 2 * t + i, 4 * half:4 * half + 4, 1:S],
                                             psum[:, 4 + half, :].rearrange("p (h i s) -> p h i s", h=4, i=2)[:, :, i, :],
                                             ACT.Copy).then_inc(sems["te_ev"], 1)
                act.wait_ge(sems["te0_ps"], t + 1)
                nc.scalar.activation(probT_cls[:, 2 * t:2 * t + 2, 1:S],
                                     psum[0:H, 7, 3 * P:4 * P].rearrange("p (i s) -> p i s", i=2), ACT.Copy)\
                    .then_inc(sems["te0_ev"], 1)
                if t + 1 < T:
                    exponential(t + 1)
                if t >= 2:
                    tx_high(act, t - 2)
                act.wait_ge(sems["pv_ps"], t + 1)
                o_ps = psum[:, 7, 0:DC * 2 * S].rearrange("p (g i s) -> p g i s", g=DC, i=2)
                for g in range(DC):
                    nc.scalar.activation(outT[:, g, 2 * t:2 * t + 2, :], o_ps[:, g, :, 1:S], ACT.Identity,
                                         bias=par("bv", g)).then_inc(sems["pv_ev"], 1)
                for g in range(DC):
                    nc.scalar.activation(outT_cls[:, g, 2 * t:2 * t + 2], o_ps[:, g, :, 0], ACT.Identity,
                                         bias=par("bv", g)).then_inc(sems["pv_ev"], 1)
            for n in range(T - 2, T + 1):
                tx_high(act, n)
            act.wait_ge(sems["diff"], 1)
            nc.scalar.activation(tw[:, :, 1], tw[:, :, 0], ACT.Exp).then_inc(sems["dexp"], 1)
            act.wait_ge(s_b1, 16)

            def hidden(e, m):
                act.wait_ge(sems["hid_ps"], FC * e + m + 1)
                if not isinstance(e, int) or e >= 1:
                    act.wait_ge(sems["hsplit"], 2 * (FC * (e - 1) + m + 1))
                nc.scalar.activation(hid[:, m, :].rearrange("p (a n) -> p a n", a=2),
                                     psum[:, 2 * (m % 2):2 * (m % 2) + 2, 0:HALF], ACT.Gelu,
                                     bias=b1_cols[:, bass.ds(e, 1), m]).then_inc(sems["gelu"], 1)

            def square(e, p, t):
                act.wait_ge(sems["negm"], T * e + t + 1)
                if not isinstance(e, int) or T * e + t > 1:
                    act.wait_ge(sems["sq"], T * e + t - 1)
                nc.scalar.activation(sq_junk[t % 2], res[:, p, t, :], ACT.Square, bias=neg_mean[:, p, t:t + 1],
                                     accum_out=sq_sum[:, p, t:t + 1]).then_inc(sems["sq"], 1)

            for m in range(FC):
                hidden(0, m)

            def slot(e, p, k):
                static = isinstance(e, int)
                for m in range(FC):
                    if not static or e + 1 < E:
                        hidden(e + 1, m)
                    square(e, p, m)
                    if m == 0 and (not static or e + 1 < E):
                        w2_high(act, e + 1, 1 - p, 16 * (k + 1 + p))
                    if m == 1 and (not static or e + 2 < E):
                        w1_high(act, e + 2, p, 16 * (k + 2))

            slot(0, 0, 0)
            with act.Fori(0, 2) as i:
                slot(2 * i + 1, 1, i)
                slot(2 * i + 2, 0, i + 1)
            for e in range(5, E):
                slot(e, e % 2, e // 2)
            act.wait_ge(sems["cls_nm"], 1)
            act.wait_ge(sems["sq"], T * E)
            nc.scalar.activation(sq_junk[0][0:E * B, :], r_cls[:, :], ACT.Square, bias=cls_small[:, 1:2],
                                 accum_out=cls_small[:, 2:3]).then_inc(sems["cls_sq"], 1)

        @block.vector
        def _(dve):
            chain = [0]

            def link(ins):
                chain[0] += 1
                ins.then_inc(sems["vchain"], 1)
                dve.wait_ge(sems["vchain"], chain[0])

            def norm1(x, rows, n):
                link(nc.vector.bn_stats(stats[0:rows, n, :], x))
                link(nc.vector.bn_aggr(mv[0:rows, n, :], stats[0:rows, n, :]))
                nc.vector.tensor_scalar(var[0:rows, n:n + 1], mv[0:rows, n, 1:2], 1.0 + EPS, EPS * EPS,
                                        ALU.mult, ALU.add).then_inc(sems["var1"], 1)

            def scale1(x, dst, rows, n, count):
                dve.wait_ge(sems["rstd1"], count)
                nc.vector.tensor_scalar(dst, x, mv[0:rows, n, 0:1], rstd[0:rows, n:n + 1], ALU.subtract, ALU.mult)\
                    .then_inc(sems["xn"], 1)

            dve.wait_ge(s_cls, 16)
            norm1(h_cls[:, :], B, T)
            dve.wait_ge(s_par, 16)
            nc.vector.tensor_tensor(bqu[:, :], PAR[:, 0:DC], PAR[:, 3 * DC:4 * DC], ALU.add).then_inc(sems["bias2"], 1)
            nc.vector.tensor_tensor(bqv[:, :], PAR[:, 0:DC], PAR[:, 4 * DC:5 * DC], ALU.add).then_inc(sems["bias2"], 1)
            scale1(h_cls[:, :], xn_cls[:, :], B, T, 1)
            for t in range(T):
                dve.wait_ge(sems["hsb"], t + 1)
                norm1(h_tok[:, t, :], P, t)
            dve.wait_ge(s_const, 16)
            dve.wait_ge(sems["pos_ps"], 1)
            pos = psum[:, 4, 0:DC * S].rearrange("p (g s) -> p g s", g=DC)
            link(nc.vector.tensor_copy(pT[:, :, :], pos))
            for g in range(DC):
                nc.vector.tensor_tensor(p_quad[:, g, :, :], pT[:, g, :].unsqueeze(1).to_broadcast([P, QH, S]),
                                        const("quad").unsqueeze(2).to_broadcast([P, QH, S]), ALU.mult)\
                    .then_inc(sems["p_quad"], 1)
            dve.wait_ge(sems["bias2"], 2)
            dve.wait_ge(sems["cls_qk"], 1)
            cq = psum[:, 6, 0:4 * B].rearrange("p (c g b) -> p c g b", c=2, g=DC)
            for g in range(DC):
                nc.vector.tensor_scalar(q0u[:, g, :], cq[:, 0, g, :], bqu[:, g:g + 1], None, ALU.add)\
                    .then_inc(sems["q0_ev"], 1)
                nc.vector.tensor_scalar(q0v[:, g, :], cq[:, 0, g, :], bqv[:, g:g + 1], None, ALU.add)\
                    .then_inc(sems["q0_ev"], 1)
                nc.vector.tensor_scalar(kT[:, g, :, 0], cq[:, 1, g, :], par("bk", g), None, ALU.add)\
                    .then_inc(sems["k0_ev"], 1)
            dve.wait_ge(sems["cls_v"], 1)
            nc.vector.tensor_tensor(v0_row[:, :], psum[0:H, 7, 0:D], const("headrow", H), ALU.mult)\
                .then_inc(sems["v0_ev"], 1)
            dve.wait_ge(sems["zeros"], 3)
            dve.wait_ge(sems["q0_ev"], 2 * DC)
            for g in range(DC):
                head = const("head")[:, g * H:(g + 1) * H]
                nc.vector.tensor_tensor(z_cls[:, g, 7 * H:8 * H], head, q0u[:, g, 0:1].to_broadcast([P, H]), ALU.mult)\
                    .then_inc(sems["z_spread"], 1)
                nc.vector.tensor_tensor(z_last[:, g, :, :], head.unsqueeze(1).to_broadcast([P, B, H]),
                                        q0v[:, g, :].unsqueeze(2).to_broadcast([P, B, H]), ALU.mult)\
                    .then_inc(sems["z_spread"], 1)

            scale1(h_tok[:, 0, :], xn[:, 0, :], P, 0, 2)
            for n in range(T):
                if n + 1 < T:
                    scale1(h_tok[:, n + 1, :], xn[:, n + 1, :], P, n + 1, n + 3)
                dve.wait_ge(sems["kps"], n + 1)
                for g in range(DC):
                    nc.vector.tensor_scalar(kT[:, g, 2 * n:2 * n + 2, 1:S],
                                            psum[:, 4 + n % 2, (2 + g) * P:(3 + g) * P].rearrange("p (i s) -> p i s", i=2),
                                            par("bk", g), None, ALU.add).then_inc(sems["k_ev"], 1)
                dve.wait_ge(sems["vps"], n + 1)
                nc.vector.tensor_tensor(v_pair[:, 2 * n:2 * n + 2, :],
                                        psum[:, 7, :].rearrange("p (i d) -> p i d", i=2),
                                        const("parity").unsqueeze(1).to_broadcast([P, 2, D]), ALU.mult)\
                    .then_inc(sems["v_ev"], 1)
                if n >= 2:
                    dve.wait_ge(sems["emb_out"], 16 * (n - 1))
                for q in (2, 3):
                    dve.wait_ge(sems["emb_ps"], NQ * n + q + 1)
                    nc.vector.tensor_copy(emb[:, n % 2, 1:S + 1, q * QH:(q + 1) * QH].rearrange("p m h -> p h m"),
                                          psum[:, q, 0:QC].rearrange("p (h m) -> p h m", h=QH))\
                        .then_inc(sems["emb_v"], 1)
            dve.wait_ge(sems["q_ev"], 4 * T)
            for g in range(DC):
                first = qvT[:, g, :].rearrange("p (b n) -> p b n", b=B)[:, :, 0:1]
                nc.vector.tensor_tensor(z_next[:, g, :, :],
                                        const("head")[:, g * H:(g + 1) * H].unsqueeze(1).to_broadcast([P, B, H]),
                                        first.to_broadcast([P, B, H]), ALU.mult).then_inc(sems["z_spread"], 1)
            def scores(t):
                p = t % 2
                dve.wait_ge(sems["ac_ps"], t + 1)
                dve.wait_ge(sems["shift_in"], 32 * (t + 1))
                if t >= 2:
                    dve.wait_ge(sems["normed"], 2 * (t - 1))
                nc.vector.tensor_tensor(score[:, p, :, :].rearrange("p (q h) j -> p q h j", q=NQ),
                                        psum[:, 0:NQ, 0:QC].rearrange("p q (h j) -> p q h j", h=QH),
                                        shifted[:, p, :, :].rearrange("p j (q h) -> p q h j", q=NQ), ALU.add)\
                    .then_inc(sems["added"], 1)
                dve.wait_ge(sems["added"], t + 1)
                nc.vector.tensor_reduce(mx[:, p, :], score[:, p, :, :], AX, ALU.max).then_inc(sems["maxed"], 1)
                dve.wait_ge(sems["maxed"], t + 1)
                nc.vector.tensor_tensor(score[:, p, :, :], score[:, p, :, :],
                                        mx[:, p, :].unsqueeze(2).to_broadcast([P, H, S]), ALU.subtract)\
                    .then_inc(sems["subbed"], 1)

            def sums(t):
                p = t % 2
                dve.wait_ge(sems["exped"], t + 1)
                nc.vector.tensor_reduce(rs[:, p, :], score[:, p, :, :], AX, ALU.add).then_inc(sems["summed"], 1)
                dve.wait_ge(sems["summed"], t + 1)
                nc.vector.reciprocal(ri[:, p, :], rs[:, p, :]).then_inc(sems["recip"], 1)

            def norm2(n):
                rows = P if n < T else B
                h = h_tok[:, n, :] if n < T else h_cls[:, :]
                dve.wait_ge(sems["wf_ps"], n + 1)
                if n == 0:
                    dve.wait_ge(sems["hbf"], 2)
                dve_h2 = nc.vector.tensor_tensor(h, psum[0:rows, 6 if n < T else 0, 0:D], h, ALU.add)
                dve_h2.then_inc(sems["h2"], 1)
                dve.wait_ge(sems["h2"], n + 1)
                link(nc.vector.bn_stats(stats[0:rows, n, :], h))
                link(nc.vector.bn_aggr(mv[0:rows, n, :], stats[0:rows, n, :]))
                nc.vector.tensor_scalar(var[0:rows, n:n + 1], mv[0:rows, n, 1:2], EPS, None, ALU.add)\
                    .then_inc(sems["var2"], 1)

            def norm2_scale(n):
                rows = P if n < T else B
                h = h_tok[:, n, :] if n < T else h_cls[:, :]
                x = xn[:, n, :] if n < T else xn_cls[:, :]
                dve.wait_ge(sems["rstd2"], n + 1)
                nc.vector.tensor_scalar(x, h, mv[0:rows, n, 0:1], rstd[0:rows, n:n + 1], ALU.subtract, ALU.mult)\
                    .then_inc(sems["xt"], 1)

            def tx_low(n):
                rows = P if n < T else B
                c0 = B + n * P if n < T else 0
                dve.wait_ge(sems["tx_h"], n + 1)
                nc.vector.tensor_tensor(xT_l[:, :, c0:c0 + rows],
                                        psum[:, 4 + n % 2, 0:DC * rows].rearrange("p (k n) -> p k n", k=DC),
                                        xT_h[:, :, c0:c0 + rows].bitcast(F32), ALU.subtract).then_inc(sems["tx_l"], 1)

            scores(0)
            dve.wait_ge(sems["clsac_ps"], 1)
            link(nc.vector.tensor_reduce(small[:, 0:1], psum[:, 7, 0:S], AX, ALU.max))
            nc.vector.tensor_scalar(e_cls[:, :], psum[:, 7, 0:S], small[:, 0:1], None, ALU.subtract)\
                .then_inc(sems["cls_sub"], 1)
            dve.wait_ge(sems["cls_exp"], 1)
            link(nc.vector.reciprocal(small[:, 2:3], small[:, 1:2]))
            nc.vector.tensor_scalar(p_cls[:, :, :], e_cls[:, 1:S].unsqueeze(1).to_broadcast([P, 2, NP]),
                                    small[:, 2:3], None, ALU.mult).then_inc(sems["cls_norm"], 1)
            nc.vector.tensor_scalar(e_cls0[:, :], const("image"), e_cls[:, 0:1], small[:, 2:3], ALU.mult, ALU.mult)\
                .then_inc(sems["e0"], 1)
            dve.wait_ge(s_gw, 16)
            nc.vector.tensor_copy(w_gate_h[:, :, :], w_gate[:, :, :]).then_inc(sems["gw_split"], 1)
            dve.wait_ge(sems["gw_split"], 1)
            nc.vector.tensor_tensor(w_gate_l[:, :, :], w_gate[:, :, :], w_gate_h[:, :, :].bitcast(F32), ALU.subtract)\
                .then_inc(sems["gw_split"], 1)
            dve.wait_ge(sems["tcls_ps"], 1)
            for par_ in range(2):
                rows = slice(par_ * NP, (par_ + 1) * NP)
                nc.vector.tensor_copy(probT[rows, :, :, 0],
                                      psum[rows, 7, 0:P].rearrange("p (b h a) -> p b h a", b=B, a=2)[:, :, :, par_])\
                    .then_inc(sems["tcls_ev"], 1)
            nc.vector.tensor_copy(probT_cls[:, :, 0], psum[0:H, 7, P:P + B]).then_inc(sems["tcls_ev"], 1)
            sums(0)
            for t in range(1, T):
                scores(t)
                if t >= 2:
                    norm2(t - 2)
                    norm2_scale(t - 2)
                if t >= 3:
                    tx_low(t - 3)
                sums(t)
            norm2(T - 2)
            norm2_scale(T - 2)
            tx_low(T - 3)
            for n in range(T - 1, T + 1):
                norm2(n)
                norm2_scale(n)
                tx_low(n - 1)
            tx_low(T)

            dve.wait_ge(sems["gate_ps"], T + 1)
            for n in range(T + 1):
                rows = P if n < T else B
                nc.vector.tensor_copy(gate[0:rows, n, :], psum[0:rows, 7, n * E:(n + 1) * E]).then_inc(sems["gate_sb"], 1)
            dve.wait_ge(sems["gate_sb"], T + 1)
            for n in range(T + 1):
                nc.vector.max(top[:, n, :], gate[:, n, :]).then_inc(sems["tops"], 1)
            dve.wait_ge(sems["tops"], T + 1)
            for n in range(T + 1):
                nc.vector.max_index(top_at[:, n, :], top[:, n, :], gate[:, n, :]).then_inc(sems["tops"], 1)
            nc.vector.tensor_tensor(tw[:, :, 0], top[:, :, 1], top[:, :, 0], ALU.subtract).then_inc(sems["diff"], 1)
            dve.wait_ge(sems["tops"], 2 * (T + 1))
            link(nc.vector.tensor_copy(top_atf[:, :, :], top_at[:, :, 0:2]))
            dve.wait_ge(sems["dexp"], 1)
            link(nc.vector.tensor_scalar(tw[:, :, 2], tw[:, :, 1], 1.0, None, ALU.add))
            link(nc.vector.reciprocal(tw[:, :, 3], tw[:, :, 2]))
            link(nc.vector.tensor_tensor(tw[:, :, 2], tw[:, :, 3], tw[:, :, 1], ALU.mult))
            for k in range(2):
                link(nc.vector.tensor_tensor(pick[:, k, :, :], const("iota").unsqueeze(1).to_broadcast([P, T + 1, E]),
                                             top_atf[:, :, k:k + 1].to_broadcast([P, T + 1, E]), ALU.is_equal))
                link(nc.vector.tensor_tensor(pick[:, k, :, :], pick[:, k, :, :],
                                             tw[:, :, 3 - k:4 - k].to_broadcast([P, T + 1, E]), ALU.mult))
            nc.vector.tensor_tensor(wE[:, :, :], pick[:, 0, :, :], pick[:, 1, :, :], ALU.add).then_inc(sems["wE"], 1)
            dve.wait_ge(sems["wE"], 1)
            nc.vector.tensor_scalar(wE_d[:, :, :], wE[:, :, :], float(D) ** 0.5, None, ALU.mult).then_inc(sems["wE"], 1)

            def hsplit(e, p, m):
                dve.wait_ge(sems["gelu"], FC * e + m + 1)
                if not isinstance(e, int) or e >= 2:
                    dve.wait_ge(sems["o_ps"], (T + 1) * (e - 1))
                nc.vector.tensor_copy(hid_h[:, p, m, :], hid[:, m, :]).then_inc(sems["hsplit"], 1)
                dve.wait_ge(sems["hsplit"], 2 * (FC * e + m) + 1)
                nc.vector.tensor_tensor(hid_l[:, p, m, :], hid[:, m, :], hid_h[:, p, m, :].bitcast(F32), ALU.subtract)\
                    .then_inc(sems["hsplit"], 1)

            def residual(e, p, t):
                dve.wait_ge(sems["o_ps"], (T + 1) * e + t + 1)
                if t == 0:
                    dve.wait_ge(sems["xb"], e + 1)
                nc.vector.scalar_tensor_tensor(res[:, p, t, :], psum[:, 4 + t % 2, 0:D], 1.0, xb[:, p, t, :],
                                               ALU.mult, ALU.add, accum_out=res_sum[:, p, t:t + 1])\
                    .then_inc(sems["r"], 1)
                dve.wait_ge(sems["r"], T * e + t + 1)
                nc.vector.tensor_scalar(neg_mean[:, p, t:t + 1], res_sum[:, p, t:t + 1], -1.0 / D, None, ALU.mult)\
                    .then_inc(sems["negm"], 1)

            def add_expert(e, p, t):
                if t == 0:
                    dve.wait_ge(sems["escale"], 3 * e + 3)
                if t >= 1 or isinstance(e, int) and e >= 1:
                    dve.wait_ge(sems["p2"], T * e + t)
                nc.vector.scalar_tensor_tensor(scaled[:, :], res[:, p, t, :], neg_mean[:, p, t:t + 1],
                                               g_rows[:, bass.ds(e, 1), :].rearrange("p o d -> p (o d)"),
                                               ALU.add, ALU.mult).then_inc(sems["scaled"], 1)
                dve.wait_ge(sems["scaled"], T * e + t + 1)
                nc.vector.scalar_tensor_tensor(acc[:, t, :], scaled[:, :], e_scale[:, p, t:t + 1], acc[:, t, :],
                                               ALU.mult, ALU.add).then_inc(sems["p2"], 1)

            for m in range(FC):
                hsplit(0, 0, m)
            dve.wait_ge(sems["wET_ps"], 1)
            nc.vector.tensor_copy(wET[:, :, :], psum[0:E, 7, 0:T * P].rearrange("p (t n) -> p t n", t=T))\
                .then_inc(sems["wET"], 1)
            for t in range(T):
                dve.wait_ge(sems["lnb_ps"], t + 1)
                nc.vector.tensor_tensor(acc[:, t, :], psum[:, 7, 0:D], h_tok[:, t, :], ALU.add).then_inc(sems["acc0"], 1)
            dve.wait_ge(sems["wcol_ps"], 1)
            nc.vector.tensor_tensor_reduce(wcol_x[:, :], psum[0:E * B, 7, 0:E], const("expert", E * B), 1.0, 0.0,
                                           ALU.mult, ALU.add, wcol[:, :]).then_inc(sems["wsel"], 1)
            dve.wait_ge(sems["wsel"], 1)
            nc.vector.tensor_scalar(wsel[:, :], const("imageof", E * B), wcol[:, :], None, ALU.mult)\
                .then_inc(sems["wsel"], 1)
            dve.wait_ge(s_g, 16)

            def slot(e, p, k):
                static = isinstance(e, int)
                for m in range(FC):
                    if not static or e + 1 < E:
                        hsplit(e + 1, 1 - p, m)
                    residual(e, p, m)
                    if not static or e >= 1:
                        add_expert(e - 1, 1 - p, m)

            slot(0, 0, 0)
            with dve.Fori(0, 2) as i:
                slot(2 * i + 1, 1, i)
                slot(2 * i + 2, 0, i + 1)
            for e in range(5, E):
                slot(e, e % 2, e // 2)
            dve.wait_ge(sems["o_ps"], (T + 1) * E)
            nc.vector.tensor_copy(oT_cls[:, :, :], psum[:, 6, 0:DC * E * B].rearrange("p (k n) -> p k n", k=DC))\
                .then_inc(sems["clsT_sb"], 1)
            for t in range(T):
                add_expert(E - 1, (E - 1) % 2, t)
            dve.wait_ge(sems["clsT_ps"], 1)
            dve.wait_ge(s_clsrows, 16 * 3 * E)
            link(nc.vector.tensor_tensor_reduce(r_cls[:, :], psum[0:E * B, 7, 0:D], b2_cls[:, :], 1.0, 0.0,
                                                ALU.add, ALU.add, cls_small[:, 0:1]))
            nc.vector.tensor_scalar(cls_small[:, 1:2], cls_small[:, 0:1], -1.0 / D, None, ALU.mult)\
                .then_inc(sems["cls_nm"], 1)
            dve.wait_ge(sems["cls_sq"], 1)
            nc.vector.tensor_scalar(cls_small[:, 3:4], cls_small[:, 2:3], 1.0 / D, EPS_FFN, ALU.mult, ALU.add)\
                .then_inc(sems["cls_sq"], 1)
            link(nc.vector.scalar_tensor_tensor(r_cls[:, :], r_cls[:, :], cls_small[:, 1:2], g_cls[:, :],
                                                ALU.add, ALU.mult))
            dve.wait_ge(sems["cls_rs"], 1)
            nc.vector.scalar_tensor_tensor(r_cls[:, :], r_cls[:, :], cls_small[:, 4:5], lnb_cls[:, :],
                                           ALU.mult, ALU.add).then_inc(sems["y_cls"], 1)
            dve.wait_ge(sems["clsout_ps"], 1)
            nc.vector.tensor_tensor(acc_cls[:, :], psum[0:B, 5, 0:D], h_cls[:, :], ALU.add).then_inc(sems["clsout"], 1)

        @block.tensor
        def _(pe):
            mm = nc.tensor.matmul
            pe.wait_ge(s_wtok, 16)

            def embed(t):
                pe.wait_ge(s_xp[t], 16)
                for k in range(KP):
                    last = mm(psum[:, t, 0:D], xp_sb[:, t, k * P:(k + 1) * P], w_tok[:, k, :],
                              start=(k == 0), stop=(k == KP - 1))
                last.then_inc(sems["hps"], 1)

            def turn_xn(t):
                p = t % 2
                pe.wait_ge(sems["xn"], t + 2)
                if t == 0:
                    pe.wait_ge(sems["p_quad"], DC)
                    pe.wait_ge(sems["vchain"], 2 * T + 3)
                if t == 1:
                    pe.wait_ge(sems["xnT"], DC)
                if t >= 2:
                    pe.wait_ge(sems["k_ev"], 2 * (t - 1))
                for k in range(DC):
                    last = nc.tensor.transpose(psum[:, 4 + p, k * P:(k + 1) * P], xn[:, t, k * P:(k + 1) * P], ident)
                last.then_inc(sems["tz"], 1)

            def qkv(t):
                p = t % 2
                pe.wait_ge(sems["xnT"], DC * (t + 2))
                if t == 0:
                    pe.wait_ge(sems["q0_ev"], 2 * DC)
                    pe.wait_ge(sems["k0_ev"], DC)
                else:
                    pe.wait_ge(sems["q_ev"], 4 * t)
                for g in range(DC):
                    for k in range(DC):
                        last = mm(psum[:, 6, g * P:(g + 1) * P], w_q[:, k, g * P:(g + 1) * P], xnT[:, p, k, :, 0, :],
                                  start=(k == 0), stop=(k == DC - 1))
                last.then_inc(sems["qps"], 1)
                for g in range(DC):
                    for k in range(DC):
                        last = mm(psum[:, 4 + p, (2 + g) * P:(3 + g) * P], w_k[:, k, g * P:(g + 1) * P],
                                  xnT[:, p, k, :, 0, :], start=(k == 0), stop=(k == DC - 1))
                last.then_inc(sems["kps"], 1)
                if t + 1 < T:
                    turn_xn(t + 1)
                if t == 0:
                    pe.wait_ge(sems["v0_ev"], 1)
                else:
                    pe.wait_ge(sems["v_ev"], t)
                for i in range(2):
                    for k in range(DC):
                        both = xnT[:, p, k, i, :, :].rearrange("p a s -> p (a s)")
                        last = mm(psum[:, 7, i * D:(i + 1) * D], both, w_v[:, k, :], start=(k == 0), stop=(k == DC - 1))
                last.then_inc(sems["vps"], 1)

            def positions(t):
                pe.wait_ge(sems["q_ev"], 4 * (t + 1))
                for q in range(NQ):
                    if t == 0:
                        pe.wait_ge(sems["hsb"], T)
                    elif q < 2:
                        pe.wait_ge(sems["emb_a"], 2 * (t - 1) + q + 1)
                    else:
                        pe.wait_ge(sems["emb_v"], 2 * (t - 1) + q - 1)
                    rows = slice((q % 2) * NP, (q % 2 + 1) * NP)
                    mm(psum[:, q, 0:QC], qvT[rows, q // 2, t * P:(t + 1) * P],
                       p_quad[rows, q // 2, :, :].rearrange("p h s -> p (h s)"), start=True, stop=True)\
                        .then_inc(sems["emb_ps"], 1)

            for t in range(T):
                embed(t)
            pe.wait_ge(s_const, 16)
            pe.wait_ge(s_wp, 16)
            pe_T = const("pe")
            for g in range(DC):
                for k in range(DC):
                    last = mm(psum[:, 4, g * S:(g + 1) * S], w_p[:, k, g * P:(g + 1) * P],
                              pe_T[:, k * S:(k + 1) * S], start=(k == 0), stop=(k == DC - 1))
            last.then_inc(sems["pos_ps"], 1)
            pe.wait_ge(sems["xn"], 1)
            for k in range(DC):
                last = nc.tensor.transpose(psum[:, 5, k * B:(k + 1) * B], xn_cls[:, k * P:(k + 1) * P],
                                           ident[0:B, 0:B])
            last.then_inc(sems["tz"], 1)
            pe.wait_ge(s_wqk, 32)
            pe.wait_ge(sems["xnT"], DC)
            for c, w in enumerate((w_q, w_k)):
                for g in range(DC):
                    for k in range(DC):
                        last = mm(psum[:, 6, (c * DC + g) * B:(c * DC + g + 1) * B], w[:, k, g * P:(g + 1) * P],
                                  xnT_cls[:, k, :], start=(k == 0), stop=(k == DC - 1))
            last.then_inc(sems["cls_qk"], 1)
            pe.wait_ge(s_wv, 16)
            for k in range(DC):
                last = mm(psum[0:H, 7, 0:D], xnT_cls[:, k, 0:1].to_broadcast([P, H]), w_v[:, k, :],
                          start=(k == 0), stop=(k == DC - 1))
            last.then_inc(sems["cls_v"], 1)

            turn_xn(0)
            for t in range(T):
                qkv(t)
                positions(t)

            def content(t):
                pe.wait_ge(sems["k_quad"], 4 * (t + 1))
                if t == 0:
                    pe.wait_ge(sems["emb_a"], 2 * T)
                    pe.wait_ge(sems["emb_v"], 2 * T)
                else:
                    pe.wait_ge(sems["added"], t)
                for q in range(NQ):
                    rows = slice((q % 2) * NP, (q % 2 + 1) * NP)
                    for i in range(2):
                        last = mm(psum[i * NP:(i + 1) * NP, q, 0:QC],
                                  quT[rows, q // 2, t * P + i * NP:t * P + (i + 1) * NP],
                                  k_quad[rows, 2 * t + i, q // 2, :, :].rearrange("p h s -> p (h s)"),
                                  start=True, stop=True)
                last.then_inc(sems["ac_ps"], 1)

            content(0)
            pe.wait_ge(sems["z_spread"], 3 * DC)
            pe.wait_ge(sems["v_ev"], T)
            for b in range(B):
                for g in range(DC):
                    mm(psum[:, 7, 0:S], z_cls[:, g, (7 - b) * H:(15 - b) * H], kT[:, g, b, :],
                       start=(b == 0 and g == 0), stop=False)
            for g in range(DC):
                mm(psum[:, 7, 0:1], z_last[:, g, :, :].rearrange("p b h -> p (b h)"), pT[:, g, S - 1:S],
                   start=False, stop=False)
                last = mm(psum[:, 7, 2:S], z_next[:, g, :, :].rearrange("p b h -> p (b h)"), pT[:, g, 0:S - 2],
                          start=False, stop=(g == DC - 1))
            last.then_inc(sems["clsac_ps"], 1)
            content(1)
            pe.wait_ge(sems["cls_norm"], 1)
            nc.tensor.transpose(psum[:, 7, 0:P], p_cls[:, :, :].rearrange("p a s -> p (a s)"), ident)
            pe.wait_ge(sems["e0"], 1)
            mm(psum[0:H, 7, P:P + B], const("headof"), e_cls0[:, :], start=True, stop=True)\
                .then_inc(sems["tcls_ps"], 1)

            def turn(t):
                p = t % 2
                pe.wait_ge(sems["normed"], 2 * (t + 1))
                if t == 0:
                    pe.wait_ge(sems["k_ev"], 2 * T)
                for half in range(2):
                    if t >= 1:
                        pe.wait_ge(sems["te_ev"], 4 * t)
                    if t >= 3 and half == (t - 3) % 2:
                        pe.wait_ge(sems["tx_l"], t - 2)
                    for n in range(4):
                        pair = 4 * half + n
                        last = nc.tensor.transpose(psum[:, 4 + half, n * P:(n + 1) * P],
                                                   prob[:, p, 2 * pair:2 * pair + 2, :].rearrange("p h j -> p (h j)"), ident)
                    last.then_inc(sems["te_ps"], 1)
                if t == 0:
                    pe.wait_ge(sems["tcls_ev"], 3)
                else:
                    pe.wait_ge(sems["pv_ev"], 4 * t)
                nc.tensor.transpose(psum[0:H, 7, 3 * P:4 * P], prob0[:, p, :], ident).then_inc(sems["te0_ps"], 1)

            def values(t):
                pe.wait_ge(sems["te_ev"], 4 * (t + 1))
                pe.wait_ge(sems["te0_ev"], t + 1)
                for g in range(DC):
                    for i in range(2):
                        b = 2 * t + i
                        c0 = (2 * g + i) * S
                        mm(psum[:, 7, c0:c0 + S], v0_row[:, g * P:(g + 1) * P], probT_cls[:, b, :],
                           start=True, stop=False, skip_group_check=True)
                        for c in range(4):
                            pair = 4 * g + c
                            last = mm(psum[32 * c:32 * c + 32, 7, c0:c0 + S], v_pair[:, b, 32 * pair:32 * pair + 32],
                                      probT[:, b, pair, :], start=False, stop=(c == 3), skip_group_check=True)
                last.then_inc(sems["pv_ps"], 1)

            def project(t):
                if t == 0:
                    pe.wait_ge(s_wf, 16)
                elif t < T:
                    pe.wait_ge(sems["h2"], t)
                else:
                    pe.wait_ge(sems["added"], T)
                pe.wait_ge(sems["pv_ev"], 4 * t + 2 if t < T else 4 * T)
                rows, bank = (P, 6) if t < T else (B, 0)
                for k in range(DC):
                    x = outT[:, k, 2 * t:2 * t + 2, :].rearrange("p i s -> p (i s)") if t < T else outT_cls[:, k, :]
                    last = mm(psum[0:rows, bank, 0:D], x, w_f[:, k, :], start=(k == 0), stop=(k == DC - 1))
                last.then_inc(sems["wf_ps"], 1)

            def turn_x(n):
                rows = P if n < T else B
                if n >= 2:
                    pe.wait_ge(sems["tx_l"], n - 1)
                x = xn[:, n, :] if n < T else xn_cls[:, :]
                pe.wait_ge(sems["xt"], n + 1)
                pe.wait_ge(sems["te_ev"], 4 * min(n + 3, T))
                for k in range(DC):
                    last = nc.tensor.transpose(psum[:, 4 + n % 2, k * rows:(k + 1) * rows], x[:, k * P:(k + 1) * P],
                                               ident[0:rows, 0:rows])
                last.then_inc(sems["tx_ps"], 1)

            for t in range(T):
                if t >= 1:
                    project(t - 1)
                turn(t)
                if t + 2 < T:
                    content(t + 2)
                if t >= 2:
                    turn_x(t - 2)
                values(t)
            project(T - 1)
            project(T)
            turn_x(T - 2)
            turn_x(T - 1)
            turn_x(T)

            pe.wait_ge(sems["tx_l"], T + 1)
            pe.wait_ge(sems["gw_split"], 2)
            pe.wait_ge(sems["pv_ev"], 4 * T)
            for n in range(T + 1):
                c0 = B + n * P if n < T else 0
                first = True
                for k in range(DC):
                    for x, w in ((xT_h, w_gate_h), (xT_h, w_gate_l), (xT_l, w_gate_h)):
                        last = mm(psum[:, 7, n * E:(n + 1) * E], x[:, k, c0:c0 + P], w[:, k, :],
                                  start=first, stop=(k == DC - 1 and x is xT_l))
                        first = False
                last.then_inc(sems["gate_ps"], 1)

            def hidden(e, p, m):
                if m == 0:
                    pe.wait_ge(sems["w1h"], e + 1)
                    pe.wait_ge(sems["w1l"], e + 1)
                if isinstance(e, int) and e == 0 and m < 2:
                    if m == 0:
                        pe.wait_ge(sems["added"], T)
                else:
                    pe.wait_ge(sems["gelu"], FC * e + m - 1)
                for k in range(DC):
                    cols = slice(k * F + m * P, k * F + (m + 1) * P)
                    for w, x in ((w1_h, xT_h), (w1_h, xT_l), (w1_l, xT_h)):
                        for half in range(2):
                            last = mm(psum[:, 2 * (m % 2) + half, 0:HALF], w[:, p, cols],
                                      x[:, k, half * HALF:(half + 1) * HALF],
                                      start=(k == 0 and w is w1_h and x is xT_h), stop=(k == DC - 1 and w is w1_l))
                last.then_inc(sems["hid_ps"], 1)

            def output(e, p, t):
                if t == 0:
                    pe.wait_ge(sems["hsplit"], 2 * FC * (e + 1))
                    pe.wait_ge(sems["w2h"], e + 1)
                    pe.wait_ge(sems["w2l"], e + 1)
                if isinstance(e, int) and e == 0 and t < 2:
                    if t == 0:
                        pe.wait_ge(sems["te_ev"], 4 * T)
                else:
                    pe.wait_ge(sems["r"], T * e + t - 1)
                for m in range(FC):
                    cols = slice(m * D, (m + 1) * D)
                    for x, w in ((hid_h, w2_h), (hid_h, w2_l), (hid_l, w2_h)):
                        last = mm(psum[:, 4 + t % 2, 0:D], x[:, p, m, B + t * P:B + (t + 1) * P], w[:, p, cols],
                                  start=(m == 0 and x is hid_h and w is w2_h), stop=(m == FC - 1 and x is hid_l))
                last.then_inc(sems["o_ps"], 1)

            def output_cls(e, p):
                for k in range(DC):
                    for m in range(FC):
                        cols = slice(m * D + k * P, m * D + (k + 1) * P)
                        for w, x in ((w2_h, hid_h), (w2_h, hid_l), (w2_l, hid_h)):
                            last = mm(psum[:, 6, bass.ds(k * E * B + e * B, B)], w[:, p, cols], x[:, p, m, 0:B],
                                      start=(m == 0 and w is w2_h and x is hid_h), stop=(m == FC - 1 and w is w2_l))
                last.then_inc(sems["o_ps"], 1)

            for m in range(FC):
                hidden(0, 0, m)
            pe.wait_ge(sems["wE"], 1)
            for t in range(T):
                last = nc.tensor.transpose(psum[0:E, 7, t * P:(t + 1) * P], wE[:, t, :], ident)
            last.then_inc(sems["wET_ps"], 1)
            pe.wait_ge(sems["wET"], 1)
            pe.wait_ge(s_lnb, 16)
            for t in range(T):
                if t >= 1:
                    pe.wait_ge(sems["acc0"], t)
                mm(psum[:, 7, 0:D], wET[:, t, :], lnb_rows[:, :], start=True, stop=True).then_inc(sems["lnb_ps"], 1)
            pe.wait_ge(sems["acc0"], T)
            mm(psum[0:E * B, 7, 0:E], const("spread", B), wE[0:B, T, :], start=True, stop=True)\
                .then_inc(sems["wcol_ps"], 1)

            def slot(e, p, k):
                static = isinstance(e, int)
                for m in range(FC):
                    if not static or e + 1 < E:
                        hidden(e + 1, 1 - p, m)
                    output(e, p, m)
                output_cls(e, p)

            slot(0, 0, 0)
            with pe.Fori(0, 2) as i:
                slot(2 * i + 1, 1, i)
                slot(2 * i + 2, 0, i + 1)
            for e in range(5, E):
                slot(e, e % 2, e // 2)
            pe.wait_ge(sems["clsT_sb"], 1)
            pe.wait_ge(sems["wsel"], 2)
            mm(psum[0:E * B, 7, 0:D], const("spread", B), xn_cls[:, :], start=True, stop=False)
            for k in range(DC):
                last = mm(psum[0:E * B, 7, k * P:(k + 1) * P], oT_cls[:, k, :], ident, start=False, stop=(k == DC - 1))
            last.then_inc(sems["clsT_ps"], 1)
            pe.wait_ge(sems["y_cls"], 1)
            pe.wait_ge(sems["r"], T * E)
            mm(psum[0:B, 5, 0:D], wsel[:, :], r_cls[:, :], start=True, stop=True).then_inc(sems["clsout_ps"], 1)


def kernel(x, cls_tok, L0_tok_W, L0_attn_Wq, L0_attn_bq, L0_attn_Wk, L0_attn_bk, L0_attn_Wv, L0_attn_bv,
           L0_attn_Wpos, L0_attn_Wf, L0_attn_bf, L0_attn_u, L0_attn_v, L0_attn_gamma, L0_attn_beta,
           L0_ffn_gate_w, L0_ffn_w1, L0_ffn_b1, L0_ffn_w2, L0_ffn_b2, L0_ffn_ln_g, L0_ffn_ln_b):
    import numpy as np
    import concourse.bacc as bacc
    from concourse.bass_utils import run_bass_kernel_spmd

    at, table = constants()
    patches = np.asarray(x).reshape(B, 3, 8, 16, 8, 16).transpose(0, 1, 3, 5, 2, 4).reshape(T, P, KP, P)
    patches = np.ascontiguousarray(patches.transpose(0, 3, 2, 1)).reshape(T, P, KP * P)
    vectors = [L0_attn_bq, L0_attn_bk, L0_attn_bv, L0_attn_u, L0_attn_v, L0_attn_gamma, L0_attn_beta]
    params = np.concatenate([np.asarray(a).reshape(DC, P).T for a in vectors], 1)
    b1t = np.asarray(L0_ffn_b1).reshape(E, FC, P).transpose(2, 0, 1)
    arrays = {
        "consts": table, "params": params, "patches": patches, "cls_tok": cls_tok, "tok_w": L0_tok_W,
        "wq": L0_attn_Wq, "wk": L0_attn_Wk, "wv": L0_attn_Wv, "wpos": L0_attn_Wpos, "wf": L0_attn_Wf,
        "bf": L0_attn_bf, "gate_w": L0_ffn_gate_w, "w1": L0_ffn_w1, "b1t": b1t, "w2": L0_ffn_w2,
        "b2": L0_ffn_b2, "ln_g": L0_ffn_ln_g, "ln_b": L0_ffn_ln_b,
    }
    arrays = {f"in_{k}": np.ascontiguousarray(a) for k, a in arrays.items()}
    nc = bacc.Bacc("TRN2", target_bir_lowering=False, num_devices=1, dynamic_dma_scratch_size=1024)
    args = [nc.dram_tensor(k, a.shape, mybir.dt.from_np(a.dtype), kind="ExternalInput").ap()
            for k, a in arrays.items()]
    out = nc.dram_tensor("out", (B, S, D), F32, kind="ExternalOutput").ap()
    build(nc, *args, out, at)
    r = run_bass_kernel_spmd(nc, [arrays], core_ids=[0])
    return r.results[0]["out"]
```

```python
from contextlib import ExitStack

import concourse.bass as bass
from concourse import mybir

F32 = mybir.dt.float32
F32R = mybir.dt.float32r
U32 = mybir.dt.uint32
ALU = mybir.AluOpType
ACT = mybir.ActivationFunctionType
AX = mybir.AxisListType.X

P = 128
B = 8
NP = 64
S = NP + 1
D = 256
DC = D // P
H = 16
HD = D // H
QH = 4
NQ = H // QH
T = B * NP // P
FP = 3 * 16 * 16
KP = FP // P
E = 8
F = 2 * D
FC = F // P
NT = B + T * P
HALF = NT // 2
EPS = 1e-5
EPS_FFN = 1e-6
QC = QH * S


def constants():
    import numpy as np

    at, parts, n = {}, [], 0

    def put(name, a):
        nonlocal n
        a = np.asarray(a, np.float32)
        full = np.zeros((P, a.shape[1]), np.float32)
        full[:a.shape[0]] = a
        at[name] = (n, n + a.shape[1])
        n += a.shape[1]
        parts.append(full)

    p = np.arange(P)
    pos = np.arange(S, dtype=np.float32)
    inv = (1.0 / 10000.0 ** (np.arange(0.0, D, 2.0, dtype=np.float32) / np.float32(D))).astype(np.float32)
    ang = pos[:, None] * inv[None, :]
    pe = np.zeros((S, D), np.float32)
    pe[:, 0::2], pe[:, 1::2] = np.sin(ang), np.cos(ang)
    put("pe", pe.T.reshape(DC, P, S).transpose(1, 0, 2).reshape(P, DC * S))
    put("ident", np.eye(P))
    put("quad", (p[:, None] // HD) % QH == np.arange(QH)[None])
    put("head", np.concatenate([p[:, None] // HD + 8 * g == np.arange(H)[None] for g in range(DC)], 1))
    put("parity", p[:, None] // NP == (np.arange(D)[None] // HD) % 2)
    put("image", p[:, None] // H == np.arange(B)[None])
    put("headof", p[:, None] % H == np.arange(H)[None])
    put("headrow", np.arange(H)[:, None] == np.arange(D)[None] // HD)
    put("iota", np.broadcast_to(np.arange(E), (P, E)))
    put("power", np.full((P, 8), -0.5))
    put("eps", np.full((P, T), D * EPS_FFN))
    put("spread", np.arange(B)[:, None] == np.arange(E * B)[None] % B)
    put("expert", np.arange(E * B)[:, None] // B == np.arange(E)[None])
    put("imageof", np.arange(E * B)[:, None] % B == np.arange(B)[None])
    return at, np.concatenate(parts, 1)


PARAMS = ["bq", "bk", "bv", "u", "v", "gamma", "beta"]


def build(nc, consts, params, xp, cls_tok, tok_w, wq, wk, wv, wpos, wf, bf, gate_w, w1, b1t, w2, b2,
          ln_g, ln_b, out, at):
    with ExitStack() as ctx:
        def sb(name, shape, dt=F32):
            return ctx.enter_context(nc.sbuf_tensor(name, shape, dt))

        def sem(name):
            return ctx.enter_context(nc.semaphore(name))

        C = sb("C", [P, consts.shape[1]])

        def const(name, rows=P):
            return C[0:rows, at[name][0]:at[name][1]]

        ident = const("ident")
        PAR = sb("PAR", [P, len(PARAMS) * DC])

        def par(name, g):
            k = PARAMS.index(name) * DC + g
            return PAR[:, k:k + 1]

        bqu = sb("bqu", [P, DC])
        bqv = sb("bqv", [P, DC])
        early = sb("early", [P, KP * (T * P + D)])
        xp_sb = early[:, 0:KP * T * P].rearrange("p (t n) -> p t n", t=T)
        w_tok = early[:, KP * T * P:].rearrange("p (k n) -> p k n", k=KP)
        w_q, w_k, w_v, w_p, w_f = (sb(f"w_{x}", [P, DC, D]) for x in "qkvpf")
        w_gate = sb("w_gate", [P, DC, E])
        w_gate_h = sb("w_gate_h", [P, DC, E], F32R)
        w_gate_l = sb("w_gate_l", [P, DC, E], F32R)
        bf_rows = sb("bf_rows", [P, D])
        lnb_rows = sb("lnb_rows", [E, D])
        b2_cls = sb("b2_cls", [E * B, D])
        g_cls = sb("g_cls", [E * B, D])
        lnb_cls = sb("lnb_cls", [E * B, D])
        b1_cols = sb("b1_cols", [P, E, FC])

        h_tok = sb("h_tok", [P, T, D])
        h_cls = sb("h_cls", [B, D])
        xn = sb("xn", [P, T, D])
        xn_cls = sb("xn_cls", [B, D])
        stats = sb("stats", [P, T + 1, 6])
        mv = sb("mv", [P, T + 1, 2])
        var = sb("var", [P, T + 1])
        rstd = sb("rstd", [P, T + 1])
        xnT = sb("xnT", [P, 2, DC, 2, 2, NP])
        xnT_cls = sb("xnT_cls", [P, DC, B])
        quT = sb("quT", [P, DC, T * P])
        qvT = sb("qvT", [P, DC, T * P])
        q0u = sb("q0u", [P, DC, B])
        q0v = sb("q0v", [P, DC, B])
        kT = sb("kT", [P, DC, B, S])
        pT = sb("pT", [P, DC, S])
        p_quad = sb("p_quad", [P, DC, QH, S])
        z_cls = sb("z_cls", [P, DC, B, H])
        z_last = sb("z_last", [P, DC, B, H])
        z_next = sb("z_next", [P, DC, B, H])
        v_pair = sb("v_pair", [P, B, D])
        v0_row = sb("v0_row", [H, D])
        prob0 = sb("prob0", [P, 2, H])
        probT_cls = sb("probT_cls", [H, B, S])
        e_cls = sb("e_cls", [P, S])
        p_cls = sb("p_cls", [P, 2, NP])
        e_cls0 = sb("e_cls0", [P, B])
        outT = sb("outT", [P, DC, B, NP])
        outT_cls = sb("outT_cls", [P, DC, B])
        small = sb("small", [P, 8])
        mx = sb("mx", [P, 2, H])
        rs = sb("rs", [P, 2, H])
        ri = sb("ri", [P, 2, H])

        xT_h = sb("xT_h", [P, DC, NT], F32R)
        xT_l = sb("xT_l", [P, DC, NT], F32R)
        w1_raw = sb("w1_raw", [P, 2, DC * F])
        w2_raw = sb("w2_raw", [P, 2, FC * D])
        w1_h = sb("w1_h", [P, 2, DC * F], F32R)
        w1_l = sb("w1_l", [P, 2, DC * F], F32R)
        w2_h = sb("w2_h", [P, 2, FC * D], F32R)
        w2_l = sb("w2_l", [P, 2, FC * D], F32R)
        gate = sb("gate", [P, T + 1, E])
        gateT = w_q[0:E, :, :].rearrange("e k n -> e (k n)")
        gateT_cls = sb("gateT_cls", [E, B])
        top = sb("top", [P, T + 1, 8])
        top_at = sb("top_at", [P, T + 1, 8], U32)
        top_atf = sb("top_atf", [P, T + 1, 2])
        tw = sb("tw", [P, T + 1, 4])
        pick = sb("pick", [P, 2, T + 1, E])
        wE = sb("wE", [P, T + 1, E])
        wE_d = sb("wE_d", [P, T + 1, E])
        wET = gateT.rearrange("e (t n) -> e t n", t=T)
        wcol_x = sb("wcol_x", [E * B, E])
        wcol = sb("wcol", [E * B, 1])
        wsel = sb("wsel", [E * B, B])
        half_early = 2 * T * D
        cls_all = early[:, 0:B * S]
        xb = early[:, 0:half_early].rearrange("p (a t n) -> p a t n", a=2, t=T)
        res = early[:, half_early:2 * half_early].rearrange("p (a t n) -> p a t n", a=2, t=T)
        res_sum = sb("res_sum", [P, 2, T])
        neg_mean = sb("neg_mean", [P, 2, T])
        sq_junk = (w_p[:, 0, :], w_v[:, 1, :])
        sq_sum = sb("sq_sum", [P, 2, T])
        e_var = sb("e_var", [P, 2, T])
        e_rstd = sb("e_rstd", [P, 2, T])
        e_scale = sb("e_scale", [P, 2, T])
        scaled = w_p[:, 1, :]
        last_y = w_f
        last_bias = sb("last_bias", [P, 2])
        cls_rows = v_pair[0:2 * B, :, :]
        o_cls = quT[0:E * B, 0, :].rearrange("p (a d) -> p a d", a=2)
        x_cls = w_k[0:E * B, 1, :]
        r_cls = w_k[0:E * B, 0, :]
        cls_small = sb("cls_small", [E * B, 8])
        acc_cls = sb("acc_cls", [B, D])

        kq_n, pt_n, em_n, sc_n = B * DC * QC, B * (H // 2) * S, (S + 1) * H, H * S
        with nc.sbuf_tensor("arena", [P, kq_n + pt_n + 2 * (em_n + 2 * sc_n + H * NP)], F32) as arena:
            o = 0
            k_quad = arena[:, o:o + kq_n].rearrange("p (b g q s) -> p b g q s", b=B, g=DC, q=QH)
            o += kq_n
            probT = arena[:, o:o + pt_n].rearrange("p (b h s) -> p b h s", b=B, s=S)
            o += pt_n
            emb = arena[:, o:o + 2 * em_n].rearrange("p (n m h) -> p n m h", n=2, h=H)
            o += 2 * em_n
            shifted = arena[:, o:o + 2 * sc_n].rearrange("p (n j h) -> p n j h", n=2, h=H)
            o += 2 * sc_n
            score = arena[:, o:o + 2 * sc_n].rearrange("p (n h j) -> p n h j", n=2, h=H)
            o += 2 * sc_n
            prob = arena[:, o:o + 2 * H * NP].rearrange("p (n h j) -> p n h j", n=2, h=H)
        hid = sb("hid", [P, FC, NT])
        hid_lh = sb("hid_lh", [P, 2, FC, 2 * NT], F32R)
        g_rows = sb("g_rows", [P, E, D])
        acc = sb("acc", [P, T, D])
        b2_rows = sb("b2_rows", [P, E, D])

        psum = ctx.enter_context(nc.psum_tensor("psum", [P, 8, 512], F32))

        scratch = nc.dram_tensor("shift_scratch", [T * P * (S + 1) * H], F32, kind="Internal")

        s_const, s_par, s_cls, s_wtok = sem("s_const"), sem("s_par"), sem("s_cls"), sem("s_wtok")
        s_xp = [sem(f"s_xp{t}") for t in range(T)]
        s_wqk, s_wv, s_wp, s_wf, s_bf = (sem(f"s_{x}") for x in ("wqk", "wv", "wp", "wf", "bf"))
        s_gw, s_b1, s_b2, s_g, s_lnb, s_clsrows = (sem(f"s_{x}") for x in ("gw", "b1", "b2", "g", "lnb", "clsrows"))
        s_w1raw = [sem(f"s_w1raw{i}") for i in range(2)]
        s_w2raw = [sem(f"s_w2raw{i}") for i in range(2)]
        names = """
            zeros bias2 hps hsb hbf var1 rstd1 xn tz xnT pos_ps p_sb p_quad qps q_ev vps v_ev kps k_ev
            k_quad z_cls cls_qk cls_v q0_ev k0_ev v0_ev z_spread emb_ps emb_a emb_v emb_out shift_in
            ac_ps added maxed subbed exped summed recip normed clsac_ps cls_max cls_exp cls_norm
            cls_bd cls_sub e0 tcls_ps tcls_ev te_ps te_ev te0_ps te0_ev pv_ps pv_ev wf_ps h2 h2cls wfcls_ps
            var2 rstd2 xt tx_ps tx_h tx_l gw_split gate_ps gate_sb tops diff dexp wE wET_ps wET wcol_ps
            wsel lnb_ps acc0
            w1h w1l w2h w2l hid_ps gelu hsplit o_ps r negm sq escale xb scaled p2
            gateT_ps gateT cls_row o_cls x_cls last_bias last_y last_g last_acc
            cls_var cls_rs y_cls clsout_ps clsout out vchain gchain
        """.split()
        sems = {n: sem("s_" + n) for n in names}

        block = ctx.enter_context(nc.Block())

        @block.sync
        def _(sp):
            sp.dma_start(w_tok[:, :, :], tok_w.rearrange("(k p) n -> p k n", p=P)).then_inc(s_wtok, 16)
            for t in range(T):
                sp.dma_start(xp_sb[:, t, :], xp[t]).then_inc(s_xp[t], 16)
            sp.dma_start(w_v[:, :, :], wv.rearrange("(k p) n -> p k n", p=P)).then_inc(s_wv, 16)
            sp.dma_start(bf_rows[:, :], bf.rearrange("(o d) -> o d", o=1).broadcast_to([P, D])).then_inc(s_bf, 16)
            for e in range(2):
                sp.dma_start(w1_raw[:, e, :].rearrange("p (k n) -> p k n", k=DC),
                             w1[e].rearrange("(k p) n -> p k n", p=P)).then_inc(s_w1raw[e], 16)
                sp.dma_start(w2_raw[:, e, :].rearrange("p (k n) -> p k n", k=FC),
                             w2[e].rearrange("(k p) n -> p k n", p=P)).then_inc(s_w2raw[e], 16)
            sp.dma_start(w_f[:, :, :], wf.rearrange("(k p) n -> p k n", p=P)).then_inc(s_wf, 16)
            sp.dma_start(w_gate[:, :, :], gate_w.rearrange("(k p) n -> p k n", p=P)).then_inc(s_gw, 16)
            sp.dma_start(b1_cols[:, :, :], b1t).then_inc(s_b1, 16)
            sp.dma_start(lnb_rows[:, :], ln_b).then_inc(s_lnb, 16)
            for dst, src in ((b2_cls, b2), (g_cls, ln_g), (lnb_cls, ln_b)):
                for e in range(E):
                    sp.dma_start(dst[e * B:(e + 1) * B, :], src[e:e + 1, :].broadcast_to([B, D]))\
                        .then_inc(s_clsrows, 16)
            for t in range(T):
                sp.wait_ge(sems["emb_a"], 2 * (t + 1))
                sp.wait_ge(sems["emb_v"], 2 * (t + 1))
                sp.dma_start(bass.AP(scratch, t * P * em_n, [[em_n, P], [1, em_n]]),
                             emb[:, t % 2, :, :].rearrange("p m h -> p (m h)")).then_inc(sems["emb_out"], 16)
                sp.wait_ge(sems["emb_out"], 16 * (t + 1))
                if t >= 2:
                    sp.wait_ge(sems["added"], t - 1)
                for i in range(2):
                    src = bass.AP(scratch, (t * P + i * NP) * em_n + (S - 1) * H, [[S * H, NP], [1, S * H]])
                    sp.dma_start(shifted[i * NP:(i + 1) * NP, t % 2, :, :].rearrange("p j h -> p (j h)"), src)\
                        .then_inc(sems["shift_in"], 16)
            sp.wait_ge(sems["wf_ps"], T + 1)
            sp.dma_start(b2_rows[:, :, :], b2.rearrange("(o e) d -> o e d", o=1).broadcast_to([P, E, D]))\
                .then_inc(s_b2, 16)
            sp.dma_start(g_rows[:, :, :], ln_g.rearrange("(o e) d -> o e d", o=1).broadcast_to([P, E, D]))\
                .then_inc(s_g, 16)

            def load_w1(e, p, n):
                sp.wait_ge(sems["w1h"], e - 1)
                sp.wait_ge(sems["w1l"], e - 1)
                sp.dma_start(w1_raw[:, p, :].rearrange("p (k n) -> p k n", k=DC),
                             w1[bass.ds(e, 1)].rearrange("o (k p) n -> p (o k) n", p=P)).then_inc(s_w1raw[p], 16)

            def load_w2(e, p, n):
                sp.wait_ge(sems["w2h"], e - 1)
                sp.wait_ge(sems["w2l"], e - 1)
                sp.dma_start(w2_raw[:, p, :].rearrange("p (k n) -> p k n", k=FC),
                             w2[bass.ds(e, 1)].rearrange("o (k p) n -> p (o k) n", p=P)).then_inc(s_w2raw[p], 16)

            with sp.Fori(0, (E - 2) // 2) as i:
                for p in range(2):
                    load_w1(2 * i + 2 + p, p, i)
                    load_w2(2 * i + 2 + p, p, i)
            for e in range(E):
                sp.wait_ge(sems["cls_row"], e + 1)
                for part in range(2):
                    sp.dma_start(o_cls[e * B:(e + 1) * B, part, :], cls_rows[part * B:(part + 1) * B, e, :])\
                        .then_inc(sems["o_cls"], 16)
            for t in range(T):
                if t < 2:
                    sp.wait_ge(sems["p2"], T * (E - 1) + t + 1)
                else:
                    sp.wait_ge(sems["last_acc"], t - 1)
                for i in range(2):
                    sp.dma_start(out[2 * t + i, 1:S, :], acc[i * NP:(i + 1) * NP, t, :]).then_inc(sems["out"], 16)
            sp.wait_ge(sems["clsout"], 1)
            sp.dma_start(out[:, 0, :], acc_cls[:, :]).then_inc(sems["out"], 16)
            sp.wait_ge(sems["out"], 16 * (2 * T + 1))

        def keys(pool, t, quad):
            pool.wait_ge(sems["k_ev"], 2 * (t + 1))
            if t == 0:
                pool.wait_ge(sems["k0_ev"], DC)
            for b in (2 * t, 2 * t + 1):
                for g in range(DC):
                    nc.gpsimd.tensor_tensor(k_quad[:, b, g, :, :],
                                            kT[:, g, b, :].unsqueeze(1).to_broadcast([P, QH, S]),
                                            quad.to_broadcast([P, QH, S]), ALU.mult)\
                        .then_inc(sems["k_quad"], 1)

        def split_w1(eng, e, p, landed):
            eng.wait_ge(s_w1raw[p], landed)
            eng.wait_ge(sems["w1h"], e + 1)
            nc.gpsimd.tensor_tensor(w1_l[:, p, :], w1_raw[:, p, :], w1_h[:, p, :].bitcast(F32), ALU.subtract)\
                .then_inc(sems["w1l"], 1)

        def split_w2(eng, e, p, landed):
            eng.wait_ge(s_w2raw[p], landed)
            eng.wait_ge(sems["w2h"], e + 1)
            nc.gpsimd.tensor_tensor(w2_l[:, p, :], w2_raw[:, p, :], w2_h[:, p, :].bitcast(F32), ALU.subtract)\
                .then_inc(sems["w2l"], 1)


        def w1_high(act, e, p, landed):
            act.wait_ge(s_w1raw[p], landed)
            if not isinstance(e, int) or e >= 2:
                act.wait_ge(sems["hid_ps"], FC * (e - 1))
                act.wait_ge(sems["w1l"], e - 1)
            nc.scalar.activation(w1_h[:, p, :], w1_raw[:, p, :], ACT.Copy).then_inc(sems["w1h"], 1)

        def w2_high(act, e, p, landed):
            act.wait_ge(s_w2raw[p], landed)
            if not isinstance(e, int) or e >= 2:
                act.wait_ge(sems["o_ps"], (T + 1) * (e - 1))
                act.wait_ge(sems["w2l"], e - 1)
            nc.scalar.activation(w2_h[:, p, :], w2_raw[:, p, :], ACT.Copy).then_inc(sems["w2h"], 1)

        def tx_high(act, n):
            rows = P if n < T else B
            c0 = B + n * P if n < T else 0
            act.wait_ge(sems["tx_ps"], n + 1)
            nc.scalar.activation(xT_h[:, :, c0:c0 + rows],
                                 psum[:, 4 + n % 2, 0:DC * rows].rearrange("p (k n) -> p k n", k=DC), ACT.Copy)\
                .then_inc(sems["tx_h"], 1)

        @block.gpsimd
        def _(pool):
            chain = [0]

            def link(ins):
                chain[0] += 1
                ins.then_inc(sems["gchain"], 1)
                pool.wait_ge(sems["gchain"], chain[0])

            nc.gpsimd.memset(emb[:, :, 0, :], 0.0).then_inc(sems["zeros"], 1)
            nc.gpsimd.memset(gate[:, T, :], 0.0).then_inc(sems["zeros"], 1)
            pool.wait_ge(s_const, 16)

            def rsqrt(col, rows, n, signal, src, dst):
                nc.gpsimd.tensor_tensor(dst, src, C[0:rows, at["power"][0]:at["power"][0] + n], ALU.pow)\
                    .then_inc(sems[signal], 1)

            def normalise(t):
                pool.wait_ge(sems["recip"], t + 1)
                if t >= 2:
                    pool.wait_ge(sems["te_ps"], 2 * (t - 1))
                    pool.wait_ge(sems["te0_ps"], t - 1)
                nc.gpsimd.tensor_tensor(prob[:, t % 2, :, :], score[:, t % 2, :, 1:S],
                                        ri[:, t % 2, :].unsqueeze(2).to_broadcast([P, H, NP]), ALU.mult)\
                    .then_inc(sems["normed"], 1)
                nc.gpsimd.tensor_tensor(prob0[:, t % 2, :], score[:, t % 2, :, 0], ri[:, t % 2, :], ALU.mult)\
                    .then_inc(sems["normed"], 1)

            pool.wait_ge(sems["var1"], 1)
            rsqrt(T, B, 1, "rstd1", var[0:B, T:T + 1], rstd[0:B, T:T + 1])
            quad = const("quad").unsqueeze(2)
            for t in range(T):
                pool.wait_ge(sems["var1"], t + 2)
                rsqrt(t, P, 1, "rstd1", var[:, t:t + 1], rstd[:, t:t + 1])
            for t in range(T):
                keys(pool, t, quad)
                if t >= 2:
                    normalise(t - 2)
            pool.wait_ge(sems["xn"], T + 1)
            pool.wait_ge(sems["hsb"], T)
            pool.wait_ge(s_bf, 16)
            nc.gpsimd.tensor_tensor(h_tok[:, :, :], h_tok[:, :, :],
                                    bf_rows[:, :].unsqueeze(1).to_broadcast([P, T, D]), ALU.add)\
                .then_inc(sems["hbf"], 1)
            nc.gpsimd.tensor_tensor(h_cls[:, :], h_cls[:, :], bf_rows[0:B, :], ALU.add).then_inc(sems["hbf"], 1)
            def rstd2(n):
                pool.wait_ge(sems["var2"], n + 1)
                rsqrt(n, P, 1, "rstd2", var[:, n:n + 1], rstd[:, n:n + 1])

            split_w1(pool, 0, 0, 16)
            split_w1(pool, 1, 1, 16)
            normalise(2)
            split_w2(pool, 0, 0, 16)
            normalise(3)
            rstd2(0)
            rstd2(1)
            rstd2(T - 2)
            rstd2(T - 1)
            pool.wait_ge(sems["var2"], T + 1)
            rsqrt(T, B, 1, "rstd2", var[0:B, T:T + 1], rstd[0:B, T:T + 1])

            def plus_b2(e, p):
                if not isinstance(e, int) or e >= 2:
                    pool.wait_ge(sems["r"], T * (e - 1))
                nc.gpsimd.tensor_tensor(xb[:, p, :, :], xn[:, :, :],
                                        b2_rows[:, bass.ds(e, 1), :].to_broadcast([P, T, D]), ALU.add)\
                    .then_inc(sems["xb"], 1)

            def scale_of(e, p, t0=0, n=T, done=0):
                pool.wait_ge(sems["sq"], T * e + t0 + n)
                ts = slice(t0, t0 + n)
                nc.gpsimd.tensor_tensor(e_var[:, p, ts], sq_sum[:, p, ts], const("eps")[:, ts], ALU.add)\
                    .then_inc(sems["escale"], 1)
                pool.wait_ge(sems["escale"], 3 * e + done + 1)
                nc.gpsimd.tensor_tensor(e_rstd[:, p, ts], e_var[:, p, ts],
                                        C[:, at["power"][0]:at["power"][0] + n], ALU.pow)\
                    .then_inc(sems["escale"], 1)
                pool.wait_ge(sems["escale"], 3 * e + done + 2)
                nc.gpsimd.tensor_tensor(e_scale[:, p, ts], e_rstd[:, p, ts], wE_of(e)[:, ts], ALU.mult)\
                    .then_inc(sems["escale"], 1)

            def wE_of(e):
                return wE_d[:, 0:T, bass.ds(e, 1)].rearrange("p t o -> p (t o)")

            pool.wait_ge(s_b2, 16)
            pool.wait_ge(sems["xt"], T + 1)
            plus_b2(0, 0)
            pool.wait_ge(sems["wE"], 2)

            def slot(e, p, k):
                if not isinstance(e, int) or e + 1 < E:
                    split_w2(pool, e + 1, 1 - p, 16 * (k + 1 + p))
                if not isinstance(e, int) or e + 2 < E:
                    split_w1(pool, e + 2, p, 16 * (k + 2))
                if not isinstance(e, int) or e + 1 < E:
                    plus_b2(e + 1, 1 - p)
                scale_of(e, p)

            slot(0, 0, 0)
            with pool.Fori(0, 2) as i:
                slot(2 * i + 1, 1, i)
                slot(2 * i + 2, 0, i + 1)
            for e in range(5, E - 1):
                slot(e, e % 2, e // 2)
            e, p = E - 1, (E - 1) % 2
            scale_of(e, p, 0, 2)
            pool.wait_ge(sems["cls_var"], 1)
            nc.gpsimd.tensor_tensor(cls_small[:, 4:5], cls_small[:, 3:4],
                                    C[0:E * B, at["power"][0]:at["power"][0] + 1], ALU.pow)\
                .then_inc(sems["cls_rs"], 1)
            scale_of(e, p, 2, 2, 3)
            pool.wait_ge(sems["negm"], T * E)
            pool.wait_ge(sems["escale"], 3 * e + 6)
            nc.gpsimd.tensor_tensor(last_bias[:, :], neg_mean[:, p, 2:T], e_scale[:, p, 2:T], ALU.mult)\
                .then_inc(sems["last_bias"], 1)
            for t in range(2, T):
                pool.wait_ge(sems["last_y"], t - 1)
                nc.gpsimd.tensor_tensor(last_y[:, t - 2, :], last_y[:, t - 2, :], g_rows[:, e, :], ALU.mult)\
                    .then_inc(sems["last_g"], 1)
                pool.wait_ge(sems["last_g"], t - 1)
                pool.wait_ge(sems["p2"], T * (E - 2) + t + 1)
                nc.gpsimd.tensor_tensor(acc[:, t, :], acc[:, t, :], last_y[:, t - 2, :], ALU.add)\
                    .then_inc(sems["last_acc"], 1)

        @block.scalar
        def _(act):
            act.dma_start(PAR[:, :], params).then_inc(s_par, 16)
            act.dma_start(h_cls[:, :], cls_tok.rearrange("a b d -> (a b) d").broadcast_to([B, D])).then_inc(s_cls, 16)
            act.dma_start(C[:, :], consts).then_inc(s_const, 16)
            act.dma_start(w_p[:, :, :], wpos.rearrange("(k p) n -> p k n", p=P)).then_inc(s_wp, 16)
            act.dma_start(w_q[:, :, :], wq.rearrange("(k p) n -> p k n", p=P)).then_inc(s_wqk, 16)
            act.dma_start(w_k[:, :, :], wk.rearrange("(k p) n -> p k n", p=P)).then_inc(s_wqk, 16)
            act.wait_ge(s_par, 16)
            for t in range(T):
                act.wait_ge(sems["hps"], t + 1)
                nc.scalar.activation(h_tok[:, t, :], psum[:, t, 0:D], ACT.Copy).then_inc(sems["hsb"], 1)
            act.wait_ge(sems["tz"], 1)
            for k in range(DC):
                nc.scalar.activation(xnT_cls[:, k, :], psum[:, 5, k * B:(k + 1) * B], ACT.Identity,
                                     scale=par("gamma", k), bias=par("beta", k)).then_inc(sems["xnT"], 1)
            act.wait_ge(sems["bias2"], 2)
            def norm_turned(n):
                act.wait_ge(sems["tz"], n + 2)
                if n >= 2:
                    act.wait_ge(sems["vps"], n - 1)
                for k in range(DC):
                    nc.scalar.activation(xnT[:, n % 2, k, :, :, :],
                                         psum[:, 4 + n % 2, k * P:(k + 1) * P]
                                         .rearrange("p (i s) -> p i s", i=2).unsqueeze(2)
                                         .to_broadcast([P, 2, 2, NP]), ACT.Identity, scale=par("gamma", k), bias=par("beta", k))\
                        .then_inc(sems["xnT"], 1)

            def exponential(t):
                act.wait_ge(sems["subbed"], t + 1)
                nc.scalar.activation(score[:, t % 2, :, :], score[:, t % 2, :, :], ACT.Exp,
                                     scale=1.0 / float(D) ** 0.5).then_inc(sems["exped"], 1)

            norm_turned(0)
            for n in range(T):
                act.wait_ge(sems["qps"], n + 1)
                for g in range(DC):
                    q_ps = psum[:, 6, g * P:(g + 1) * P]
                    for dst, bias in ((quT, bqu), (qvT, bqv)):
                        nc.scalar.activation(dst[:, g, n * P:(n + 1) * P], q_ps, ACT.Identity,
                                             bias=bias[:, g:g + 1]).then_inc(sems["q_ev"], 1)
                if n + 1 < T:
                    norm_turned(n + 1)
                if n >= 2:
                    exponential(n - 2)
                if n == 0:
                    act.wait_ge(sems["zeros"], 2)
                if n >= 2:
                    act.wait_ge(sems["emb_out"], 16 * (n - 1))
                for q in range(2):
                    act.wait_ge(sems["emb_ps"], NQ * n + q + 1)
                    nc.scalar.activation(emb[:, n % 2, 1:S + 1, q * QH:(q + 1) * QH].rearrange("p m h -> p h m"),
                                         psum[:, q, 0:QC].rearrange("p (h m) -> p h m", h=QH), ACT.Copy)\
                        .then_inc(sems["emb_a"], 1)
            def turned(t):
                for half in range(2):
                    act.wait_ge(sems["te_ps"], 2 * t + half + 1)
                    for i in range(2):
                        nc.scalar.activation(probT[:, 2 * t + i, 4 * half:4 * half + 4, 1:S],
                                             psum[:, 4 + half, :].rearrange("p (h i s) -> p h i s", h=4, i=2)[:, :, i, :],
                                             ACT.Copy).then_inc(sems["te_ev"], 1)

            turned(0)
            act.wait_ge(sems["cls_sub"], 1)
            nc.scalar.activation(e_cls[:, :], e_cls[:, :], ACT.Exp, scale=1.0 / float(D) ** 0.5,
                                 accum_out=small[:, 1:2]).then_inc(sems["cls_exp"], 1)
            exponential(2)
            w1_high(act, 0, 0, 16)
            w1_high(act, 1, 1, 16)
            w2_high(act, 0, 0, 16)
            for t in range(T):
                if t >= 1:
                    turned(t)
                act.wait_ge(sems["te0_ps"], t + 1)
                nc.scalar.activation(probT_cls[:, 2 * t:2 * t + 2, 1:S],
                                     psum[0:H, 7, 3 * P:4 * P].rearrange("p (i s) -> p i s", i=2), ACT.Copy)\
                    .then_inc(sems["te0_ev"], 1)
                if t >= 2:
                    tx_high(act, t - 2)
                act.wait_ge(sems["pv_ps"], t + 1)
                o_ps = psum[:, 7, 0:DC * 2 * S].rearrange("p (g i s) -> p g i s", g=DC, i=2)
                for g in range(DC):
                    nc.scalar.activation(outT[:, g, 2 * t:2 * t + 2, :], o_ps[:, g, :, 1:S], ACT.Identity,
                                         bias=par("bv", g)).then_inc(sems["pv_ev"], 1)
                for g in range(DC):
                    nc.scalar.activation(outT_cls[:, g, 2 * t:2 * t + 2], o_ps[:, g, :, 0], ACT.Identity,
                                         bias=par("bv", g)).then_inc(sems["pv_ev"], 1)
                if t == 0:
                    exponential(T - 1)
            for n in range(T - 2, T + 1):
                tx_high(act, n)
            act.wait_ge(sems["gateT_ps"], 1)
            nc.scalar.activation(gateT[:, 0:HALF - B], psum[0:E, 6, B:HALF], ACT.Copy).then_inc(sems["gateT"], 1)
            nc.scalar.activation(gateT[:, HALF - B:T * P], psum[0:E, 7, 0:HALF], ACT.Copy).then_inc(sems["gateT"], 1)
            nc.scalar.activation(gateT_cls[:, :], psum[0:E, 6, 0:B], ACT.Copy).then_inc(sems["gateT"], 1)
            act.wait_ge(sems["diff"], 1)
            nc.scalar.activation(tw[:, :, 1], tw[:, :, 0], ACT.Exp).then_inc(sems["dexp"], 1)
            act.wait_ge(s_b1, 16)

            def hidden(e, p, m):
                act.wait_ge(sems["hid_ps"], FC * e + m + 1)
                if not isinstance(e, int) or e >= 1:
                    act.wait_ge(sems["hsplit"], 2 * (FC * (e - 1) + m + 1))
                if not isinstance(e, int) or e >= 2:
                    act.wait_ge(sems["o_ps"], (T + 1) * (e - 1))
                for dst in (hid[:, m, :], hid_lh[:, p, m, NT:2 * NT]):
                    nc.scalar.activation(dst.rearrange("p (a n) -> p a n", a=2),
                                         psum[:, 2 * (m % 2):2 * (m % 2) + 2, 0:HALF], ACT.Gelu,
                                         bias=b1_cols[:, bass.ds(e, 1), m]).then_inc(sems["gelu"], 1)

            def square(e, p, t):
                act.wait_ge(sems["negm"], T * e + t + 1)
                if not isinstance(e, int) or T * e + t > 1:
                    act.wait_ge(sems["sq"], T * e + t - 1)
                nc.scalar.activation(sq_junk[t % 2], res[:, p, t, :], ACT.Square, bias=neg_mean[:, p, t:t + 1],
                                     accum_out=sq_sum[:, p, t:t + 1]).then_inc(sems["sq"], 1)

            for m in range(FC):
                hidden(0, 0, m)

            def cls_row(e):
                act.wait_ge(sems["o_ps"], (T + 1) * e + (1 if isinstance(e, int) and e == E - 1 else T + 1))
                nc.scalar.activation(cls_rows[:, bass.ds(e, 1), :].rearrange("p o d -> p (o d)"),
                                     psum[0:2 * B, 6, 0:D], ACT.Copy).then_inc(sems["cls_row"], 1)

            def slot(e, p, k):
                for m in range(FC):
                    hidden(e + 1, 1 - p, m)
                    if m == 0 and (not isinstance(e, int) or e >= 1):
                        cls_row(e - 1)
                    if m >= 1:
                        square(e, p, m - 1)
                    if m == 0:
                        w2_high(act, e + 1, 1 - p, 16 * (k + 1 + p))
                    if m == 1 and (not isinstance(e, int) or e + 2 < E):
                        w1_high(act, e + 2, p, 16 * (k + 2))
                square(e, p, FC - 1)

            slot(0, 0, 0)
            with act.Fori(0, 2) as i:
                slot(2 * i + 1, 1, i)
                slot(2 * i + 2, 0, i + 1)
            for e in range(5, E - 1):
                slot(e, e % 2, e // 2)
            cls_row(E - 2)
            cls_row(E - 1)
            e, p = E - 1, (E - 1) % 2
            for t in range(T):
                square(e, p, t)
            act.wait_ge(sems["last_bias"], 1)
            for t in range(2, T):
                nc.scalar.activation(last_y[:, t - 2, :], res[:, p, t, :], ACT.Identity, scale=e_scale[:, p, t:t + 1],
                                     bias=last_bias[:, t - 2:t - 1]).then_inc(sems["last_y"], 1)

        @block.vector
        def _(dve):
            chain = [0]

            def link(ins):
                chain[0] += 1
                ins.then_inc(sems["vchain"], 1)
                dve.wait_ge(sems["vchain"], chain[0])

            def norm1(x, rows, n):
                link(nc.vector.bn_stats(stats[0:rows, n, :], x))
                link(nc.vector.bn_aggr(mv[0:rows, n, :], stats[0:rows, n, :]))
                nc.vector.tensor_scalar(var[0:rows, n:n + 1], mv[0:rows, n, 1:2], 1.0 + EPS, EPS * EPS,
                                        ALU.mult, ALU.add).then_inc(sems["var1"], 1)

            def scale1(x, dst, rows, n, count):
                dve.wait_ge(sems["rstd1"], count)
                nc.vector.tensor_scalar(dst, x, mv[0:rows, n, 0:1], rstd[0:rows, n:n + 1], ALU.subtract, ALU.mult)\
                    .then_inc(sems["xn"], 1)

            dve.wait_ge(s_cls, 16)
            norm1(h_cls[:, :], B, T)
            dve.wait_ge(s_par, 16)
            nc.vector.tensor_tensor(bqu[:, :], PAR[:, 0:DC], PAR[:, 3 * DC:4 * DC], ALU.add).then_inc(sems["bias2"], 1)
            nc.vector.tensor_tensor(bqv[:, :], PAR[:, 0:DC], PAR[:, 4 * DC:5 * DC], ALU.add).then_inc(sems["bias2"], 1)
            scale1(h_cls[:, :], xn_cls[:, :], B, T, 1)
            for t in range(T):
                dve.wait_ge(sems["hsb"], t + 1)
                norm1(h_tok[:, t, :], P, t)
            dve.wait_ge(s_const, 16)
            dve.wait_ge(sems["pos_ps"], 1)
            pos = psum[:, 4, 0:DC * S].rearrange("p (g s) -> p g s", g=DC)
            link(nc.vector.tensor_copy(pT[:, :, :], pos))
            for g in range(DC):
                nc.vector.tensor_tensor(p_quad[:, g, :, :], pT[:, g, :].unsqueeze(1).to_broadcast([P, QH, S]),
                                        const("quad").unsqueeze(2).to_broadcast([P, QH, S]), ALU.mult)\
                    .then_inc(sems["p_quad"], 1)
            dve.wait_ge(sems["bias2"], 2)
            dve.wait_ge(sems["cls_qk"], 1)
            cq = psum[:, 6, 0:4 * B].rearrange("p (c g b) -> p c g b", c=2, g=DC)
            for g in range(DC):
                nc.vector.tensor_scalar(q0u[:, g, :], cq[:, 0, g, :], bqu[:, g:g + 1], None, ALU.add)\
                    .then_inc(sems["q0_ev"], 1)
                nc.vector.tensor_scalar(q0v[:, g, :], cq[:, 0, g, :], bqv[:, g:g + 1], None, ALU.add)\
                    .then_inc(sems["q0_ev"], 1)
                nc.vector.tensor_scalar(kT[:, g, :, 0], cq[:, 1, g, :], par("bk", g), None, ALU.add)\
                    .then_inc(sems["k0_ev"], 1)
            dve.wait_ge(sems["cls_v"], 1)
            nc.vector.tensor_tensor(v0_row[:, :], psum[0:H, 7, 0:D], const("headrow", H), ALU.mult)\
                .then_inc(sems["v0_ev"], 1)
            dve.wait_ge(sems["zeros"], 2)
            dve.wait_ge(sems["q0_ev"], 2 * DC)
            for g in range(DC):
                head = const("head")[:, g * H:(g + 1) * H]
                nc.vector.tensor_tensor(z_cls[:, g, :, :], head.unsqueeze(1).to_broadcast([P, B, H]),
                                        q0u[:, g, :].unsqueeze(2).to_broadcast([P, B, H]), ALU.mult)\
                    .then_inc(sems["z_spread"], 1)
                nc.vector.tensor_tensor(z_last[:, g, :, :], head.unsqueeze(1).to_broadcast([P, B, H]),
                                        q0v[:, g, :].unsqueeze(2).to_broadcast([P, B, H]), ALU.mult)\
                    .then_inc(sems["z_spread"], 1)

            def scores(t):
                p = t % 2
                dve.wait_ge(sems["ac_ps"], t + 1)
                dve.wait_ge(sems["shift_in"], 32 * (t + 1))
                if t >= 2:
                    dve.wait_ge(sems["normed"], 2 * (t - 1))
                nc.vector.tensor_tensor(score[:, p, :, :].rearrange("p (q h) j -> p q h j", q=NQ),
                                        psum[:, 0:NQ, 0:QC].rearrange("p q (h j) -> p q h j", h=QH),
                                        shifted[:, p, :, :].rearrange("p j (q h) -> p q h j", q=NQ), ALU.add)\
                    .then_inc(sems["added"], 1)

            def less_maximum(t):
                p = t % 2
                dve.wait_ge(sems["added"], t + 1)
                nc.vector.tensor_reduce(mx[:, p, :], score[:, p, :, :], AX, ALU.max).then_inc(sems["maxed"], 1)
                dve.wait_ge(sems["maxed"], t + 1)
                nc.vector.tensor_tensor(score[:, p, :, :], score[:, p, :, :],
                                        mx[:, p, :].unsqueeze(2).to_broadcast([P, H, S]), ALU.subtract)\
                    .then_inc(sems["subbed"], 1)

            def sums(t):
                p = t % 2
                dve.wait_ge(sems["exped"], t + 1)
                nc.vector.tensor_reduce(rs[:, p, :], score[:, p, :, :], AX, ALU.add).then_inc(sems["summed"], 1)
                dve.wait_ge(sems["summed"], t + 1)
                nc.vector.reciprocal(ri[:, p, :], rs[:, p, :]).then_inc(sems["recip"], 1)

            def spread_next():
                dve.wait_ge(sems["q_ev"], 4 * T)
                for g in range(DC):
                    first = qvT[:, g, :].rearrange("p (b n) -> p b n", b=B)[:, :, 0:1]
                    nc.vector.tensor_tensor(z_next[:, g, :, :],
                                            const("head")[:, g * H:(g + 1) * H].unsqueeze(1).to_broadcast([P, B, H]),
                                            first.to_broadcast([P, B, H]), ALU.mult).then_inc(sems["z_spread"], 1)

            for n in range(T):
                scale1(h_tok[:, n, :], xn[:, n, :], P, n, n + 2)
            for n in range(T):
                dve.wait_ge(sems["kps"], n + 1)
                for g in range(DC):
                    nc.vector.tensor_scalar(kT[:, g, 2 * n:2 * n + 2, 1:S],
                                            psum[:, 4 + n % 2, (2 + g) * P:(3 + g) * P].rearrange("p (i s) -> p i s", i=2),
                                            par("bk", g), None, ALU.add).then_inc(sems["k_ev"], 1)
                dve.wait_ge(sems["vps"], n + 1)
                nc.vector.tensor_tensor(v_pair[:, 2 * n:2 * n + 2, :],
                                        psum[:, 7, :].rearrange("p (i d) -> p i d", i=2),
                                        const("parity").unsqueeze(1).to_broadcast([P, 2, D]), ALU.mult)\
                    .then_inc(sems["v_ev"], 1)
                if n >= 2:
                    dve.wait_ge(sems["emb_out"], 16 * (n - 1))
                for q in (2, 3):
                    dve.wait_ge(sems["emb_ps"], NQ * n + q + 1)
                    nc.vector.tensor_copy(emb[:, n % 2, 1:S + 1, q * QH:(q + 1) * QH].rearrange("p m h -> p h m"),
                                          psum[:, q, 0:QC].rearrange("p (h m) -> p h m", h=QH))\
                        .then_inc(sems["emb_v"], 1)
                if n == T - 1:
                    spread_next()
                if n >= 2:
                    sums(n - 2)
                if n in (1, 2):
                    scores(n - 1)
                    less_maximum(n - 1)
            def norm2(n):
                rows = P if n < T else B
                h = h_tok[:, n, :] if n < T else h_cls[:, :]
                dve.wait_ge(sems["wf_ps"], n + 1)
                if n == 0:
                    dve.wait_ge(sems["hbf"], 2)
                dve_h2 = nc.vector.tensor_tensor(h, psum[0:rows, 6 if n < T else 0, 0:D], h, ALU.add)
                dve_h2.then_inc(sems["h2"], 1)
                dve.wait_ge(sems["h2"], n + 1)
                link(nc.vector.bn_stats(stats[0:rows, n, :], h))
                link(nc.vector.bn_aggr(mv[0:rows, n, :], stats[0:rows, n, :]))
                nc.vector.tensor_scalar(var[0:rows, n:n + 1], mv[0:rows, n, 1:2], EPS, None, ALU.add)\
                    .then_inc(sems["var2"], 1)

            def norm2_scale(n):
                rows = P if n < T else B
                h = h_tok[:, n, :] if n < T else h_cls[:, :]
                x = xn[:, n, :] if n < T else xn_cls[:, :]
                dve.wait_ge(sems["rstd2"], n + 1)
                nc.vector.tensor_scalar(x, h, mv[0:rows, n, 0:1], rstd[0:rows, n:n + 1], ALU.subtract, ALU.mult)\
                    .then_inc(sems["xt"], 1)

            def tx_low(n):
                rows = P if n < T else B
                c0 = B + n * P if n < T else 0
                dve.wait_ge(sems["tx_h"], n + 1)
                nc.vector.tensor_tensor(xT_l[:, :, c0:c0 + rows],
                                        psum[:, 4 + n % 2, 0:DC * rows].rearrange("p (k n) -> p k n", k=DC),
                                        xT_h[:, :, c0:c0 + rows].bitcast(F32), ALU.subtract).then_inc(sems["tx_l"], 1)

            dve.wait_ge(sems["clsac_ps"], 1)
            link(nc.vector.tensor_tensor(cls_all[:, :].rearrange("p (a b s) -> p a b s", a=2, b=4),
                                         psum[:, 6:8, 0:4 * S].rearrange("p a (b s) -> p a b s", b=4),
                                         const("image").rearrange("p (a b) -> p a b", a=2).unsqueeze(3)
                                         .to_broadcast([P, 2, 4, S]), ALU.mult))
            link(nc.vector.tensor_reduce(e_cls[:, :], cls_all[:, :].rearrange("p (b s) -> p s b", b=B), AX, ALU.add))
            nc.vector.tensor_tensor(e_cls[:, 0:1], e_cls[:, 0:1], psum[:, 7, 4 * S:4 * S + 1], ALU.add)\
                .then_inc(sems["cls_bd"], 1)
            nc.vector.tensor_tensor(e_cls[:, 2:S], e_cls[:, 2:S], psum[:, 7, 4 * S + 2:5 * S], ALU.add)\
                .then_inc(sems["cls_bd"], 1)
            dve.wait_ge(sems["cls_bd"], 2)
            link(nc.vector.tensor_reduce(small[:, 0:1], e_cls[:, :], AX, ALU.max))
            nc.vector.tensor_scalar(e_cls[:, :], e_cls[:, :], small[:, 0:1], None, ALU.subtract)\
                .then_inc(sems["cls_sub"], 1)
            dve.wait_ge(sems["cls_exp"], 1)
            link(nc.vector.reciprocal(small[:, 2:3], small[:, 1:2]))
            nc.vector.tensor_scalar(p_cls[:, :, :], e_cls[:, 1:S].unsqueeze(1).to_broadcast([P, 2, NP]),
                                    small[:, 2:3], None, ALU.mult).then_inc(sems["cls_norm"], 1)
            nc.vector.tensor_scalar(e_cls0[:, :], const("image"), e_cls[:, 0:1], small[:, 2:3], ALU.mult, ALU.mult)\
                .then_inc(sems["e0"], 1)
            dve.wait_ge(s_gw, 16)
            nc.vector.tensor_copy(w_gate_h[:, :, :], w_gate[:, :, :]).then_inc(sems["gw_split"], 1)
            dve.wait_ge(sems["gw_split"], 1)
            nc.vector.tensor_tensor(w_gate_l[:, :, :], w_gate[:, :, :], w_gate_h[:, :, :].bitcast(F32), ALU.subtract)\
                .then_inc(sems["gw_split"], 1)
            scores(2)
            dve.wait_ge(sems["tcls_ps"], 1)
            for par_ in range(2):
                rows = slice(par_ * NP, (par_ + 1) * NP)
                nc.vector.tensor_copy(probT[rows, :, :, 0],
                                      psum[rows, 7, 0:P].rearrange("p (b h a) -> p b h a", b=B, a=2)[:, :, :, par_])\
                    .then_inc(sems["tcls_ev"], 1)
            nc.vector.tensor_copy(probT_cls[:, :, 0], psum[0:H, 7, P:P + B]).then_inc(sems["tcls_ev"], 1)
            less_maximum(2)
            sums(2)
            scores(3)
            less_maximum(3)
            sums(3)
            for n in range(T - 1):
                norm2(n)
                norm2_scale(n)
                if n >= 1:
                    tx_low(n - 1)
            norm2(T - 1)
            norm2(T)
            norm2_scale(T - 1)
            norm2_scale(T)
            for n in range(T - 2, T + 1):
                tx_low(n)

            dve.wait_ge(sems["gate_ps"], 1)
            nc.vector.tensor_copy(gate[:, 0:T, :], psum[:, 7, 0:T * E].rearrange("p (t n) -> p t n", t=T))\
                .then_inc(sems["gate_sb"], 1)
            nc.vector.tensor_copy(gate[0:B, T, :], psum[0:B, 7, T * E:(T + 1) * E]).then_inc(sems["gate_sb"], 1)
            dve.wait_ge(sems["gate_sb"], 2)
            for n in range(T + 1):
                nc.vector.max(top[:, n, :], gate[:, n, :]).then_inc(sems["tops"], 1)
            dve.wait_ge(sems["tops"], T + 1)
            for n in range(T + 1):
                nc.vector.max_index(top_at[:, n, :], top[:, n, :], gate[:, n, :]).then_inc(sems["tops"], 1)
            nc.vector.tensor_tensor(tw[:, :, 0], top[:, :, 1], top[:, :, 0], ALU.subtract).then_inc(sems["diff"], 1)
            dve.wait_ge(sems["tops"], 2 * (T + 1))
            link(nc.vector.tensor_copy(top_atf[:, :, :], top_at[:, :, 0:2]))
            dve.wait_ge(sems["dexp"], 1)
            link(nc.vector.tensor_scalar(tw[:, :, 2], tw[:, :, 1], 1.0, None, ALU.add))
            link(nc.vector.reciprocal(tw[:, :, 3], tw[:, :, 2]))
            link(nc.vector.tensor_tensor(tw[:, :, 2], tw[:, :, 3], tw[:, :, 1], ALU.mult))
            for k in range(2):
                link(nc.vector.tensor_tensor(pick[:, k, :, :], const("iota").unsqueeze(1).to_broadcast([P, T + 1, E]),
                                             top_atf[:, :, k:k + 1].to_broadcast([P, T + 1, E]), ALU.is_equal))
                link(nc.vector.tensor_tensor(pick[:, k, :, :], pick[:, k, :, :],
                                             tw[:, :, 3 - k:4 - k].to_broadcast([P, T + 1, E]), ALU.mult))
            nc.vector.tensor_tensor(wE[:, :, :], pick[:, 0, :, :], pick[:, 1, :, :], ALU.add).then_inc(sems["wE"], 1)
            dve.wait_ge(sems["wE"], 1)
            nc.vector.tensor_scalar(wE_d[:, :, :], wE[:, :, :], float(D) ** 0.5, None, ALU.mult).then_inc(sems["wE"], 1)

            def hsplit(e, p, m):
                dve.wait_ge(sems["gelu"], 2 * (FC * e + m + 1))
                if not isinstance(e, int) or e >= 2:
                    dve.wait_ge(sems["o_ps"], (T + 1) * (e - 1))
                nc.vector.tensor_tensor(hid_lh[:, p, m, T * P:NT], hid[:, m, 0:B],
                                        hid_lh[:, p, m, NT:NT + B].bitcast(F32), ALU.subtract)\
                    .then_inc(sems["hsplit"], 1)
                nc.vector.tensor_tensor(hid_lh[:, p, m, 0:T * P], hid[:, m, B:NT],
                                        hid_lh[:, p, m, NT + B:2 * NT].bitcast(F32), ALU.subtract)\
                    .then_inc(sems["hsplit"], 1)

            def residual(e, p, t):
                last = isinstance(e, int) and e == E - 1
                dve.wait_ge(sems["o_ps"], (T + 1) * e + t + (2 if last else 1))
                if t == 0:
                    dve.wait_ge(sems["xb"], e + 1)
                nc.vector.scalar_tensor_tensor(res[:, p, t, :], psum[:, 4 + t % 2, 0:D], 1.0, xb[:, p, t, :],
                                               ALU.mult, ALU.add, accum_out=res_sum[:, p, t:t + 1])\
                    .then_inc(sems["r"], 1)
                dve.wait_ge(sems["r"], T * e + t + 1)
                nc.vector.tensor_scalar(neg_mean[:, p, t:t + 1], res_sum[:, p, t:t + 1], -1.0 / D, None, ALU.mult)\
                    .then_inc(sems["negm"], 1)

            def add_expert(e, p, t):
                if t == 0:
                    dve.wait_ge(sems["escale"], 3 * e + 3)
                if t >= 1 or isinstance(e, int) and e >= 1:
                    dve.wait_ge(sems["p2"], T * e + t)
                nc.vector.scalar_tensor_tensor(scaled[:, :], res[:, p, t, :], neg_mean[:, p, t:t + 1],
                                               g_rows[:, bass.ds(e, 1), :].rearrange("p o d -> p (o d)"),
                                               ALU.add, ALU.mult).then_inc(sems["scaled"], 1)
                dve.wait_ge(sems["scaled"], T * e + t + 1)
                nc.vector.scalar_tensor_tensor(acc[:, t, :], scaled[:, :], e_scale[:, p, t:t + 1], acc[:, t, :],
                                               ALU.mult, ALU.add).then_inc(sems["p2"], 1)

            for m in range(FC):
                hsplit(0, 0, m)
            dve.wait_ge(sems["wET_ps"], 1)
            nc.vector.tensor_copy(wET[:, :, :], psum[0:E, 7, 0:T * P].rearrange("p (t n) -> p t n", t=T))\
                .then_inc(sems["wET"], 1)
            def start_acc(t):
                dve.wait_ge(sems["lnb_ps"], t + 1)
                nc.vector.tensor_tensor(acc[:, t, :], psum[:, 6 + t % 2, 0:D], h_tok[:, t, :], ALU.add)\
                    .then_inc(sems["acc0"], 1)

            def class_rows():
                dve.wait_ge(sems["wcol_ps"], 1)
                nc.vector.tensor_tensor_reduce(wcol_x[:, :], psum[0:E * B, 7, D:D + E], const("expert", E * B), 1.0, 0.0,
                                               ALU.mult, ALU.add, wcol[:, :]).then_inc(sems["wsel"], 1)
                dve.wait_ge(sems["wsel"], 1)
                nc.vector.tensor_scalar(wsel[:, :], const("imageof", E * B), wcol[:, :], None, ALU.mult)\
                    .then_inc(sems["wsel"], 1)
                dve.wait_ge(s_clsrows, 16 * 3 * E)
                nc.vector.tensor_tensor(x_cls[:, :], psum[0:E * B, 7, 0:D], b2_cls[:, :], ALU.add)\
                    .then_inc(sems["x_cls"], 1)

            def slot(e, p, k):
                for m in range(FC):
                    hsplit(e + 1, 1 - p, m)
                    if isinstance(e, int) and e == 0 and m < 2:
                        start_acc(2 * m)
                        start_acc(2 * m + 1)
                    residual(e, p, m)
                    if not isinstance(e, int) or e >= 1:
                        add_expert(e - 1, 1 - p, m)
                    if isinstance(e, int) and e == 0 and m == 2:
                        class_rows()

            slot(0, 0, 0)
            dve.wait_ge(s_g, 16)
            with dve.Fori(0, 2) as i:
                slot(2 * i + 1, 1, i)
                slot(2 * i + 2, 0, i + 1)
            for e in range(5, E - 1):
                slot(e, e % 2, e // 2)
            e, p = E - 1, (E - 1) % 2
            for m in range(T):
                residual(e, p, m)
                add_expert(e - 1, 1 - p, m)
                if m == 2:
                    dve.wait_ge(sems["o_cls"], 16 * 2 * E)
                    dve.wait_ge(sems["x_cls"], 1)
                    link(nc.vector.tensor_tensor(r_cls[:, :], o_cls[:, 0, :], o_cls[:, 1, :], ALU.add))
                    link(nc.vector.tensor_tensor(r_cls[:, :], r_cls[:, :], x_cls[:, :], ALU.add))
                    link(nc.vector.bn_stats(stats[0:E * B, T, :], r_cls[:, :]))
                    link(nc.vector.bn_aggr(mv[0:E * B, T, :], stats[0:E * B, T, :]))
                    nc.vector.tensor_scalar(cls_small[:, 3:4], mv[0:E * B, T, 1:2], EPS_FFN, None, ALU.add)\
                        .then_inc(sems["cls_var"], 1)
                    link(nc.vector.scalar_tensor_tensor(r_cls[:, :], r_cls[:, :], mv[0:E * B, T, 0:1], g_cls[:, :],
                                                        ALU.subtract, ALU.mult))
            dve.wait_ge(sems["cls_rs"], 1)
            nc.vector.scalar_tensor_tensor(r_cls[:, :], r_cls[:, :], cls_small[:, 4:5], lnb_cls[:, :],
                                           ALU.mult, ALU.add).then_inc(sems["y_cls"], 1)
            for t in range(2):
                add_expert(e, p, t)
            dve.wait_ge(sems["clsout_ps"], 1)
            nc.vector.tensor_tensor(acc_cls[:, :], psum[0:B, 7, 0:D], h_cls[:, :], ALU.add).then_inc(sems["clsout"], 1)

        @block.tensor
        def _(pe):
            mm = nc.tensor.matmul
            pe.wait_ge(s_wtok, 16)

            def embed(t):
                pe.wait_ge(s_xp[t], 16)
                for k in range(KP):
                    last = mm(psum[:, t, 0:D], xp_sb[:, t, k * P:(k + 1) * P], w_tok[:, k, :],
                              start=(k == 0), stop=(k == KP - 1))
                last.then_inc(sems["hps"], 1)

            def turn_xn(t):
                p = t % 2
                pe.wait_ge(sems["xn"], t + 2)
                if t == 0:
                    pe.wait_ge(sems["p_quad"], DC)
                    pe.wait_ge(sems["vchain"], 2 * T + 3)
                if t == 1:
                    pe.wait_ge(sems["xnT"], DC)
                if t >= 2:
                    pe.wait_ge(sems["k_ev"], 2 * (t - 1))
                for k in range(DC):
                    last = nc.tensor.transpose(psum[:, 4 + p, k * P:(k + 1) * P], xn[:, t, k * P:(k + 1) * P], ident)
                last.then_inc(sems["tz"], 1)

            def content(t):
                pe.wait_ge(sems["k_quad"], 4 * (t + 1))
                if t + 1 < T:
                    pe.wait_ge(sems["emb_a"], 2 * (t + 2))
                    pe.wait_ge(sems["emb_v"], 2 * (t + 2))
                else:
                    pe.wait_ge(sems["added"], t)
                for q in range(NQ):
                    rows = slice((q % 2) * NP, (q % 2 + 1) * NP)
                    for i in range(2):
                        last = mm(psum[i * NP:(i + 1) * NP, q, 0:QC],
                                  quT[rows, q // 2, t * P + i * NP:t * P + (i + 1) * NP],
                                  k_quad[rows, 2 * t + i, q // 2, :, :].rearrange("p h s -> p (h s)"),
                                  start=True, stop=True)
                last.then_inc(sems["ac_ps"], 1)

            def qkv(t):
                p = t % 2
                pe.wait_ge(sems["xnT"], DC * (t + 2))
                if t == 0:
                    pe.wait_ge(sems["q0_ev"], 2 * DC)
                    pe.wait_ge(sems["k0_ev"], DC)
                else:
                    pe.wait_ge(sems["q_ev"], 4 * t)
                for g in range(DC):
                    for k in range(DC):
                        last = mm(psum[:, 6, g * P:(g + 1) * P], w_q[:, k, g * P:(g + 1) * P], xnT[:, p, k, :, 0, :],
                                  start=(k == 0), stop=(k == DC - 1))
                last.then_inc(sems["qps"], 1)
                if t >= 2:
                    content(t - 2)
                for g in range(DC):
                    for k in range(DC):
                        last = mm(psum[:, 4 + p, (2 + g) * P:(3 + g) * P], w_k[:, k, g * P:(g + 1) * P],
                                  xnT[:, p, k, :, 0, :], start=(k == 0), stop=(k == DC - 1))
                last.then_inc(sems["kps"], 1)
                if t + 1 < T:
                    turn_xn(t + 1)
                if t == 0:
                    pe.wait_ge(sems["v0_ev"], 1)
                else:
                    pe.wait_ge(sems["v_ev"], t)
                for i in range(2):
                    for k in range(DC):
                        both = xnT[:, p, k, i, :, :].rearrange("p a s -> p (a s)")
                        last = mm(psum[:, 7, i * D:(i + 1) * D], both, w_v[:, k, :], start=(k == 0), stop=(k == DC - 1))
                last.then_inc(sems["vps"], 1)

            def positions(t):
                pe.wait_ge(sems["q_ev"], 4 * (t + 1))
                if t >= 2:
                    pe.wait_ge(sems["added"], t - 1)
                for q in range(NQ):
                    if t == 0:
                        pe.wait_ge(sems["hsb"], T)
                    elif q < 2:
                        pe.wait_ge(sems["emb_a"], 2 * (t - 1) + q + 1)
                    else:
                        pe.wait_ge(sems["emb_v"], 2 * (t - 1) + q - 1)
                    rows = slice((q % 2) * NP, (q % 2 + 1) * NP)
                    mm(psum[:, q, 0:QC], qvT[rows, q // 2, t * P:(t + 1) * P],
                       p_quad[rows, q // 2, :, :].rearrange("p h s -> p (h s)"), start=True, stop=True)\
                        .then_inc(sems["emb_ps"], 1)

            for t in range(T):
                embed(t)
            pe.wait_ge(s_const, 16)
            pe.wait_ge(s_wp, 16)
            pe_T = const("pe")
            for g in range(DC):
                for k in range(DC):
                    last = mm(psum[:, 4, g * S:(g + 1) * S], w_p[:, k, g * P:(g + 1) * P],
                              pe_T[:, k * S:(k + 1) * S], start=(k == 0), stop=(k == DC - 1))
            last.then_inc(sems["pos_ps"], 1)
            pe.wait_ge(sems["xn"], 1)
            for k in range(DC):
                last = nc.tensor.transpose(psum[:, 5, k * B:(k + 1) * B], xn_cls[:, k * P:(k + 1) * P],
                                           ident[0:B, 0:B])
            last.then_inc(sems["tz"], 1)
            pe.wait_ge(s_wqk, 32)
            pe.wait_ge(sems["xnT"], DC)
            for c, w in enumerate((w_q, w_k)):
                for g in range(DC):
                    for k in range(DC):
                        last = mm(psum[:, 6, (c * DC + g) * B:(c * DC + g + 1) * B], w[:, k, g * P:(g + 1) * P],
                                  xnT_cls[:, k, :], start=(k == 0), stop=(k == DC - 1))
            last.then_inc(sems["cls_qk"], 1)
            pe.wait_ge(s_wv, 16)
            for k in range(DC):
                last = mm(psum[0:H, 7, 0:D], xnT_cls[:, k, 0:1].to_broadcast([P, H]), w_v[:, k, :],
                          start=(k == 0), stop=(k == DC - 1))
            last.then_inc(sems["cls_v"], 1)

            turn_xn(0)
            def class_content():
                pe.wait_ge(sems["z_spread"], 2 * DC)
                pe.wait_ge(sems["k_ev"], 2 * T)
                pe.wait_ge(sems["q_ev"], 4 * T)
                pe.wait_ge(sems["v_ev"], T)
                for half in range(2):
                    for g in range(DC):
                        mm(psum[:, 6 + half, 0:4 * S], z_cls[:, g, :, :].rearrange("p b h -> p (b h)"),
                           kT[:, g, 4 * half:4 * half + 4, :].rearrange("p b s -> p (b s)"),
                           start=(g == 0), stop=(g == DC - 1))

            def class_positions():
                pe.wait_ge(sems["z_spread"], 3 * DC)
                for g in range(DC):
                    mm(psum[:, 7, 4 * S:4 * S + 1], z_last[:, g, :, :].rearrange("p b h -> p (b h)"), pT[:, g, S - 1:S],
                       start=(g == 0), stop=(g == DC - 1))
                for g in range(DC):
                    last = mm(psum[:, 7, 4 * S + 2:5 * S], z_next[:, g, :, :].rearrange("p b h -> p (b h)"),
                              pT[:, g, 0:S - 2], start=(g == 0), stop=(g == DC - 1))
                last.then_inc(sems["clsac_ps"], 1)

            def turn_classes():
                pe.wait_ge(sems["cls_norm"], 1)
                nc.tensor.transpose(psum[:, 7, 0:P], p_cls[:, :, :].rearrange("p a s -> p (a s)"), ident)
                pe.wait_ge(sems["e0"], 1)
                mm(psum[0:H, 7, P:P + B], const("headof"), e_cls0[:, :], start=True, stop=True)\
                    .then_inc(sems["tcls_ps"], 1)

            def turn(t):
                p = t % 2
                pe.wait_ge(sems["normed"], 2 * (t + 1))
                if t == 0:
                    pe.wait_ge(sems["k_ev"], 2 * T)
                for half in range(2):
                    if t >= 1:
                        pe.wait_ge(sems["te_ev"], 4 * t)
                    if t >= 3 and half == (t - 3) % 2:
                        pe.wait_ge(sems["tx_l"], t - 2)
                    for n in range(4):
                        pair = 4 * half + n
                        last = nc.tensor.transpose(psum[:, 4 + half, n * P:(n + 1) * P],
                                                   prob[:, p, 2 * pair:2 * pair + 2, :].rearrange("p h j -> p (h j)"), ident)
                    last.then_inc(sems["te_ps"], 1)

            def turn_0(t):
                p = t % 2
                if t == 0:
                    pe.wait_ge(sems["tcls_ev"], 3)
                else:
                    pe.wait_ge(sems["pv_ev"], 4 * t)
                nc.tensor.transpose(psum[0:H, 7, 3 * P:4 * P], prob0[:, p, :], ident).then_inc(sems["te0_ps"], 1)

            def values(t):
                pe.wait_ge(sems["te_ev"], 4 * (t + 1))
                pe.wait_ge(sems["te0_ev"], t + 1)
                for g in range(DC):
                    for i in range(2):
                        b = 2 * t + i
                        c0 = (2 * g + i) * S
                        mm(psum[:, 7, c0:c0 + S], v0_row[:, g * P:(g + 1) * P], probT_cls[:, b, :],
                           start=True, stop=False, skip_group_check=True)
                        for c in range(4):
                            pair = 4 * g + c
                            last = mm(psum[32 * c:32 * c + 32, 7, c0:c0 + S], v_pair[:, b, 32 * pair:32 * pair + 32],
                                      probT[:, b, pair, :], start=False, stop=(c == 3), skip_group_check=True)
                last.then_inc(sems["pv_ps"], 1)

            def project(t):
                if t == 0:
                    pe.wait_ge(s_wf, 16)
                elif t < T:
                    pe.wait_ge(sems["h2"], t)
                else:
                    pe.wait_ge(sems["added"], T)
                pe.wait_ge(sems["pv_ev"], 4 * t + 2 if t < T else 4 * T)
                rows, bank = (P, 6) if t < T else (B, 0)
                for k in range(DC):
                    x = outT[:, k, 2 * t:2 * t + 2, :].rearrange("p i s -> p (i s)") if t < T else outT_cls[:, k, :]
                    last = mm(psum[0:rows, bank, 0:D], x, w_f[:, k, :], start=(k == 0), stop=(k == DC - 1))
                last.then_inc(sems["wf_ps"], 1)

            def turn_x(n):
                rows = P if n < T else B
                if n >= 2:
                    pe.wait_ge(sems["tx_l"], n - 1)
                x = xn[:, n, :] if n < T else xn_cls[:, :]
                pe.wait_ge(sems["xt"], n + 1)
                pe.wait_ge(sems["te_ev"], 4 * min(n + 3, T))
                for k in range(DC):
                    last = nc.tensor.transpose(psum[:, 4 + n % 2, k * rows:(k + 1) * rows], x[:, k * P:(k + 1) * P],
                                               ident[0:rows, 0:rows])
                last.then_inc(sems["tx_ps"], 1)

            for t in range(T):
                qkv(t)
                positions(t)
            turn(0)
            class_content()
            class_positions()
            content(T - 2)
            for t in range(T):
                if t >= 1:
                    turn(t)
                else:
                    turn_classes()
                    content(T - 1)
                turn_0(t)
                if t >= 1:
                    project(t - 1)
                if t >= 2:
                    turn_x(t - 2)
                values(t)
            project(T - 1)
            project(T)
            turn_x(T - 2)
            turn_x(T - 1)
            turn_x(T)

            pe.wait_ge(sems["tx_l"], T + 1)
            pe.wait_ge(sems["gw_split"], 2)
            pe.wait_ge(sems["pv_ev"], 4 * T)
            for k in range(DC):
                for w, x in ((w_gate_h, xT_h), (w_gate_h, xT_l), (w_gate_l, xT_h)):
                    for half in range(2):
                        last = mm(psum[0:E, 6 + half, 0:HALF], w[:, k, :], x[:, k, half * HALF:(half + 1) * HALF],
                                  start=(k == 0 and w is w_gate_h and x is xT_h), stop=(k == DC - 1 and w is w_gate_l))
            last.then_inc(sems["gateT_ps"], 1)

            def hidden(e, p, m):
                if m == 0:
                    pe.wait_ge(sems["w1h"], e + 1)
                    pe.wait_ge(sems["w1l"], e + 1)
                if isinstance(e, int) and e == 0 and m < 2:
                    if m == 0:
                        pe.wait_ge(sems["added"], T)
                else:
                    pe.wait_ge(sems["gelu"], 2 * (FC * e + m - 1))
                for k in range(DC):
                    cols = slice(k * F + m * P, k * F + (m + 1) * P)
                    for w, x in ((w1_h, xT_h), (w1_h, xT_l), (w1_l, xT_h)):
                        for half in range(2):
                            last = mm(psum[:, 2 * (m % 2) + half, 0:HALF], w[:, p, cols],
                                      x[:, k, half * HALF:(half + 1) * HALF],
                                      start=(k == 0 and w is w1_h and x is xT_h), stop=(k == DC - 1 and w is w1_l))
                last.then_inc(sems["hid_ps"], 1)

            def output(e, p, t):
                if t == 0:
                    pe.wait_ge(sems["hsplit"], 2 * FC * (e + 1))
                    pe.wait_ge(sems["w2h"], e + 1)
                    pe.wait_ge(sems["w2l"], e + 1)
                if isinstance(e, int) and e == 0 and t < 2:
                    if t == 0:
                        pe.wait_ge(sems["te_ev"], 4 * T)
                else:
                    pe.wait_ge(sems["r"], T * e + t - 1)
                for m in range(FC):
                    cols = slice(m * D, (m + 1) * D)
                    for c0, w in ((NT + B, w2_h), (NT + B, w2_l), (0, w2_h)):
                        last = mm(psum[:, 4 + t % 2, 0:D], hid_lh[:, p, m, c0 + t * P:c0 + (t + 1) * P], w[:, p, cols],
                                  start=(m == 0 and c0 > 0 and w is w2_h), stop=(m == FC - 1 and c0 == 0))
                last.then_inc(sems["o_ps"], 1)

            def output_cls(e, p):
                if isinstance(e, int) and e == 0:
                    pe.wait_ge(sems["acc0"], T)
                else:
                    pe.wait_ge(sems["cls_row"], e)
                if isinstance(e, int) and e == E - 1:
                    pe.wait_ge(sems["hsplit"], 2 * FC * (e + 1))
                    pe.wait_ge(sems["w2h"], e + 1)
                    pe.wait_ge(sems["w2l"], e + 1)
                for m in range(FC):
                    cols = slice(m * D, (m + 1) * D)
                    mm(psum[0:2 * B, 6, 0:D], hid_lh[:, p, m, T * P:NT + B], w2_h[:, p, cols],
                       start=(m == 0), stop=(m == FC - 1), skip_group_check=True)
                    last = mm(psum[0:B, 6, 0:D], hid_lh[:, p, m, NT:NT + B], w2_l[:, p, cols],
                              start=False, stop=(m == FC - 1), skip_group_check=True)
                last.then_inc(sems["o_ps"], 1)

            pe.wait_ge(sems["gateT"], 3)
            for n in range(T):
                nc.tensor.transpose(psum[:, 7, n * E:(n + 1) * E], gateT[:, n * P:(n + 1) * P], ident[0:E, 0:E])
            nc.tensor.transpose(psum[0:B, 7, T * E:(T + 1) * E], gateT_cls[:, :], ident[0:E, 0:E])\
                .then_inc(sems["gate_ps"], 1)
            for m in range(FC):
                hidden(0, 0, m)
            pe.wait_ge(sems["wE"], 1)
            for t in range(T):
                last = nc.tensor.transpose(psum[0:E, 7, t * P:(t + 1) * P], wE[:, t, :], ident)
            last.then_inc(sems["wET_ps"], 1)

            def norm_bias(t):
                if t == 0:
                    pe.wait_ge(sems["wET"], 1)
                    pe.wait_ge(s_lnb, 16)
                if t >= 2:
                    pe.wait_ge(sems["acc0"], t - 1)
                mm(psum[:, 6 + t % 2, 0:D], wET[:, t, :], lnb_rows[:, :], start=True, stop=True)\
                    .then_inc(sems["lnb_ps"], 1)

            def cls_rows_of():
                pe.wait_ge(sems["acc0"], T)
                mm(psum[0:E * B, 7, D:D + E], const("spread", B), wE[0:B, T, :], start=True, stop=True)
                mm(psum[0:E * B, 7, 0:D], const("spread", B), xn_cls[:, :], start=True, stop=True)\
                    .then_inc(sems["wcol_ps"], 1)

            def slot(e, p, k):
                for m in range(FC):
                    hidden(e + 1, 1 - p, m)
                    if isinstance(e, int) and e == 0 and m < 2:
                        norm_bias(2 * m)
                        norm_bias(2 * m + 1)
                    output(e, p, m)
                    if isinstance(e, int) and e == 0 and m == 2:
                        cls_rows_of()
                output_cls(e, p)

            slot(0, 0, 0)
            with pe.Fori(0, 2) as i:
                slot(2 * i + 1, 1, i)
                slot(2 * i + 2, 0, i + 1)
            for e in range(5, E - 1):
                slot(e, e % 2, e // 2)
            output_cls(E - 1, (E - 1) % 2)
            for t in range(T):
                output(E - 1, (E - 1) % 2, t)
            pe.wait_ge(sems["y_cls"], 1)
            pe.wait_ge(sems["wsel"], 2)
            mm(psum[0:B, 7, 0:D], wsel[:, :], r_cls[:, :], start=True, stop=True).then_inc(sems["clsout_ps"], 1)


def kernel(x, cls_tok, L0_tok_W, L0_attn_Wq, L0_attn_bq, L0_attn_Wk, L0_attn_bk, L0_attn_Wv, L0_attn_bv,
           L0_attn_Wpos, L0_attn_Wf, L0_attn_bf, L0_attn_u, L0_attn_v, L0_attn_gamma, L0_attn_beta,
           L0_ffn_gate_w, L0_ffn_w1, L0_ffn_b1, L0_ffn_w2, L0_ffn_b2, L0_ffn_ln_g, L0_ffn_ln_b):
    import numpy as np
    import concourse.bacc as bacc
    from concourse.bass_utils import run_bass_kernel_spmd

    at, table = constants()
    patches = np.asarray(x).reshape(B, 3, 8, 16, 8, 16).transpose(0, 1, 3, 5, 2, 4).reshape(T, P, KP, P)
    patches = np.ascontiguousarray(patches.transpose(0, 3, 2, 1)).reshape(T, P, KP * P)
    vectors = [L0_attn_bq, L0_attn_bk, L0_attn_bv, L0_attn_u, L0_attn_v, L0_attn_gamma, L0_attn_beta]
    params = np.concatenate([np.asarray(a).reshape(DC, P).T for a in vectors], 1)
    b1t = np.asarray(L0_ffn_b1).reshape(E, FC, P).transpose(2, 0, 1)
    arrays = {
        "consts": table, "params": params, "patches": patches, "cls_tok": cls_tok, "tok_w": L0_tok_W,
        "wq": L0_attn_Wq, "wk": L0_attn_Wk, "wv": L0_attn_Wv, "wpos": L0_attn_Wpos, "wf": L0_attn_Wf,
        "bf": L0_attn_bf, "gate_w": L0_ffn_gate_w, "w1": L0_ffn_w1, "b1t": b1t, "w2": L0_ffn_w2,
        "b2": L0_ffn_b2, "ln_g": L0_ffn_ln_g, "ln_b": L0_ffn_ln_b,
    }
    arrays = {f"in_{k}": np.ascontiguousarray(a) for k, a in arrays.items()}
    nc = bacc.Bacc("TRN2", target_bir_lowering=False, num_devices=1, dynamic_dma_scratch_size=1024)
    args = [nc.dram_tensor(k, a.shape, mybir.dt.from_np(a.dtype), kind="ExternalInput").ap()
            for k, a in arrays.items()]
    out = nc.dram_tensor("out", (B, S, D), F32, kind="ExternalOutput").ap()
    build(nc, *args, out, at)
    r = run_bass_kernel_spmd(nc, [arrays], core_ids=[0])
    return r.results[0]["out"]
```

```python
from contextlib import ExitStack

import concourse.bass as bass
from concourse import mybir

F32 = mybir.dt.float32
F32R = mybir.dt.float32r
U32 = mybir.dt.uint32
ALU = mybir.AluOpType
ACT = mybir.ActivationFunctionType
AX = mybir.AxisListType.X

P = 128
B = 8
NP = 64
S = NP + 1
D = 256
DC = D // P
H = 16
HD = D // H
SHARE = 8
QH = 4
NQ = H // QH
T = B * NP // P
FP = 3 * 16 * 16
KP = FP // P
E = 8
F = 2 * D
FC = F // P
HALF = B + T // 2 * P
NT = 2 * HALF
EPS = 1e-5
EPS_FFN = 1e-6
QC = QH * S


def column(n):
    return 0 if n == T else B + (n - 2) * P if n >= 2 else HALF + B + n * P


def constants():
    import numpy as np

    at, parts, n = {}, [], 0

    def put(name, a):
        nonlocal n
        a = np.asarray(a, np.float32)
        full = np.zeros((P, a.shape[1]), np.float32)
        full[:a.shape[0]] = a
        at[name] = (n, n + a.shape[1])
        n += a.shape[1]
        parts.append(full)

    p = np.arange(P)
    pos = np.arange(S, dtype=np.float32)
    inv = (1.0 / 10000.0 ** (np.arange(0.0, D, 2.0, dtype=np.float32) / np.float32(D))).astype(np.float32)
    ang = pos[:, None] * inv[None, :]
    pe = np.zeros((S, D), np.float32)
    pe[:, 0::2], pe[:, 1::2] = np.sin(ang), np.cos(ang)
    put("pe", pe.T.reshape(DC, P, S).transpose(1, 0, 2).reshape(P, DC * S))
    put("ident", np.eye(P))
    put("quad", (p[:, None] // HD) % QH == np.arange(QH)[None])
    put("head", np.concatenate([p[:, None] // HD + 8 * g == np.arange(H)[None] for g in range(DC)], 1))
    put("parity", p[:, None] // NP == (np.arange(D)[None] // HD) % 2)
    put("image", p[:, None] // H == np.arange(B)[None])
    put("headof", p[:, None] % H == np.arange(H)[None])
    put("headrow", np.arange(H)[:, None] == np.arange(D)[None] // HD)
    put("iota", np.broadcast_to(np.arange(E), (P, E)))
    put("e", np.full((P, T + 1), np.e))
    put("zero", np.zeros((P, DC * B)))
    put("power", np.full((P, 8), -0.5))
    put("eps", np.full((P, T), D * EPS_FFN))
    put("spread", np.arange(B)[:, None] == np.arange(E * B)[None] % B)
    put("expert", np.arange(E * B)[:, None] // B == np.arange(E)[None])
    put("imageof", np.arange(E * B)[:, None] % B == np.arange(B)[None])
    return at, np.concatenate(parts, 1)


PARAMS = ["bq", "bk", "bv", "u", "v", "gamma", "beta"]


def build(nc, consts, params, xp, cls_tok, tok_w, wq, wk, wv, wpos, wf, bf, gate_w, w1, b1t, w2, b2,
          ln_g, ln_b, out, at):
    with ExitStack() as ctx:
        def sb(name, shape, dt=F32):
            return ctx.enter_context(nc.sbuf_tensor(name, shape, dt))

        def sem(name):
            return ctx.enter_context(nc.semaphore(name))

        C = sb("C", [P, consts.shape[1]])

        def const(name, rows=P):
            return C[0:rows, at[name][0]:at[name][1]]

        ident = const("ident")
        PAR = sb("PAR", [P, len(PARAMS) * DC])

        def par(name, g):
            k = PARAMS.index(name) * DC + g
            return PAR[:, k:k + 1]

        bqu = sb("bqu", [P, DC])
        bqv = sb("bqv", [P, DC])
        early = sb("early", [P, KP * (T * P + D)])
        xp_sb = early[:, 0:KP * T * P].rearrange("p (t n) -> p t n", t=T)
        w_tok = early[:, KP * T * P:].rearrange("p (k n) -> p k n", k=KP)
        w_q, w_k, w_v, w_p, w_f = (sb(f"w_{x}", [P, DC, D]) for x in "qkvpf")
        w_gate = sb("w_gate", [P, DC, E])
        w_gate_h = sb("w_gate_h", [P, DC, E], F32R)
        w_gate_l = sb("w_gate_l", [P, DC, E], F32R)
        bf_rows = sb("bf_rows", [P, D])
        lnb_rows = sb("lnb_rows", [E, D])
        b2_cls = sb("b2_cls", [E * B, D])
        g_cls = sb("g_cls", [E * B, D])
        lnb_cls = sb("lnb_cls", [E * B, D])
        b1_cols = sb("b1_cols", [P, E, FC])

        h_tok = sb("h_tok", [P, T, D])
        h_cls = sb("h_cls", [B, D])
        xn = sb("xn", [P, T, D])
        xn_cls = sb("xn_cls", [B, D])
        stats = sb("stats", [P, T + 1, 6])
        mv = sb("mv", [P, T + 1, 2])
        var = sb("var", [P, T + 1])
        rstd = sb("rstd", [P, T + 1])
        xnT = sb("xnT", [P, 2, DC, 2, 2, NP])
        xnT_cls = sb("xnT_cls", [P, DC, B])
        quT = sb("quT", [P, DC, T * P])
        qvT = sb("qvT", [P, DC, T * P])
        q0u = sb("q0u", [P, DC, B])
        q0v = sb("q0v", [P, DC, B])
        kT = sb("kT", [P, DC, B, S])
        pT = sb("pT", [P, DC, S])
        p_quad = sb("p_quad", [P, DC, QH, S])
        z_cls = sb("z_cls", [P, DC, B, H])
        z_last = sb("z_last", [P, DC, B, H])
        z_next = sb("z_next", [P, DC, B, H])
        v_pair = sb("v_pair", [P, B, D])
        v0_row = sb("v0_row", [H, D])
        prob0 = sb("prob0", [P, 2, H])
        probT_cls = sb("probT_cls", [H, B, S])
        e_cls = sb("e_cls", [P, S])
        p_cls = sb("p_cls", [P, 2, NP])
        e_cls0 = sb("e_cls0", [P, B])
        outT = sb("outT", [P, DC, B, NP])
        outT_cls = sb("outT_cls", [P, DC, B])
        small = sb("small", [P, 8])
        mx = sb("mx", [P, 2, H])
        rs = sb("rs", [P, 2, H])
        ri = sb("ri", [P, 2, H])

        xT_h = sb("xT_h", [P, DC, NT], F32R)
        xT_l = sb("xT_l", [P, DC, NT], F32R)
        w1_raw = sb("w1_raw", [P, 2, DC * F])
        w2_raw = sb("w2_raw", [P, 2, FC * D])
        w1_h = sb("w1_h", [P, 2, DC * F], F32R)
        w1_l = sb("w1_l", [P, 2, DC * F], F32R)
        w2_h = sb("w2_h", [P, 2, FC * D], F32R)
        w2_l = sb("w2_l", [P, 2, FC * D], F32R)
        gate = sb("gate", [P, T + 1, E])
        gateT = w_q[0:E, :, :].rearrange("e k n -> e (k n)")
        gateT_cls = sb("gateT_cls", [E, B])
        top = sb("top", [P, T + 1, 8])
        top_at = sb("top_at", [P, T + 1, 8], U32)
        top_atf = sb("top_atf", [P, T + 1, 2])
        tw = sb("tw", [P, T + 1, 4])
        pick = sb("pick", [P, 2, T + 1, E])
        wE = sb("wE", [P, T + 1, E])
        wE_d = sb("wE_d", [P, T + 1, E])
        wET = gateT.rearrange("e (t n) -> e t n", t=T)
        wcol_x = sb("wcol_x", [E * B, E])
        wcol = sb("wcol", [E * B, 1])
        wsel = sb("wsel", [E * B, B])
        half_early = 2 * T * D
        cls_all = early[:, 0:B * S]
        xb = early[:, 0:half_early].rearrange("p (a t n) -> p a t n", a=2, t=T)
        res = early[:, half_early:2 * half_early].rearrange("p (a t n) -> p a t n", a=2, t=T)
        res_sum = sb("res_sum", [P, 2, T])
        neg_mean = sb("neg_mean", [P, 2, T])
        sq_junk = (w_p[:, 0, :], w_v[:, 1, :])
        sq_sum = sb("sq_sum", [P, 2, T])
        e_var = sb("e_var", [P, 2, T])
        e_rstd = sb("e_rstd", [P, 2, T])
        e_scale = sb("e_scale", [P, 2, T])
        scaled = w_p[:, 1, :]
        last_y = (qvT[:, :, :].rearrange("p k (a d) -> p (k a) d", a=2), w_f)
        last_bias = sb("last_bias", [P, 2, T])
        cls_rows = v_pair[0:2 * B, :, :]
        o_cls = quT[0:E * B, 0, :].rearrange("p (a d) -> p a d", a=2)
        x_cls = w_k[0:E * B, 1, :]
        r_cls = w_k[0:E * B, 0, :]
        cls_small = sb("cls_small", [E * B, 8])
        acc_cls = sb("acc_cls", [B, D])
        ones = sb("ones", [P, P])

        kq_n, pt_n, em_n, sc_n = B * DC * QC, B * (H // 2) * S, (S + 1) * H, H * S
        with nc.sbuf_tensor("arena", [P, kq_n + pt_n + 2 * (em_n + 2 * sc_n + H * NP)], F32) as arena:
            o = 0
            k_quad = arena[:, o:o + kq_n].rearrange("p (b g q s) -> p b g q s", b=B, g=DC, q=QH)
            o += kq_n
            probT = arena[:, o:o + pt_n].rearrange("p (b h s) -> p b h s", b=B, s=S)
            o += pt_n
            emb = arena[:, o:o + 2 * em_n].rearrange("p (n m h) -> p n m h", n=2, h=H)
            o += 2 * em_n
            shifted = arena[:, o:o + 2 * sc_n].rearrange("p (n j h) -> p n j h", n=2, h=H)
            o += 2 * sc_n
            score = arena[:, o:o + 2 * sc_n].rearrange("p (n h j) -> p n h j", n=2, h=H)
            o += 2 * sc_n
            prob = arena[:, o:o + 2 * H * NP].rearrange("p (n h j) -> p n h j", n=2, h=H)
        hid = sb("hid", [P, FC, NT])
        HIGH = T * P + B
        hid_lh = sb("hid_lh", [P, 2, FC, HIGH + NT], F32R)
        g_rows = sb("g_rows", [P, E, D])
        acc = sb("acc", [P, T, D])
        b2_rows = sb("b2_rows", [P, E, D])

        key0_bank = (7, 6, 0, 0)
        value_bank = (7, 6, 7, 6)
        project_bank = (3, 1, 2, 3, 0)
        psum = ctx.enter_context(nc.psum_tensor("psum", [P, 8, 512], F32))

        scratch = nc.dram_tensor("shift_scratch", [T * P * (S + 1) * H], F32, kind="Internal")

        s_const, s_par, s_cls = sem("s_const"), sem("s_par"), sem("s_cls")
        s_wtok = [sem(f"s_wtok{i}") for i in range(2)]
        s_xp = [sem(f"s_xp{t}") for t in range(T)]
        s_wqk, s_wv, s_wp, s_wf, s_bf = (sem(f"s_{x}") for x in ("wqk", "wv", "wp", "wf", "bf"))
        s_gw, s_b1, s_b2, s_g, s_lnb, s_clsrows = (sem(f"s_{x}") for x in ("gw", "b1", "b2", "g", "lnb", "clsrows"))
        s_w1raw = [sem(f"s_w1raw{i}") for i in range(2)]
        s_w2raw = [sem(f"s_w2raw{i}") for i in range(2)]
        s_shift_in = [sem(f"s_shift_in{i}") for i in range(2)]

        names = """
            ones zeros bias2 hps hsb hbf var1 rstd1 xn tz xnT pos_ps p_sb p_quad qps q_ev vps v_ev kps k_ev
            k_quad z_cls cls_qk cls_v q0_ev k0_ev v0_ev z_spread emb_ps emb_a emb_v emb_out
            ac_ps added maxed subbed exped summed recip normed normed_d clsac_ps cls_max cls_exp cls_norm
            tables pad cls_bd cls_sub e0 tcls_ps tcls_ev te_ps te_ev te0_ps te0_ev pv_ps pv_ev wf_ps h2 h2cls wfcls_ps
            var2 rstd2 xt tx_ps tx_h tx_l gw_split gate_ps gate_sb tops diff dexp wE wET_ps wET wcol_ps
            wsel lnb_ps acc0
            w1h w1l w2h w2l hid_ps gelu hsplit o_ps r negm sq escale xb scaled p2
            gateT_ps gateT cls_row o_cls x_cls last_bias last_y last_g last_acc
            cls_var cls_rs y_cls clsout_ps clsout out vchain gchain
        """.split()
        sems = {n: sem("s_" + n) for n in names}

        block = ctx.enter_context(nc.Block())

        @block.sync
        def _(sp):
            sp.dma_start(xp_sb[:, 0, :], xp[0]).then_inc(s_xp[0], 16)
            for k in (0, KP // 2):
                sp.dma_start(w_tok[:, k:k + KP // 2, :],
                             tok_w[k * P:(k + KP // 2) * P, :].rearrange("(k p) n -> p k n", p=P))\
                    .then_inc(s_wtok[k // (KP // 2)], 16)
            for t in range(1, T):
                sp.dma_start(xp_sb[:, t, :], xp[t]).then_inc(s_xp[t], 16)
            sp.dma_start(w_v[:, :, :], wv.rearrange("(k p) n -> p k n", p=P)).then_inc(s_wv, 16)
            sp.dma_start(bf_rows[:, :], bf.rearrange("(o d) -> o d", o=1).broadcast_to([P, D])).then_inc(s_bf, 16)
            for e in range(2):
                sp.dma_start(w1_raw[:, e, :].rearrange("p (k n) -> p k n", k=DC),
                             w1[e].rearrange("(k p) n -> p k n", p=P)).then_inc(s_w1raw[e], 16)
                sp.dma_start(w2_raw[:, e, :].rearrange("p (k n) -> p k n", k=FC),
                             w2[e].rearrange("(k p) n -> p k n", p=P)).then_inc(s_w2raw[e], 16)
            sp.dma_start(w_f[:, :, :], wf.rearrange("(k p) n -> p k n", p=P)).then_inc(s_wf, 16)
            sp.dma_start(w_gate[:, :, :], gate_w.rearrange("(k p) n -> p k n", p=P)).then_inc(s_gw, 16)
            sp.dma_start(b1_cols[:, :, :], b1t).then_inc(s_b1, 16)
            sp.dma_start(lnb_rows[:, :], ln_b).then_inc(s_lnb, 16)
            for dst, src in ((b2_cls, b2), (g_cls, ln_g), (lnb_cls, ln_b)):
                sp.dma_start(dst[:, :], src.rearrange("e (o d) -> e o d", o=1).broadcast_to([E, B, D]))\
                    .then_inc(s_clsrows, 16)
            for t in range(T):
                sp.wait_ge(sems["emb_a"], 2 * (t + 1))
                sp.wait_ge(sems["emb_v"], 2 * (t + 1))
                sp.dma_start(bass.AP(scratch, t * P * em_n, [[em_n, P], [1, em_n]]),
                             emb[:, t % 2, :, :].rearrange("p m h -> p (m h)")).then_inc(sems["emb_out"], 16)
                sp.wait_ge(sems["emb_out"], 16 * (t + 1))
                if t >= 2:
                    sp.wait_ge(sems["added"], t - 1)
                src = bass.AP(scratch, t * P * em_n + (S - 1) * H, [[NP * em_n, 2], [S * H, NP], [1, S * H]])
                sp.dma_start(shifted[:, t % 2, :, :].rearrange("p j h -> p (j h)"), src).then_inc(s_shift_in[t % 2], 16)
            sp.wait_ge(sems["wf_ps"], T + 1)
            sp.dma_start(b2_rows[:, :, :], b2.rearrange("(o e) d -> o e d", o=1).broadcast_to([P, E, D]))\
                .then_inc(s_b2, 16)
            sp.dma_start(g_rows[:, :, :], ln_g.rearrange("(o e) d -> o e d", o=1).broadcast_to([P, E, D]))\
                .then_inc(s_g, 16)

            def load_w1(e, p, n):
                sp.wait_ge(sems["w1h"], e - 1)
                sp.wait_ge(sems["w1l"], e - 1)
                sp.dma_start(w1_raw[:, p, :].rearrange("p (k n) -> p k n", k=DC),
                             w1[bass.ds(e, 1)].rearrange("o (k p) n -> p (o k) n", p=P)).then_inc(s_w1raw[p], 16)

            def load_w2(e, p, n):
                sp.wait_ge(sems["w2h"], e - 1)
                sp.wait_ge(sems["w2l"], e - 1)
                sp.dma_start(w2_raw[:, p, :].rearrange("p (k n) -> p k n", k=FC),
                             w2[bass.ds(e, 1)].rearrange("o (k p) n -> p (o k) n", p=P)).then_inc(s_w2raw[p], 16)

            with sp.Fori(0, (E - 2) // 2) as i:
                for p in range(2):
                    load_w1(2 * i + 2 + p, p, i)
                    load_w2(2 * i + 2 + p, p, i)
            for e in range(E):
                sp.wait_ge(sems["cls_row"], e + 1)
                for part in range(2):
                    sp.dma_start(o_cls[e * B:(e + 1) * B, part, :], cls_rows[part * B:(part + 1) * B, e, :])\
                        .then_inc(sems["o_cls"], 16)
            for t in range(2):
                sp.wait_ge(sems["p2"], T * (E - 2) + 2 + t + 1)
                sp.dma_start(out[2 * t:2 * t + 2, 1:S, :], acc[:, t, :]).then_inc(sems["out"], 16)
            sp.wait_ge(sems["clsout"], 1)
            sp.dma_start(out[:, 0, :], acc_cls[:, :]).then_inc(sems["out"], 16)
            sp.wait_ge(sems["out"], 16 * (T + 1))

        def keys(pool, t, quad):
            pool.wait_ge(sems["k_ev"], 2 * (t + 1))
            if t == 0:
                pool.wait_ge(sems["k0_ev"], DC)
            for b in (2 * t, 2 * t + 1):
                for g in range(DC):
                    nc.gpsimd.tensor_tensor(k_quad[:, b, g, :, :],
                                            kT[:, g, b, :].unsqueeze(1).to_broadcast([P, QH, S]),
                                            quad.to_broadcast([P, QH, S]), ALU.mult)\
                        .then_inc(sems["k_quad"], 1)

        def split_w1(eng, e, p, landed):
            eng.wait_ge(s_w1raw[p], landed)
            eng.wait_ge(sems["w1h"], e + 1)
            nc.gpsimd.tensor_tensor(w1_l[:, p, :], w1_raw[:, p, :], w1_h[:, p, :].bitcast(F32), ALU.subtract)\
                .then_inc(sems["w1l"], 1)

        def split_w2(eng, e, p, landed):
            eng.wait_ge(s_w2raw[p], landed)
            eng.wait_ge(sems["w2h"], e + 1)
            nc.gpsimd.tensor_tensor(w2_l[:, p, :], w2_raw[:, p, :], w2_h[:, p, :].bitcast(F32), ALU.subtract)\
                .then_inc(sems["w2l"], 1)


        def w1_high(act, e, p, landed):
            act.wait_ge(s_w1raw[p], landed)
            if not isinstance(e, int) or e >= 2:
                act.wait_ge(sems["hid_ps"], FC * (e - 1))
                act.wait_ge(sems["w1l"], e - 1)
            nc.scalar.activation(w1_h[:, p, :], w1_raw[:, p, :], ACT.Copy).then_inc(sems["w1h"], 1)

        def w2_high(act, e, p, landed):
            act.wait_ge(s_w2raw[p], landed)
            if not isinstance(e, int) or e >= 2:
                act.wait_ge(sems["o_ps"], (T + 1) * (e - 1))
                act.wait_ge(sems["w2l"], e - 1)
            nc.scalar.activation(w2_h[:, p, :], w2_raw[:, p, :], ACT.Copy).then_inc(sems["w2h"], 1)

        def tx_high(act, n):
            rows = P if n < T else B
            c0 = column(n)
            act.wait_ge(sems["tx_ps"], n + 1)
            nc.scalar.activation(xT_h[:, :, c0:c0 + rows],
                                 psum[:, 4 + n % 2, 0:DC * rows].rearrange("p (k n) -> p k n", k=DC), ACT.Copy)\
                .then_inc(sems["tx_h"], 1)

        @block.gpsimd
        def _(pool):
            chain = [0]

            def link(ins):
                chain[0] += 1
                ins.then_inc(sems["gchain"], 1)
                pool.wait_ge(sems["gchain"], chain[0])

            nc.gpsimd.memset(emb[:, :, 0, :], 0.0).then_inc(sems["zeros"], 1)
            nc.gpsimd.memset(gate[:, T, :], 0.0).then_inc(sems["zeros"], 1)
            pool.wait_ge(s_const, 16)

            def rsqrt(col, rows, n, signal, src, dst):
                nc.gpsimd.tensor_tensor(dst, src, C[0:rows, at["power"][0]:at["power"][0] + n], ALU.pow)\
                    .then_inc(sems[signal], 1)

            def normalise(t):
                pool.wait_ge(sems["recip"], t + 1)
                if t >= 2:
                    pool.wait_ge(sems["te_ps"], 2 * (t - 1))
                    pool.wait_ge(sems["te0_ps"], t - 1)
                heads = slice(0, H if t < T - 1 else SHARE)
                nc.gpsimd.tensor_tensor(prob[:, t % 2, heads, :], score[:, t % 2, heads, 1:S],
                                        ri[:, t % 2, heads].unsqueeze(2)
                                        .to_broadcast([P, heads.stop, NP]), ALU.mult)\
                    .then_inc(sems["normed"], 1)
                nc.gpsimd.tensor_tensor(prob0[:, t % 2, :], score[:, t % 2, :, 0], ri[:, t % 2, :], ALU.mult)\
                    .then_inc(sems["normed"], 1)

            pool.wait_ge(sems["var1"], 1)
            rsqrt(T, B, 1, "rstd1", var[0:B, T:T + 1], rstd[0:B, T:T + 1])
            quad = const("quad").unsqueeze(2)
            for t in range(T):
                pool.wait_ge(sems["var1"], t + 2)
                rsqrt(t, P, 1, "rstd1", var[:, t:t + 1], rstd[:, t:t + 1])
            for t in range(T):
                keys(pool, t, quad)
                if t >= 2:
                    normalise(t - 2)
            pool.wait_ge(sems["xn"], T + 1)
            pool.wait_ge(sems["hsb"], T)
            pool.wait_ge(s_bf, 16)
            nc.gpsimd.tensor_tensor(h_tok[:, :, :], h_tok[:, :, :],
                                    bf_rows[:, :].unsqueeze(1).to_broadcast([P, T, D]), ALU.add)\
                .then_inc(sems["hbf"], 1)
            nc.gpsimd.tensor_tensor(h_cls[:, :], h_cls[:, :], bf_rows[0:B, :], ALU.add).then_inc(sems["hbf"], 1)
            def rstd2(n):
                pool.wait_ge(sems["var2"], n + 1)
                rsqrt(n, P, 1, "rstd2", var[:, n:n + 1], rstd[:, n:n + 1])

            split_w1(pool, 0, 0, 16)
            split_w1(pool, 1, 1, 16)
            normalise(2)
            split_w2(pool, 0, 0, 16)
            normalise(3)
            rstd2(0)
            rstd2(1)
            rstd2(T - 2)
            rstd2(T - 1)
            pool.wait_ge(sems["var2"], T + 1)
            rsqrt(T, B, 1, "rstd2", var[0:B, T:T + 1], rstd[0:B, T:T + 1])

            def plus_b2(e, p):
                if not isinstance(e, int) or e >= 2:
                    pool.wait_ge(sems["r"], T * (e - 1))
                nc.gpsimd.tensor_tensor(xb[:, p, :, :], xn[:, :, :],
                                        b2_rows[:, bass.ds(e, 1), :].to_broadcast([P, T, D]), ALU.add)\
                    .then_inc(sems["xb"], 1)

            def scale_of(e, p, t0=0, n=T, done=0):
                pool.wait_ge(sems["sq"], T * e + t0 + n)
                ts = slice(t0, t0 + n)
                nc.gpsimd.tensor_tensor(e_var[:, p, ts], sq_sum[:, p, ts], const("eps")[:, ts], ALU.add)\
                    .then_inc(sems["escale"], 1)
                pool.wait_ge(sems["escale"], 3 * e + done + 1)
                nc.gpsimd.tensor_tensor(e_rstd[:, p, ts], e_var[:, p, ts],
                                        C[:, at["power"][0]:at["power"][0] + n], ALU.pow)\
                    .then_inc(sems["escale"], 1)
                pool.wait_ge(sems["escale"], 3 * e + done + 2)
                nc.gpsimd.tensor_tensor(e_scale[:, p, ts], e_rstd[:, p, ts], wE_of(e)[:, ts], ALU.mult)\
                    .then_inc(sems["escale"], 1)

            def wE_of(e):
                return wE_d[:, 0:T, bass.ds(e, 1)].rearrange("p t o -> p (t o)")

            pool.wait_ge(s_b2, 16)
            pool.wait_ge(sems["xt"], T + 1)
            pool.wait_ge(sems["diff"], 1)
            nc.gpsimd.tensor_tensor(tw[:, :, 1], const("e"), tw[:, :, 0], ALU.pow).then_inc(sems["dexp"], 1)
            plus_b2(0, 0)
            pool.wait_ge(sems["wE"], 2)

            def slot(e, p, k):
                if not isinstance(e, int) or e + 1 < E:
                    split_w2(pool, e + 1, 1 - p, 16 * (k + 1 + p))
                if not isinstance(e, int) or e + 2 < E:
                    split_w1(pool, e + 2, p, 16 * (k + 2))
                if not isinstance(e, int) or e + 1 < E:
                    plus_b2(e + 1, 1 - p)
                scale_of(e, p)

            slot(0, 0, 0)
            with pool.Fori(0, 2) as i:
                slot(2 * i + 1, 1, i)
                slot(2 * i + 2, 0, i + 1)
            for e in range(5, E - 1):
                slot(e, e % 2, e // 2)
            def bias_of(e, i, t0):
                p = e % 2
                pool.wait_ge(sems["negm"], T * (e + 1))
                pool.wait_ge(sems["escale"], 3 * (e + 1) + 3 * i)
                nc.gpsimd.tensor_tensor(last_bias[:, i, t0:T], neg_mean[:, p, t0:T], e_scale[:, p, t0:T], ALU.mult)\
                    .then_inc(sems["last_bias"], 1)

            def add_tile(e, t, y, n):
                pool.wait_ge(sems["last_y"], n + 1)
                nc.gpsimd.tensor_tensor(y, y, g_rows[:, e, :], ALU.mult).then_inc(sems["last_g"], 1)
                pool.wait_ge(sems["last_g"], n + 1)
                if e == E - 2:
                    pool.wait_ge(sems["p2"], T * (E - 3) + t + 1)
                else:
                    pool.wait_ge(sems["last_acc"], 2)
                nc.gpsimd.tensor_tensor(acc[:, t, :], acc[:, t, :], y, ALU.add).then_inc(sems["last_acc"], 1)

            bias_of(E - 2, 0, 2)
            for t in range(2, T):
                add_tile(E - 2, t, last_y[0][:, t, :], t - 2)
            e, p = E - 1, (E - 1) % 2
            scale_of(e, p, 0, 2)
            scale_of(e, p, 2, 2, 3)
            bias_of(e, 1, T - 1)
            pool.wait_ge(sems["cls_var"], 1)
            nc.gpsimd.tensor_tensor(cls_small[:, 4:5], cls_small[:, 3:4],
                                    C[0:E * B, at["power"][0]:at["power"][0] + 1], ALU.pow)\
                .then_inc(sems["cls_rs"], 1)
            add_tile(e, T - 1, last_y[1][:, 0, :], 2)

        @block.scalar
        def _(act):
            act.dma_start(PAR[:, :], params).then_inc(s_par, 16)
            act.dma_start(h_cls[:, :], cls_tok.rearrange("a b d -> (a b) d").broadcast_to([B, D])).then_inc(s_cls, 16)
            act.dma_start(C[:, :], consts).then_inc(s_const, 16)
            act.dma_start(w_p[:, :, :], wpos.rearrange("(k p) n -> p k n", p=P)).then_inc(s_wp, 16)
            act.dma_start(w_q[:, :, :], wq.rearrange("(k p) n -> p k n", p=P)).then_inc(s_wqk, 16)
            act.dma_start(w_k[:, :, :], wk.rearrange("(k p) n -> p k n", p=P)).then_inc(s_wqk, 16)
            act.wait_ge(s_par, 16)
            def norm_turned(n):
                act.wait_ge(sems["tz"], n + 2)
                if n >= 2:
                    act.wait_ge(sems["vps"], n - 1)
                for k in range(DC):
                    nc.scalar.activation(xnT[:, n % 2, k, :, :, :],
                                         psum[:, 4 + n % 2, k * P:(k + 1) * P]
                                         .rearrange("p (i s) -> p i s", i=2).unsqueeze(2)
                                         .to_broadcast([P, 2, 2, NP]), ACT.Identity, scale=par("gamma", k), bias=par("beta", k))\
                        .then_inc(sems["xnT"], 1)

            def exponential(t):
                act.wait_ge(sems["subbed"], t + 1)
                nc.scalar.activation(score[:, t % 2, :, :], score[:, t % 2, :, :], ACT.Exp,
                                     scale=1.0 / float(D) ** 0.5).then_inc(sems["exped"], 1)

            for t in range(T):
                act.wait_ge(sems["hps"], t + 1)
                nc.scalar.activation(h_tok[:, t, :], psum[:, t, 0:D], ACT.Copy).then_inc(sems["hsb"], 1)
                if t == 1:
                    act.wait_ge(sems["tz"], 1)
                    for k in range(DC):
                        nc.scalar.activation(xnT_cls[:, k, :], psum[:, 5, k * B:(k + 1) * B], ACT.Identity,
                                             scale=par("gamma", k), bias=par("beta", k)).then_inc(sems["xnT"], 1)
                if t == 2:
                    norm_turned(0)
            act.wait_ge(sems["bias2"], 2)
            for n in range(T):
                act.wait_ge(sems["qps"], n + 1)
                for g in range(DC):
                    q_ps = psum[:, 6, g * P:(g + 1) * P]
                    for dst, bias in ((quT, bqu), (qvT, bqv)):
                        nc.scalar.activation(dst[:, g, n * P:(n + 1) * P], q_ps, ACT.Identity,
                                             bias=bias[:, g:g + 1]).then_inc(sems["q_ev"], 1)
                if n + 1 < T:
                    norm_turned(n + 1)
                if n >= 2:
                    exponential(n - 2)
                if n == 0:
                    act.wait_ge(sems["zeros"], 2)
                if n >= 2:
                    act.wait_ge(sems["emb_out"], 16 * (n - 1))
                for q in range(2):
                    act.wait_ge(sems["emb_ps"], NQ * n + q + 1)
                    nc.scalar.activation(emb[:, n % 2, 1:S + 1, q * QH:(q + 1) * QH].rearrange("p m h -> p h m"),
                                         psum[:, q, 0:QC].rearrange("p (h m) -> p h m", h=QH), ACT.Copy)\
                        .then_inc(sems["emb_a"], 1)
            def turned(t):
                for half in range(2):
                    act.wait_ge(sems["te_ps"], 2 * t + half + 1)
                    for i in range(2):
                        nc.scalar.activation(probT[:, 2 * t + i, 4 * half:4 * half + 4, 1:S],
                                             psum[:, 4 + half, :].rearrange("p (h i s) -> p h i s", h=4, i=2)[:, :, i, :],
                                             ACT.Copy).then_inc(sems["te_ev"], 1)

            def key0_turned(t):
                act.wait_ge(sems["te0_ps"], t + 1)
                nc.scalar.activation(probT_cls[:, 2 * t:2 * t + 2, 1:S],
                                     psum[0:H, key0_bank[t], 3 * P:4 * P].rearrange("p (i s) -> p i s", i=2), ACT.Copy)\
                    .then_inc(sems["te0_ev"], 1)

            turned(0)
            act.wait_ge(sems["cls_sub"], 1)
            nc.scalar.activation(e_cls[:, :], e_cls[:, :], ACT.Exp, scale=1.0 / float(D) ** 0.5,
                                 accum_out=small[:, 1:2]).then_inc(sems["cls_exp"], 1)
            turned(1)
            w1_high(act, 0, 0, 16)
            key0_turned(0)
            key0_turned(1)
            w1_high(act, 1, 1, 16)
            w2_high(act, 0, 0, 16)
            exponential(2)

            def outputs(t):
                act.wait_ge(sems["pv_ps"], t + 1)
                o_ps = psum[:, value_bank[t], 0:DC * 2 * S].rearrange("p (g i s) -> p g i s", g=DC, i=2)
                for g in range(DC):
                    nc.scalar.activation(outT[:, g, 2 * t:2 * t + 2, :], o_ps[:, g, :, 1:S], ACT.Identity,
                                         bias=par("bv", g)).then_inc(sems["pv_ev"], 1)
                for g in range(DC):
                    nc.scalar.activation(outT_cls[:, g, 2 * t:2 * t + 2], o_ps[:, g, :, 0], ACT.Identity,
                                         bias=par("bv", g)).then_inc(sems["pv_ev"], 1)

            outputs(0)
            outputs(1)
            turned(2)
            key0_turned(2)
            exponential(T - 1)
            outputs(2)
            turned(T - 1)
            key0_turned(T - 1)
            tx_high(act, 0)
            outputs(T - 1)
            tx_high(act, 1)
            act.wait_ge(s_const, 16)
            nc.scalar.activation(small[:, 3:4], const("zero")[:, 0:1], ACT.Gelu).then_inc(sems["tables"], 1)
            for n in range(T - 2, T + 1):
                tx_high(act, n)
                if n == T - 2:
                    act.wait_ge(sems["gateT_ps"], 1)
                    nc.scalar.activation(gateT[:, 0:2 * P], psum[0:E, 7, B:HALF], ACT.Copy).then_inc(sems["gateT"], 1)
            act.wait_ge(sems["gateT_ps"], 2)
            nc.scalar.activation(gateT[:, 2 * P:T * P], psum[0:E, 6, B:HALF], ACT.Copy).then_inc(sems["gateT"], 1)
            nc.scalar.activation(gateT_cls[:, :], psum[0:E, 6, 0:B], ACT.Copy).then_inc(sems["gateT"], 1)
            act.wait_ge(s_b1, 16)

            def hidden(e, p, m):
                act.wait_ge(sems["hid_ps"], FC * e + m + 1)
                if not isinstance(e, int) or e >= 1:
                    act.wait_ge(sems["hsplit"], 2 * (FC * (e - 1) + m + 1))
                if not isinstance(e, int) or e >= 2:
                    act.wait_ge(sems["o_ps"], (T + 1) * (e - 1))
                for dst in (hid[:, m, :], hid_lh[:, p, m, HIGH:HIGH + NT]):
                    nc.scalar.activation(dst.rearrange("p (a n) -> p a n", a=2),
                                         psum[:, 2 * (m % 2):2 * (m % 2) + 2, 0:HALF], ACT.Gelu,
                                         bias=b1_cols[:, bass.ds(e, 1), m]).then_inc(sems["gelu"], 1)

            def square(e, p, t):
                act.wait_ge(sems["negm"], T * e + t + 1)
                if not isinstance(e, int) or T * e + t > 1:
                    act.wait_ge(sems["sq"], T * e + t - 1)
                nc.scalar.activation(sq_junk[t % 2], res[:, p, t, :], ACT.Square, bias=neg_mean[:, p, t:t + 1],
                                     accum_out=sq_sum[:, p, t:t + 1]).then_inc(sems["sq"], 1)

            for m in range(FC):
                hidden(0, 0, m)

            def cls_row(e):
                act.wait_ge(sems["o_ps"], (T + 1) * e + (1 if isinstance(e, int) and e == E - 1 else T + 1))
                nc.scalar.activation(cls_rows[:, bass.ds(e, 1), :].rearrange("p o d -> p (o d)"),
                                     psum[0:2 * B, 7 if isinstance(e, int) and e == E - 1 else 6, 0:D], ACT.Copy)\
                    .then_inc(sems["cls_row"], 1)

            def slot(e, p, k):
                for m in range(FC):
                    hidden(e + 1, 1 - p, m)
                    if m == 0 and (not isinstance(e, int) or e >= 1):
                        cls_row(e - 1)
                    if m >= 1:
                        square(e, p, m - 1)
                    if m == 0:
                        w2_high(act, e + 1, 1 - p, 16 * (k + 1 + p))
                    if m == 1 and (not isinstance(e, int) or e + 2 < E):
                        w1_high(act, e + 2, p, 16 * (k + 2))
                square(e, p, FC - 1)

            slot(0, 0, 0)
            with act.Fori(0, 2) as i:
                slot(2 * i + 1, 1, i)
                slot(2 * i + 2, 0, i + 1)
            for e in range(5, E - 1):
                slot(e, e % 2, e // 2)
            def last_tile(e, i, t, y):
                p = e % 2
                act.wait_ge(sems["last_bias"], i + 1)
                nc.scalar.activation(y, res[:, p, t, :], ACT.Identity, scale=e_scale[:, p, t:t + 1],
                                     bias=last_bias[:, i, t:t + 1]).then_inc(sems["last_y"], 1)

            cls_row(E - 2)
            cls_row(E - 1)
            for t in range(2, T):
                last_tile(E - 2, 0, t, last_y[0][:, t, :])
            for t in range(T):
                square(E - 1, (E - 1) % 2, t)
            last_tile(E - 1, 1, T - 1, last_y[1][:, 0, :])
            for t in (T - 1, T - 2):
                if t == T - 1:
                    act.wait_ge(sems["last_acc"], 3)
                else:
                    act.wait_ge(sems["p2"], T * (E - 2) + 2 + t + 1)
                act.dma_start(out[2 * t:2 * t + 2, 1:S, :], acc[:, t, :]).then_inc(sems["out"], 16)

        @block.vector
        def _(dve):
            chain = [0]
            nc.vector.memset(ones[:, :], 1.0).then_inc(sems["ones"], 1)

            def link(ins):
                chain[0] += 1
                ins.then_inc(sems["vchain"], 1)
                dve.wait_ge(sems["vchain"], chain[0])

            def norm1(x, rows, n):
                link(nc.vector.bn_stats(stats[0:rows, n, :], x))
                link(nc.vector.bn_aggr(mv[0:rows, n, :], stats[0:rows, n, :]))
                nc.vector.tensor_scalar(var[0:rows, n:n + 1], mv[0:rows, n, 1:2], 1.0 + EPS, EPS * EPS,
                                        ALU.mult, ALU.add).then_inc(sems["var1"], 1)

            def scale1(x, dst, rows, n, count):
                dve.wait_ge(sems["rstd1"], count)
                nc.vector.tensor_scalar(dst, x, mv[0:rows, n, 0:1], rstd[0:rows, n:n + 1], ALU.subtract, ALU.mult)\
                    .then_inc(sems["xn"], 1)

            dve.wait_ge(s_cls, 16)
            norm1(h_cls[:, :], B, T)
            dve.wait_ge(s_par, 16)
            nc.vector.tensor_tensor(bqu[:, :], PAR[:, 0:DC], PAR[:, 3 * DC:4 * DC], ALU.add).then_inc(sems["bias2"], 1)
            nc.vector.tensor_tensor(bqv[:, :], PAR[:, 0:DC], PAR[:, 4 * DC:5 * DC], ALU.add).then_inc(sems["bias2"], 1)
            scale1(h_cls[:, :], xn_cls[:, :], B, T, 1)
            def scores(t):
                p = t % 2
                dve.wait_ge(sems["ac_ps"], t + 1)
                dve.wait_ge(s_shift_in[t % 2], 16 * (t // 2 + 1))
                if t >= 2:
                    dve.wait_ge(sems["normed"], 2 * (t - 1))
                nc.vector.tensor_tensor(score[:, p, :, :].rearrange("p (q h) j -> p q h j", q=NQ),
                                        psum[:, 0:NQ, 0:QC].rearrange("p q (h j) -> p q h j", h=QH),
                                        shifted[:, p, :, :].rearrange("p j (q h) -> p q h j", q=NQ), ALU.add)\
                    .then_inc(sems["added"], 1)

            def less_maximum(t):
                p = t % 2
                dve.wait_ge(sems["added"], t + 1)
                nc.vector.tensor_reduce(mx[:, p, :], score[:, p, :, :], AX, ALU.max).then_inc(sems["maxed"], 1)
                dve.wait_ge(sems["maxed"], t + 1)
                nc.vector.tensor_tensor(score[:, p, :, :], score[:, p, :, :],
                                        mx[:, p, :].unsqueeze(2).to_broadcast([P, H, S]), ALU.subtract)\
                    .then_inc(sems["subbed"], 1)

            def sums(t):
                p = t % 2
                dve.wait_ge(sems["exped"], t + 1)
                nc.vector.tensor_reduce(rs[:, p, :], score[:, p, :, :], AX, ALU.add).then_inc(sems["summed"], 1)
                dve.wait_ge(sems["summed"], t + 1)
                nc.vector.reciprocal(ri[:, p, :], rs[:, p, :]).then_inc(sems["recip"], 1)

            def tile_norm(t):
                dve.wait_ge(sems["hsb"], t + 1)
                norm1(h_tok[:, t, :], P, t)

            def tile_scale(t):
                scale1(h_tok[:, t, :], xn[:, t, :], P, t, t + 2)

            def spread_next():
                dve.wait_ge(sems["q_ev"], 4 * T)
                for g in range(DC):
                    first = qvT[:, g, :].rearrange("p (b n) -> p b n", b=B)[:, :, 0:1]
                    nc.vector.tensor_tensor(z_next[:, g, :, :],
                                            const("head")[:, g * H:(g + 1) * H].unsqueeze(1).to_broadcast([P, B, H]),
                                            first.to_broadcast([P, B, H]), ALU.mult).then_inc(sems["z_spread"], 1)

            tile_norm(0)
            tile_norm(1)
            tile_scale(0)
            dve.wait_ge(s_const, 16)
            dve.wait_ge(sems["pos_ps"], 1)
            pos = psum[:, T - 1, D:D + DC * S].rearrange("p (g s) -> p g s", g=DC)
            link(nc.vector.tensor_copy(pT[:, :, :], pos))
            for g in range(DC):
                nc.vector.tensor_tensor(p_quad[:, g, :, :], pT[:, g, :].unsqueeze(1).to_broadcast([P, QH, S]),
                                        const("quad").unsqueeze(2).to_broadcast([P, QH, S]), ALU.mult)\
                    .then_inc(sems["p_quad"], 1)
            tile_norm(2)
            tile_scale(1)
            dve.wait_ge(sems["bias2"], 2)
            dve.wait_ge(sems["cls_qk"], 1)
            cq = psum[:, 6, 0:4 * B].rearrange("p (c g b) -> p c g b", c=2, g=DC)
            for g in range(DC):
                nc.vector.tensor_scalar(q0u[:, g, :], cq[:, 0, g, :], bqu[:, g:g + 1], None, ALU.add)\
                    .then_inc(sems["q0_ev"], 1)
                nc.vector.tensor_scalar(q0v[:, g, :], cq[:, 0, g, :], bqv[:, g:g + 1], None, ALU.add)\
                    .then_inc(sems["q0_ev"], 1)
                nc.vector.tensor_scalar(kT[:, g, :, 0], cq[:, 1, g, :], par("bk", g), None, ALU.add)\
                    .then_inc(sems["k0_ev"], 1)
            dve.wait_ge(sems["cls_v"], 1)
            nc.vector.tensor_tensor(v0_row[:, :], psum[0:H, 7, 0:D], const("headrow", H), ALU.mult)\
                .then_inc(sems["v0_ev"], 1)
            tile_norm(3)
            tile_scale(2)
            dve.wait_ge(sems["zeros"], 2)
            dve.wait_ge(sems["q0_ev"], 2 * DC)
            for g in range(DC):
                head = const("head")[:, g * H:(g + 1) * H]
                nc.vector.tensor_tensor(z_cls[:, g, :, :], head.unsqueeze(1).to_broadcast([P, B, H]),
                                        q0u[:, g, :].unsqueeze(2).to_broadcast([P, B, H]), ALU.mult)\
                    .then_inc(sems["z_spread"], 1)
                nc.vector.tensor_tensor(z_last[:, g, :, :], head.unsqueeze(1).to_broadcast([P, B, H]),
                                        q0v[:, g, :].unsqueeze(2).to_broadcast([P, B, H]), ALU.mult)\
                    .then_inc(sems["z_spread"], 1)

            tile_scale(3)
            for n in range(T):
                dve.wait_ge(sems["kps"], n + 1)
                for g in range(DC):
                    nc.vector.tensor_scalar(kT[:, g, 2 * n:2 * n + 2, 1:S],
                                            psum[:, 4 + n % 2, (2 + g) * P:(3 + g) * P].rearrange("p (i s) -> p i s", i=2),
                                            par("bk", g), None, ALU.add).then_inc(sems["k_ev"], 1)
                dve.wait_ge(sems["vps"], n + 1)
                nc.vector.tensor_tensor(v_pair[:, 2 * n:2 * n + 2, :],
                                        psum[:, 7, :].rearrange("p (i d) -> p i d", i=2),
                                        const("parity").unsqueeze(1).to_broadcast([P, 2, D]), ALU.mult)\
                    .then_inc(sems["v_ev"], 1)
                if n >= 2:
                    dve.wait_ge(sems["emb_out"], 16 * (n - 1))
                for q in (2, 3):
                    dve.wait_ge(sems["emb_ps"], NQ * n + q + 1)
                    nc.vector.tensor_copy(emb[:, n % 2, 1:S + 1, q * QH:(q + 1) * QH].rearrange("p m h -> p h m"),
                                          psum[:, q, 0:QC].rearrange("p (h m) -> p h m", h=QH))\
                        .then_inc(sems["emb_v"], 1)
                if n == T - 1:
                    spread_next()
                if n >= 2:
                    sums(n - 2)
                if n in (1, 2):
                    scores(n - 1)
                    less_maximum(n - 1)
            def norm2(n):
                rows = P if n < T else B
                h = h_tok[:, n, :] if n < T else h_cls[:, :]
                dve.wait_ge(sems["wf_ps"], n + 1)
                if n == 0:
                    dve.wait_ge(sems["hbf"], 2)
                dve_h2 = nc.vector.tensor_tensor(h, psum[0:rows, project_bank[n], 0:D], h, ALU.add)
                dve_h2.then_inc(sems["h2"], 1)
                dve.wait_ge(sems["h2"], n + 1)
                link(nc.vector.bn_stats(stats[0:rows, n, :], h))
                link(nc.vector.bn_aggr(mv[0:rows, n, :], stats[0:rows, n, :]))
                nc.vector.tensor_scalar(var[0:rows, n:n + 1], mv[0:rows, n, 1:2], EPS, None, ALU.add)\
                    .then_inc(sems["var2"], 1)

            def norm2_scale(n):
                rows = P if n < T else B
                h = h_tok[:, n, :] if n < T else h_cls[:, :]
                x = xn[:, n, :] if n < T else xn_cls[:, :]
                dve.wait_ge(sems["rstd2"], n + 1)
                nc.vector.tensor_scalar(x, h, mv[0:rows, n, 0:1], rstd[0:rows, n:n + 1], ALU.subtract, ALU.mult)\
                    .then_inc(sems["xt"], 1)

            def tx_low(n):
                rows = P if n < T else B
                c0 = column(n)
                dve.wait_ge(sems["tx_h"], n + 1)
                nc.vector.tensor_tensor(xT_l[:, :, c0:c0 + rows],
                                        psum[:, 4 + n % 2, 0:DC * rows].rearrange("p (k n) -> p k n", k=DC),
                                        xT_h[:, :, c0:c0 + rows].bitcast(F32), ALU.subtract).then_inc(sems["tx_l"], 1)

            dve.wait_ge(sems["clsac_ps"], 1)
            link(nc.vector.tensor_tensor(cls_all[:, :].rearrange("p (a b s) -> p a b s", a=2, b=4),
                                         psum[:, 6:8, 0:4 * S].rearrange("p a (b s) -> p a b s", b=4),
                                         const("image").rearrange("p (a b) -> p a b", a=2).unsqueeze(3)
                                         .to_broadcast([P, 2, 4, S]), ALU.mult))
            link(nc.vector.tensor_reduce(e_cls[:, :], cls_all[:, :].rearrange("p (b s) -> p s b", b=B), AX, ALU.add))
            nc.vector.tensor_tensor(e_cls[:, 0:1], e_cls[:, 0:1], psum[:, 7, 4 * S:4 * S + 1], ALU.add)\
                .then_inc(sems["cls_bd"], 1)
            nc.vector.tensor_tensor(e_cls[:, 2:S], e_cls[:, 2:S], psum[:, 7, 4 * S + 2:5 * S], ALU.add)\
                .then_inc(sems["cls_bd"], 1)
            dve.wait_ge(sems["cls_bd"], 2)
            link(nc.vector.tensor_reduce(small[:, 0:1], e_cls[:, :], AX, ALU.max))
            nc.vector.tensor_scalar(e_cls[:, :], e_cls[:, :], small[:, 0:1], None, ALU.subtract)\
                .then_inc(sems["cls_sub"], 1)
            dve.wait_ge(sems["cls_exp"], 1)
            link(nc.vector.reciprocal(small[:, 2:3], small[:, 1:2]))
            nc.vector.tensor_scalar(p_cls[:, :, :], e_cls[:, 1:S].unsqueeze(1).to_broadcast([P, 2, NP]),
                                    small[:, 2:3], None, ALU.mult).then_inc(sems["cls_norm"], 1)
            nc.vector.tensor_scalar(e_cls0[:, :], const("image"), e_cls[:, 0:1], small[:, 2:3], ALU.mult, ALU.mult)\
                .then_inc(sems["e0"], 1)
            scores(2)
            dve.wait_ge(sems["tcls_ps"], 1)
            for par_ in range(2):
                rows = slice(par_ * NP, (par_ + 1) * NP)
                nc.vector.tensor_copy(probT[rows, :, :, 0],
                                      psum[rows, 7, 0:P].rearrange("p (b h a) -> p b h a", b=B, a=2)[:, :, :, par_])\
                    .then_inc(sems["tcls_ev"], 1)
            nc.vector.tensor_copy(probT_cls[:, :, 0], psum[0:H, 7, P:P + B]).then_inc(sems["tcls_ev"], 1)
            less_maximum(2)
            sums(2)
            scores(3)
            less_maximum(3)
            for x in (xT_h, xT_l):
                nc.vector.tensor_copy(x[:, :, HALF:HALF + B], const("zero").rearrange("p (k n) -> p k n", k=DC))\
                    .then_inc(sems["pad"], 1)
            dve.wait_ge(s_gw, 16)
            nc.vector.tensor_copy(w_gate_h[:, :, :], w_gate[:, :, :]).then_inc(sems["gw_split"], 1)
            dve.wait_ge(sems["gw_split"], 1)
            nc.vector.tensor_tensor(w_gate_l[:, :, :], w_gate[:, :, :], w_gate_h[:, :, :].bitcast(F32), ALU.subtract)\
                .then_inc(sems["gw_split"], 1)
            sums(3)
            dve.wait_ge(sems["recip"], T)
            dve.wait_ge(sems["te_ps"], 2 * (T - 2))
            nc.vector.tensor_tensor(prob[:, 1, SHARE:, :], score[:, 1, SHARE:, 1:S],
                                    ri[:, 1, SHARE:].unsqueeze(2).to_broadcast([P, H - SHARE, NP]), ALU.mult)\
                .then_inc(sems["normed_d"], 1)
            for n in range(T - 1):
                norm2(n)
                if n >= 1:
                    tx_low(n - 1)
                norm2_scale(n)
            norm2(T - 1)
            norm2(T)
            norm2_scale(T - 1)
            norm2_scale(T)
            for n in range(T - 2, T + 1):
                tx_low(n)

            def hsplit(e, p, m):
                dve.wait_ge(sems["gelu"], 2 * (FC * e + m + 1))
                if not isinstance(e, int) or e >= 2:
                    dve.wait_ge(sems["o_ps"], (T + 1) * (e - 1))
                nc.vector.tensor_tensor(hid_lh[:, p, m, T * P:HIGH], hid[:, m, 0:B],
                                        hid_lh[:, p, m, HIGH:HIGH + B].bitcast(F32), ALU.subtract)\
                    .then_inc(sems["hsplit"], 1)
                nc.vector.tensor_tensor(hid_lh[:, p, m, 0:T * P].rearrange("p (a n) -> p a n", a=2),
                                        hid[:, m, :].rearrange("p (a n) -> p a n", a=2)[:, :, B:],
                                        hid_lh[:, p, m, HIGH:].bitcast(F32)
                                        .rearrange("p (a n) -> p a n", a=2)[:, :, B:], ALU.subtract)\
                    .then_inc(sems["hsplit"], 1)

            dve.wait_ge(sems["gate_ps"], 1)
            nc.vector.tensor_copy(gate[:, 0:T, :], psum[:, 7, 0:T * E].rearrange("p (t n) -> p t n", t=T))\
                .then_inc(sems["gate_sb"], 1)
            nc.vector.tensor_copy(gate[0:B, T, :], psum[0:B, 7, T * E:(T + 1) * E]).then_inc(sems["gate_sb"], 1)
            dve.wait_ge(sems["gate_sb"], 2)
            for n in range(T + 1):
                nc.vector.max(top[:, n, :], gate[:, n, :]).then_inc(sems["tops"], 1)
            dve.wait_ge(sems["tops"], T + 1)
            for n in range(T + 1):
                nc.vector.max_index(top_at[:, n, :], top[:, n, :], gate[:, n, :]).then_inc(sems["tops"], 1)
            nc.vector.tensor_tensor(tw[:, :, 0], top[:, :, 1], top[:, :, 0], ALU.subtract).then_inc(sems["diff"], 1)
            dve.wait_ge(sems["tops"], 2 * (T + 1))
            link(nc.vector.tensor_copy(top_atf[:, :, :], top_at[:, :, 0:2]))
            for k in range(2):
                link(nc.vector.tensor_tensor(pick[:, k, :, :], const("iota").unsqueeze(1).to_broadcast([P, T + 1, E]),
                                             top_atf[:, :, k:k + 1].to_broadcast([P, T + 1, E]), ALU.is_equal))
            hsplit(0, 0, 0)
            dve.wait_ge(sems["dexp"], 1)
            link(nc.vector.tensor_scalar(tw[:, :, 2], tw[:, :, 1], 1.0, None, ALU.add))
            link(nc.vector.reciprocal(tw[:, :, 3], tw[:, :, 2]))
            link(nc.vector.tensor_tensor(tw[:, :, 2], tw[:, :, 3], tw[:, :, 1], ALU.mult))
            for k in range(2):
                link(nc.vector.tensor_tensor(pick[:, k, :, :], pick[:, k, :, :],
                                             tw[:, :, 3 - k:4 - k].to_broadcast([P, T + 1, E]), ALU.mult))
            nc.vector.tensor_tensor(wE[:, :, :], pick[:, 0, :, :], pick[:, 1, :, :], ALU.add).then_inc(sems["wE"], 1)
            dve.wait_ge(sems["wE"], 1)
            nc.vector.tensor_scalar(wE_d[:, :, :], wE[:, :, :], float(D) ** 0.5, None, ALU.mult).then_inc(sems["wE"], 1)

            def residual(e, p, t):
                last = isinstance(e, int) and e == E - 1
                dve.wait_ge(sems["o_ps"], (T + 1) * e + t + (2 if last else 1))
                if t == 0:
                    dve.wait_ge(sems["xb"], e + 1)
                nc.vector.scalar_tensor_tensor(res[:, p, t, :], psum[:, 4 + t % 2, 0:D], 1.0, xb[:, p, t, :],
                                               ALU.mult, ALU.add, accum_out=res_sum[:, p, t:t + 1])\
                    .then_inc(sems["r"], 1)
                dve.wait_ge(sems["r"], T * e + t + 1)
                nc.vector.tensor_scalar(neg_mean[:, p, t:t + 1], res_sum[:, p, t:t + 1], -1.0 / D, None, ALU.mult)\
                    .then_inc(sems["negm"], 1)

            def add_expert(e, p, t, n=None):
                if n is None:
                    n = T * e + t
                if t == 0:
                    dve.wait_ge(sems["escale"], 3 * e + 3)
                if not isinstance(n, int) or n >= 1:
                    dve.wait_ge(sems["p2"], n)
                nc.vector.scalar_tensor_tensor(scaled[:, :], res[:, p, t, :], neg_mean[:, p, t:t + 1],
                                               g_rows[:, bass.ds(e, 1), :].rearrange("p o d -> p (o d)"),
                                               ALU.add, ALU.mult).then_inc(sems["scaled"], 1)
                dve.wait_ge(sems["scaled"], n + 1)
                nc.vector.scalar_tensor_tensor(acc[:, t, :], scaled[:, :], e_scale[:, p, t:t + 1], acc[:, t, :],
                                               ALU.mult, ALU.add).then_inc(sems["p2"], 1)

            for m in range(1, FC):
                if m == FC - 1:
                    dve.wait_ge(sems["wET_ps"], 1)
                    nc.vector.tensor_copy(wET[:, :, :], psum[0:E, 7, 0:T * P].rearrange("p (t n) -> p t n", t=T))\
                        .then_inc(sems["wET"], 1)
                hsplit(0, 0, m)

            def start_acc(t):
                dve.wait_ge(sems["lnb_ps"], t + 1)
                nc.vector.tensor_tensor(acc[:, t, :], psum[:, 6 + t % 2, 0:D], h_tok[:, t, :], ALU.add)\
                    .then_inc(sems["acc0"], 1)

            def class_rows():
                dve.wait_ge(sems["wcol_ps"], 1)
                nc.vector.tensor_tensor_reduce(wcol_x[:, :], psum[0:E * B, 7, D:D + E], const("expert", E * B), 1.0, 0.0,
                                               ALU.mult, ALU.add, wcol[:, :]).then_inc(sems["wsel"], 1)
                dve.wait_ge(sems["wsel"], 1)
                nc.vector.tensor_scalar(wsel[:, :], const("imageof", E * B), wcol[:, :], None, ALU.mult)\
                    .then_inc(sems["wsel"], 1)
                dve.wait_ge(s_clsrows, 16 * 3)
                nc.vector.tensor_tensor(x_cls[:, :], psum[0:E * B, 7, 0:D], b2_cls[:, :], ALU.add)\
                    .then_inc(sems["x_cls"], 1)

            def slot(e, p, k):
                for m in range(FC):
                    hsplit(e + 1, 1 - p, m)
                    if isinstance(e, int) and e == 0 and m < 2:
                        start_acc(2 * m)
                        start_acc(2 * m + 1)
                    residual(e, p, m)
                    if not isinstance(e, int) or e >= 1:
                        add_expert(e - 1, 1 - p, m)
                    if isinstance(e, int) and e == 0 and m == 2:
                        class_rows()

            slot(0, 0, 0)
            dve.wait_ge(s_g, 16)
            with dve.Fori(0, 2) as i:
                slot(2 * i + 1, 1, i)
                slot(2 * i + 2, 0, i + 1)
            for e in range(5, E - 1):
                slot(e, e % 2, e // 2)
            e, p = E - 1, (E - 1) % 2
            for t in range(T):
                if t < 2:
                    add_expert(e - 1, 1 - p, t)
                residual(e, p, t)
            for t in range(2):
                add_expert(e, p, t, T * (E - 2) + 2 + t)
            dve.wait_ge(sems["o_cls"], 16 * 2 * E)
            dve.wait_ge(sems["x_cls"], 1)
            link(nc.vector.tensor_tensor(r_cls[:, :], o_cls[:, 0, :], o_cls[:, 1, :], ALU.add))
            link(nc.vector.tensor_tensor(r_cls[:, :], r_cls[:, :], x_cls[:, :], ALU.add))
            link(nc.vector.bn_stats(stats[0:E * B, T, :], r_cls[:, :]))
            link(nc.vector.bn_aggr(mv[0:E * B, T, :], stats[0:E * B, T, :]))
            nc.vector.tensor_scalar(cls_small[:, 3:4], mv[0:E * B, T, 1:2], EPS_FFN, None, ALU.add)\
                .then_inc(sems["cls_var"], 1)
            link(nc.vector.scalar_tensor_tensor(r_cls[:, :], r_cls[:, :], mv[0:E * B, T, 0:1], g_cls[:, :],
                                                ALU.subtract, ALU.mult))
            dve.wait_ge(sems["last_acc"], 1)
            dve.wait_ge(sems["escale"], 3 * e + 6)
            add_expert(e, p, 2, T * (E - 2) + 4)
            dve.wait_ge(sems["cls_rs"], 1)
            nc.vector.scalar_tensor_tensor(r_cls[:, :], r_cls[:, :], cls_small[:, 4:5], lnb_cls[:, :],
                                           ALU.mult, ALU.add).then_inc(sems["y_cls"], 1)
            dve.wait_ge(sems["clsout_ps"], 1)
            nc.vector.tensor_tensor(acc_cls[:, :], psum[0:B, 7, 0:D], h_cls[:, :], ALU.add).then_inc(sems["clsout"], 1)

        @block.tensor
        def _(pe):
            mm = nc.tensor.matmul

            def raise_clock(n, bank):
                for _ in range(n):
                    mm(psum[:, bank, 0:P], ones[:, :], ones[:, :], start=True, stop=True)

            pe.wait_ge(sems["ones"], 1)

            def embed(t):
                pe.wait_ge(s_xp[t], 16)
                if t == T - 1:
                    pe.wait_ge(sems["p_quad"], DC)
                for k in range(KP):
                    if t == 0 and k % (KP // 2) == 0:
                        pe.wait_ge(s_wtok[k // (KP // 2)], 16)
                    last = mm(psum[:, t, 0:D], xp_sb[:, t, k * P:(k + 1) * P], w_tok[:, k, :],
                              start=(k == 0), stop=(k == KP - 1))
                last.then_inc(sems["hps"], 1)

            def turn_xn(t):
                p = t % 2
                pe.wait_ge(sems["xn"], t + 2)
                if t == 1:
                    pe.wait_ge(sems["xnT"], DC)
                if t >= 2:
                    pe.wait_ge(sems["k_ev"], 2 * (t - 1))
                for k in range(DC):
                    last = nc.tensor.transpose(psum[:, 4 + p, k * P:(k + 1) * P], xn[:, t, k * P:(k + 1) * P], ident)
                last.then_inc(sems["tz"], 1)

            def content(t):
                pe.wait_ge(sems["k_quad"], 4 * (t + 1))
                if t + 1 < T:
                    pe.wait_ge(sems["emb_a"], 2 * (t + 2))
                    pe.wait_ge(sems["emb_v"], 2 * (t + 2))
                else:
                    pe.wait_ge(sems["added"], t)
                for q in range(NQ):
                    rows = slice((q % 2) * NP, (q % 2 + 1) * NP)
                    for i in range(2):
                        last = mm(psum[i * NP:(i + 1) * NP, q, 0:QC],
                                  quT[rows, q // 2, t * P + i * NP:t * P + (i + 1) * NP],
                                  k_quad[rows, 2 * t + i, q // 2, :, :].rearrange("p h s -> p (h s)"),
                                  start=True, stop=True)
                last.then_inc(sems["ac_ps"], 1)

            def qkv(t):
                p = t % 2
                pe.wait_ge(sems["xnT"], DC * (t + 2))
                if t == 0:
                    pe.wait_ge(sems["q0_ev"], 2 * DC)
                    pe.wait_ge(sems["k0_ev"], DC)
                else:
                    pe.wait_ge(sems["q_ev"], 4 * t)
                for g in range(DC):
                    for k in range(DC):
                        last = mm(psum[:, 6, g * P:(g + 1) * P], w_q[:, k, g * P:(g + 1) * P], xnT[:, p, k, :, 0, :],
                                  start=(k == 0), stop=(k == DC - 1))
                last.then_inc(sems["qps"], 1)
                if t >= 2:
                    content(t - 2)
                for g in range(DC):
                    for k in range(DC):
                        last = mm(psum[:, 4 + p, (2 + g) * P:(3 + g) * P], w_k[:, k, g * P:(g + 1) * P],
                                  xnT[:, p, k, :, 0, :], start=(k == 0), stop=(k == DC - 1))
                last.then_inc(sems["kps"], 1)
                if t + 1 < T:
                    turn_xn(t + 1)
                if t == 0:
                    pe.wait_ge(sems["v0_ev"], 1)
                else:
                    pe.wait_ge(sems["v_ev"], t)
                for i in range(2):
                    for k in range(DC):
                        both = xnT[:, p, k, i, :, :].rearrange("p a s -> p (a s)")
                        last = mm(psum[:, 7, i * D:(i + 1) * D], both, w_v[:, k, :], start=(k == 0), stop=(k == DC - 1))
                last.then_inc(sems["vps"], 1)

            def positions(t):
                pe.wait_ge(sems["q_ev"], 4 * (t + 1))
                if t >= 2:
                    pe.wait_ge(sems["added"], t - 1)
                for q in range(NQ):
                    if t == 0:
                        pe.wait_ge(sems["hsb"], T)
                    elif q < 2:
                        pe.wait_ge(sems["emb_a"], 2 * (t - 1) + q + 1)
                    else:
                        pe.wait_ge(sems["emb_v"], 2 * (t - 1) + q - 1)
                    rows = slice((q % 2) * NP, (q % 2 + 1) * NP)
                    mm(psum[:, q, 0:QC], qvT[rows, q // 2, t * P:(t + 1) * P],
                       p_quad[rows, q // 2, :, :].rearrange("p h s -> p (h s)"), start=True, stop=True)\
                        .then_inc(sems["emb_ps"], 1)

            embed(0)
            embed(1)
            pe.wait_ge(s_const, 16)
            pe.wait_ge(s_wp, 16)
            pe_T = const("pe")
            for g in range(DC):
                for k in range(DC):
                    last = mm(psum[:, T - 1, D + g * S:D + (g + 1) * S], w_p[:, k, g * P:(g + 1) * P],
                              pe_T[:, k * S:(k + 1) * S], start=(k == 0), stop=(k == DC - 1))
            last.then_inc(sems["pos_ps"], 1)
            pe.wait_ge(sems["xn"], 1)
            for k in range(DC):
                last = nc.tensor.transpose(psum[:, 5, k * B:(k + 1) * B], xn_cls[:, k * P:(k + 1) * P],
                                           ident[0:B, 0:B])
            last.then_inc(sems["tz"], 1)
            embed(2)
            turn_xn(0)
            pe.wait_ge(s_wqk, 32)
            pe.wait_ge(sems["xnT"], DC)
            for c, w in enumerate((w_q, w_k)):
                for g in range(DC):
                    for k in range(DC):
                        last = mm(psum[:, 6, (c * DC + g) * B:(c * DC + g + 1) * B], w[:, k, g * P:(g + 1) * P],
                                  xnT_cls[:, k, :], start=(k == 0), stop=(k == DC - 1))
            last.then_inc(sems["cls_qk"], 1)
            pe.wait_ge(s_wv, 16)
            for k in range(DC):
                last = mm(psum[0:H, 7, 0:D], xnT_cls[:, k, 0:1].to_broadcast([P, H]), w_v[:, k, :],
                          start=(k == 0), stop=(k == DC - 1))
            last.then_inc(sems["cls_v"], 1)

            embed(3)
            def class_content():
                pe.wait_ge(sems["z_spread"], 2 * DC)
                pe.wait_ge(sems["k_ev"], 2 * T)
                pe.wait_ge(sems["q_ev"], 4 * T)
                pe.wait_ge(sems["v_ev"], T)
                for half in range(2):
                    for g in range(DC):
                        mm(psum[:, 6 + half, 0:4 * S], z_cls[:, g, :, :].rearrange("p b h -> p (b h)"),
                           kT[:, g, 4 * half:4 * half + 4, :].rearrange("p b s -> p (b s)"),
                           start=(g == 0), stop=(g == DC - 1))

            def class_positions():
                pe.wait_ge(sems["z_spread"], 3 * DC)
                for g in range(DC):
                    mm(psum[:, 7, 4 * S:4 * S + 1], z_last[:, g, :, :].rearrange("p b h -> p (b h)"), pT[:, g, S - 1:S],
                       start=(g == 0), stop=(g == DC - 1))
                for g in range(DC):
                    last = mm(psum[:, 7, 4 * S + 2:5 * S], z_next[:, g, :, :].rearrange("p b h -> p (b h)"),
                              pT[:, g, 0:S - 2], start=(g == 0), stop=(g == DC - 1))
                last.then_inc(sems["clsac_ps"], 1)

            def turn_classes():
                pe.wait_ge(sems["cls_norm"], 1)
                nc.tensor.transpose(psum[:, 7, 0:P], p_cls[:, :, :].rearrange("p a s -> p (a s)"), ident)
                pe.wait_ge(sems["e0"], 1)
                mm(psum[0:H, 7, P:P + B], const("headof"), e_cls0[:, :], start=True, stop=True)\
                    .then_inc(sems["tcls_ps"], 1)

            def turn(t):
                p = t % 2
                pe.wait_ge(sems["normed"], 2 * (t + 1))
                if t == T - 1:
                    pe.wait_ge(sems["normed_d"], 1)
                if t == 0:
                    pe.wait_ge(sems["k_ev"], 2 * T)
                for half in range(2):
                    if t >= 1:
                        pe.wait_ge(sems["te_ev"], 4 * t)
                    for n in range(4):
                        pair = 4 * half + n
                        last = nc.tensor.transpose(psum[:, 4 + half, n * P:(n + 1) * P],
                                                   prob[:, p, 2 * pair:2 * pair + 2, :].rearrange("p h j -> p (h j)"), ident)
                    last.then_inc(sems["te_ps"], 1)

            def turn_0(t):
                p = t % 2
                if t == 0:
                    pe.wait_ge(sems["tcls_ev"], 3)
                elif t >= 2:
                    pe.wait_ge(sems["added"], T)
                    pe.wait_ge(sems["te0_ev"], t)
                nc.tensor.transpose(psum[0:H, key0_bank[t], 3 * P:4 * P], prob0[:, p, :], ident)\
                    .then_inc(sems["te0_ps"], 1)

            def values(t):
                bank = value_bank[t]
                pe.wait_ge(sems["te_ev"], 4 * (t + 1))
                pe.wait_ge(sems["te0_ev"], max(t, 1) + 1)
                if t >= 2:
                    pe.wait_ge(sems["pv_ev"], 4 * (t - 1))
                for g in range(DC):
                    for i in range(2):
                        b = 2 * t + i
                        c0 = (2 * g + i) * S
                        mm(psum[:, bank, c0:c0 + S], v0_row[:, g * P:(g + 1) * P], probT_cls[:, b, :],
                           start=True, stop=False, skip_group_check=True)
                        for c in range(4):
                            pair = 4 * g + c
                            last = mm(psum[32 * c:32 * c + 32, bank, c0:c0 + S],
                                      v_pair[:, b, 32 * pair:32 * pair + 32],
                                      probT[:, b, pair, :], start=False, stop=(c == 3), skip_group_check=True)
                last.then_inc(sems["pv_ps"], 1)

            def project(t):
                if t == 0:
                    pe.wait_ge(s_wf, 16)
                    pe.wait_ge(sems["added"], T)
                elif t == T - 1:
                    pe.wait_ge(sems["h2"], 1)
                pe.wait_ge(sems["pv_ev"], 4 * t + 2 if t < T else 4 * T)
                rows, bank = (P if t < T else B), project_bank[t]
                for k in range(DC):
                    x = outT[:, k, 2 * t:2 * t + 2, :].rearrange("p i s -> p (i s)") if t < T else outT_cls[:, k, :]
                    last = mm(psum[0:rows, bank, 0:D], x, w_f[:, k, :], start=(k == 0), stop=(k == DC - 1))
                last.then_inc(sems["wf_ps"], 1)

            def turn_x(n):
                rows = P if n < T else B
                if n >= 2:
                    pe.wait_ge(sems["tx_l"], n - 1)
                x = xn[:, n, :] if n < T else xn_cls[:, :]
                pe.wait_ge(sems["xt"], n + 1)
                pe.wait_ge(sems["te_ev"], 4 * T)
                for k in range(DC):
                    last = nc.tensor.transpose(psum[:, 4 + n % 2, k * rows:(k + 1) * rows], x[:, k * P:(k + 1) * P],
                                               ident[0:rows, 0:rows])
                last.then_inc(sems["tx_ps"], 1)

            def gate_scores(half):
                if half == 1:
                    pe.wait_ge(sems["tx_l"], 2)
                    pe.wait_ge(sems["pad"], 2)
                    pe.wait_ge(sems["gw_split"], 2)
                    pe.wait_ge(sems["pv_ev"], 4 * T)
                else:
                    pe.wait_ge(sems["tx_l"], T + 1)
                    pe.wait_ge(sems["h2"], T)
                for k in range(DC):
                    for w, x in ((w_gate_h, xT_h), (w_gate_h, xT_l), (w_gate_l, xT_h)):
                        last = mm(psum[0:E, 6 + half, 0:HALF], w[:, k, :], x[:, k, half * HALF:(half + 1) * HALF],
                                  start=(k == 0 and w is w_gate_h and x is xT_h), stop=(k == DC - 1 and w is w_gate_l))
                last.then_inc(sems["gateT_ps"], 1)

            def hidden(e, p, m, halves=(0, 1)):
                ahead = 1 in halves and len(halves) == 1
                if m == 0:
                    pe.wait_ge(sems["w1h"], e + 1)
                    pe.wait_ge(sems["w1l"], e + 1)
                if isinstance(e, int) and e == 0 and m < 2:
                    if ahead:
                        pe.wait_ge(sems["added"], T)
                        pe.wait_ge(sems["tx_l"], 2)
                    else:
                        pe.wait_ge(sems["tx_l"], T + 1)
                        pe.wait_ge(sems["h2"], T + 1)
                else:
                    pe.wait_ge(sems["gelu"], 2 * (FC * e + m - 1))
                for k in range(DC):
                    cols = slice(k * F + m * P, k * F + (m + 1) * P)
                    for w, x in ((w1_h, xT_h), (w1_h, xT_l), (w1_l, xT_h)):
                        for half in halves:
                            last = mm(psum[:, 2 * (m % 2) + half, 0:HALF], w[:, p, cols],
                                      x[:, k, half * HALF:(half + 1) * HALF],
                                      start=(k == 0 and w is w1_h and x is xT_h), stop=(k == DC - 1 and w is w1_l))
                if not ahead:
                    last.then_inc(sems["hid_ps"], 1)

            def output(e, p, t):
                if t == 0:
                    pe.wait_ge(sems["hsplit"], 2 * FC * (e + 1))
                    pe.wait_ge(sems["w2h"], e + 1)
                    pe.wait_ge(sems["w2l"], e + 1)
                if isinstance(e, int) and e == 0 and t < 2:
                    if t == 0:
                        pe.wait_ge(sems["te_ev"], 4 * T)
                else:
                    pe.wait_ge(sems["r"], T * e + t - 1)
                for m in range(FC):
                    cols = slice(m * D, (m + 1) * D)
                    for low, w in ((False, w2_h), (False, w2_l), (True, w2_h)):
                        c0 = (t + 2) % T * P if low else HIGH + column(t)
                        last = mm(psum[:, 4 + t % 2, 0:D], hid_lh[:, p, m, c0:c0 + P], w[:, p, cols],
                                  start=(m == 0 and not low and w is w2_h), stop=(m == FC - 1 and low))
                last.then_inc(sems["o_ps"], 1)

            def output_cls(e, p):
                bank = 7 if isinstance(e, int) and e == E - 1 else 6
                if isinstance(e, int) and e == 0:
                    pe.wait_ge(sems["acc0"], T)
                elif bank == 7:
                    pe.wait_ge(sems["x_cls"], 1)
                else:
                    pe.wait_ge(sems["cls_row"], e)
                if isinstance(e, int) and e == E - 1:
                    pe.wait_ge(sems["hsplit"], 2 * FC * (e + 1))
                    pe.wait_ge(sems["w2h"], e + 1)
                    pe.wait_ge(sems["w2l"], e + 1)
                for m in range(FC):
                    cols = slice(m * D, (m + 1) * D)
                    mm(psum[0:2 * B, bank, 0:D], hid_lh[:, p, m, T * P:HIGH + B], w2_h[:, p, cols],
                       start=(m == 0), stop=(m == FC - 1), skip_group_check=True)
                    last = mm(psum[0:B, bank, 0:D], hid_lh[:, p, m, HIGH:HIGH + B], w2_l[:, p, cols],
                              start=False, stop=(m == FC - 1), skip_group_check=True)
                last.then_inc(sems["o_ps"], 1)

            for t in range(T):
                qkv(t)
                positions(t)
            turn(0)
            class_content()
            class_positions()
            content(T - 2)
            turn(1)
            turn_classes()
            raise_clock(6, 6)
            turn_0(0)
            turn_0(1)
            content(T - 1)
            values(0)
            values(1)
            turn(2)
            turn_0(2)
            project(0)
            values(2)
            project(1)
            turn(T - 1)
            turn_0(T - 1)
            project(2)
            turn_x(0)
            values(T - 1)
            turn_x(1)
            project(T - 1)
            project(T)
            hidden(0, 0, 0, (1,))
            turn_x(T - 2)
            gate_scores(1)
            turn_x(T - 1)
            hidden(0, 0, 1, (1,))
            turn_x(T)
            gate_scores(0)

            hidden(0, 0, 0, (0,))
            pe.wait_ge(sems["gateT"], 3)
            for n in range(T):
                nc.tensor.transpose(psum[:, 7, n * E:(n + 1) * E], gateT[:, n * P:(n + 1) * P], ident[0:E, 0:E])
            nc.tensor.transpose(psum[0:B, 7, T * E:(T + 1) * E], gateT_cls[:, :], ident[0:E, 0:E])\
                .then_inc(sems["gate_ps"], 1)
            for m in range(1, FC):
                hidden(0, 0, m, (0,) if m < 2 else (0, 1))
            pe.wait_ge(sems["wE"], 1)
            for t in range(T):
                last = nc.tensor.transpose(psum[0:E, 7, t * P:(t + 1) * P], wE[:, t, :], ident)
            last.then_inc(sems["wET_ps"], 1)

            def norm_bias(t):
                if t == 0:
                    pe.wait_ge(sems["wET"], 1)
                    pe.wait_ge(s_lnb, 16)
                if t >= 2:
                    pe.wait_ge(sems["acc0"], t - 1)
                mm(psum[:, 6 + t % 2, 0:D], wET[:, t, :], lnb_rows[:, :], start=True, stop=True)\
                    .then_inc(sems["lnb_ps"], 1)

            def cls_rows_of():
                pe.wait_ge(sems["acc0"], T)
                mm(psum[0:E * B, 7, D:D + E], const("spread", B), wE[0:B, T, :], start=True, stop=True)
                mm(psum[0:E * B, 7, 0:D], const("spread", B), xn_cls[:, :], start=True, stop=True)\
                    .then_inc(sems["wcol_ps"], 1)

            def slot(e, p, k):
                for m in range(FC):
                    hidden(e + 1, 1 - p, m)
                    if isinstance(e, int) and e == 0 and m < 2:
                        norm_bias(2 * m)
                        norm_bias(2 * m + 1)
                    output(e, p, m)
                    if isinstance(e, int) and e == 0 and m == 2:
                        cls_rows_of()
                output_cls(e, p)

            slot(0, 0, 0)
            with pe.Fori(0, 2) as i:
                slot(2 * i + 1, 1, i)
                slot(2 * i + 2, 0, i + 1)
            for e in range(5, E - 1):
                slot(e, e % 2, e // 2)
            output_cls(E - 1, (E - 1) % 2)
            for t in range(T):
                output(E - 1, (E - 1) % 2, t)
            pe.wait_ge(sems["y_cls"], 1)
            pe.wait_ge(sems["wsel"], 2)
            mm(psum[0:B, 7, 0:D], wsel[:, :], r_cls[:, :], start=True, stop=True).then_inc(sems["clsout_ps"], 1)


def kernel(x, cls_tok, L0_tok_W, L0_attn_Wq, L0_attn_bq, L0_attn_Wk, L0_attn_bk, L0_attn_Wv, L0_attn_bv,
           L0_attn_Wpos, L0_attn_Wf, L0_attn_bf, L0_attn_u, L0_attn_v, L0_attn_gamma, L0_attn_beta,
           L0_ffn_gate_w, L0_ffn_w1, L0_ffn_b1, L0_ffn_w2, L0_ffn_b2, L0_ffn_ln_g, L0_ffn_ln_b):
    import numpy as np
    import concourse.bacc as bacc
    from concourse.bass_utils import run_bass_kernel_spmd

    at, table = constants()
    patches = np.asarray(x).reshape(B, 3, 8, 16, 8, 16).transpose(0, 1, 3, 5, 2, 4).reshape(T, P, KP, P)
    patches = np.ascontiguousarray(patches.transpose(0, 3, 2, 1)).reshape(T, P, KP * P)
    vectors = [L0_attn_bq, L0_attn_bk, L0_attn_bv, L0_attn_u, L0_attn_v, L0_attn_gamma, L0_attn_beta]
    params = np.concatenate([np.asarray(a).reshape(DC, P).T for a in vectors], 1)
    b1t = np.asarray(L0_ffn_b1).reshape(E, FC, P).transpose(2, 0, 1)
    arrays = {
        "consts": table, "params": params, "patches": patches, "cls_tok": cls_tok, "tok_w": L0_tok_W,
        "wq": L0_attn_Wq, "wk": L0_attn_Wk, "wv": L0_attn_Wv, "wpos": L0_attn_Wpos, "wf": L0_attn_Wf,
        "bf": L0_attn_bf, "gate_w": L0_ffn_gate_w, "w1": L0_ffn_w1, "b1t": b1t, "w2": L0_ffn_w2,
        "b2": L0_ffn_b2, "ln_g": L0_ffn_ln_g, "ln_b": L0_ffn_ln_b,
    }
    arrays = {f"in_{k}": np.ascontiguousarray(a) for k, a in arrays.items()}
    nc = bacc.Bacc("TRN2", target_bir_lowering=False, num_devices=1, dynamic_dma_scratch_size=1024)
    args = [nc.dram_tensor(k, a.shape, mybir.dt.from_np(a.dtype), kind="ExternalInput").ap()
            for k, a in arrays.items()]
    out = nc.dram_tensor("out", (B, S, D), F32, kind="ExternalOutput").ap()
    build(nc, *args, out, at)
    r = run_bass_kernel_spmd(nc, [arrays], core_ids=[0])
    return r.results[0]["out"]
```
